# Optimizing a Trainium2 kernel written in Bass

```python
import numpy as np
import jax
import jax.numpy as jnp

def _softmax(x, axis=-1):
    return jax.nn.softmax(x, axis=axis)
def _gelu(x):
    return jax.nn.gelu(x, approximate=True)
def _silu(x):
    return jax.nn.silu(x)
def _sigmoid(x):
    return jax.nn.sigmoid(x)
def _layernorm(x, axis=-1, eps=1e-5):
    m = jnp.mean(x, axis=axis, keepdims=True)
    v = jnp.var(x, axis=axis, keepdims=True)
    return (x - m) / jnp.sqrt(v + eps)
def _scatter_add(tgt, idx, src, axis=0):
    return tgt.at[idx].add(src)
def _segment_sum(src, seg, n):
    return jax.ops.segment_sum(src, seg, n)

kernel_name = 'mk_conv_attn_hybrid_d2_conv_nchw128_7392fe'

def setup_inputs(seed: int = 0):
    np.random.seed(seed)
    _w = jnp.asarray
    def _rec_inputs():
        import jax
        import jax.numpy as jnp
        _gk = jax.random.key(seed)
        x = -0.0005207 + 1.001 * jax.random.normal(jax.random.fold_in(_gk, 1), (4, 128, 64, 64), jnp.float32)
        return x
    x = _rec_inputs()
    def _L0_conv_setup():
        import jax, jax.numpy as jnp
        import numpy as np
        CHANNELS = 128
        NUM_HEADS = 4
        GROUPS = 8
        EPS = 1e-05

        def _group_norm(x, weight, bias):
            b, c, h, w = x.shape
            xg = x.reshape(b, GROUPS, -1)
            mean = jnp.mean(xg, axis=-1, keepdims=True)
            var = jnp.mean(jnp.square(xg - mean), axis=-1, keepdims=True)
            xn = ((xg - mean) * jax.lax.rsqrt(var + EPS)).reshape(b, c, h, w)
            return xn * weight[None, :, None, None] + bias[None, :, None, None]
        key = jax.random.key(seed)
        ks = jax.random.split(key, 3)
        b, c, h, w = (4, CHANNELS, 64, 64)
        x = jax.random.normal(ks[0], (b, c, h, w), dtype=jnp.float32)
        norm_w = jnp.ones((c,), dtype=jnp.float32)
        norm_b = jnp.zeros((c,), dtype=jnp.float32)
        qkv_w = jax.random.normal(ks[1], (3 * c, c), dtype=jnp.float32) * c ** (-0.5)
        qkv_b = jnp.zeros((3 * c,), dtype=jnp.float32)
        proj_w = jax.random.normal(ks[2], (c, c), dtype=jnp.float32) * c ** (-0.5)
        proj_b = jnp.zeros((c,), dtype=jnp.float32)
        return {'x': x, 'norm_w': norm_w, 'norm_b': norm_b, 'qkv_w': qkv_w, 'qkv_b': qkv_b, 'proj_w': proj_w, 'proj_b': proj_b}
    _L0_conv_all = _L0_conv_setup()
    _L0_conv_in = {k: v for k, v in _L0_conv_all.items() if k in ('norm_w', 'norm_b', 'qkv_w', 'qkv_b', 'proj_w', 'proj_b', )}
    del _L0_conv_all

    def _L1_attn_setup():
        import jax, jax.numpy as jnp
        import numpy as np
        BS = 32

        def _build_leaf_block_connectivity(edge_index, edge_values, positions, num_blocks, dtype):
            rows, cols = (edge_index[0], edge_index[1])
            br, bc = (rows // BS, cols // BS)
            in_blk = (br == bc) & (br < num_blocks)
            b_safe = jnp.where(in_blk, br, num_blocks)
            rl, cl = (rows % BS, cols % BS)
            dx = positions[cols] - positions[rows]
            ef_flat = jnp.concatenate([dx, edge_values[:, None]], axis=1).astype(dtype)
            diag = jnp.arange(BS)
            attn_mask = jnp.zeros((num_blocks + 1, BS, BS + 1), dtype)
            attn_mask = attn_mask.at[:, diag, diag].set(1.0)
            attn_mask = attn_mask.at[:, :, BS].set(1.0)
            attn_mask = attn_mask.at[b_safe, rl, cl].set(1.0)
            edge_feats = jnp.zeros((num_blocks + 1, BS, BS + 1, 4), dtype)
            edge_feats = edge_feats.at[b_safe, rl, cl].set(ef_flat)
            return (attn_mask[:num_blocks], edge_feats[:num_blocks])
        key = jax.random.key(seed)
        ks = jax.random.split(key, 10)
        N, C, E, H = (262144, 128, 4194304, 4)
        x = jax.random.normal(ks[0], (1, N, C), jnp.float32)
        rows = jax.random.randint(ks[1], (E,), 0, N, dtype=jnp.int32)
        offs = jax.random.randint(ks[2], (E,), -16, 16, dtype=jnp.int32)
        cols = jnp.clip(rows + offs, 0, N - 1)
        edge_index = jnp.stack([rows, cols], axis=0)
        edge_values = jax.random.normal(ks[3], (E,), jnp.float32)
        positions = jax.random.uniform(ks[4], (N, 3), jnp.float32)
        qkv_w = jax.random.normal(ks[5], (C, 3 * C), jnp.float32) * 0.02
        qkv_b = jnp.zeros((3 * C,), jnp.float32)
        proj_w = jax.random.normal(ks[6], (C, C), jnp.float32) * 0.02
        proj_b = jnp.zeros((C,), jnp.float32)
        gate_w = jax.random.normal(ks[7], (H, 1), jnp.float32) * 0.01
        gate_b = jnp.zeros((H,), jnp.float32)
        return {'x': x, 'edge_index': edge_index, 'edge_values': edge_values, 'positions': positions, 'qkv_w': qkv_w, 'qkv_b': qkv_b, 'proj_w': proj_w, 'proj_b': proj_b, 'gate_w': gate_w, 'gate_b': gate_b}
    _L1_attn_all = _L1_attn_setup()
    _L1_attn_in = {k: v for k, v in _L1_attn_all.items() if k in ('edge_index', 'edge_values', 'positions', 'qkv_w', 'qkv_b', 'proj_w', 'proj_b', 'gate_w', 'gate_b', )}
    del _L1_attn_all

    def _L1_ffn_setup():
        import jax, jax.numpy as jnp
        import numpy as np
        B, N, D, C, E, K = (8, 8192, 128, 128, 8, 2)
        key = jax.random.key(seed)
        k0, k1, k2 = jax.random.split(key, 3)
        x = jax.random.normal(k0, (B, N, D), dtype=jnp.float32)
        router_w = jax.random.normal(k1, (D, E), dtype=jnp.float32) * 0.05
        router_b = jnp.zeros((E,), dtype=jnp.float32)
        expert_w = jax.random.normal(k2, (E, D, C), dtype=jnp.float32) * (1.0 / np.sqrt(D))
        expert_b = jnp.zeros((E, C), dtype=jnp.float32)
        return {'x': x, 'router_w': router_w, 'router_b': router_b, 'expert_w': expert_w, 'expert_b': expert_b}
    _L1_ffn_all = _L1_ffn_setup()
    _L1_ffn_in = {k: v for k, v in _L1_ffn_all.items() if k in ('router_w', 'router_b', 'expert_w', 'expert_b', )}
    del _L1_ffn_all

    return {
        "x": x,
        "L0_conv_norm_w": _L0_conv_in["norm_w"],
        "L0_conv_norm_b": _L0_conv_in["norm_b"],
        "L0_conv_qkv_w": _L0_conv_in["qkv_w"],
        "L0_conv_qkv_b": _L0_conv_in["qkv_b"],
        "L0_conv_proj_w": _L0_conv_in["proj_w"],
        "L0_conv_proj_b": _L0_conv_in["proj_b"],
        "L1_attn_edge_index": _L1_attn_in["edge_index"],
        "L1_attn_edge_values": _L1_attn_in["edge_values"],
        "L1_attn_positions": _L1_attn_in["positions"],
        "L1_attn_qkv_w": _L1_attn_in["qkv_w"],
        "L1_attn_qkv_b": _L1_attn_in["qkv_b"],
        "L1_attn_proj_w": _L1_attn_in["proj_w"],
        "L1_attn_proj_b": _L1_attn_in["proj_b"],
        "L1_attn_gate_w": _L1_attn_in["gate_w"],
        "L1_attn_gate_b": _L1_attn_in["gate_b"],
        "L1_ffn_router_w": _L1_ffn_in["router_w"],
        "L1_ffn_router_b": _L1_ffn_in["router_b"],
        "L1_ffn_expert_w": _L1_ffn_in["expert_w"],
        "L1_ffn_expert_b": _L1_ffn_in["expert_b"],
    }

def reference(x, L0_conv_norm_w, L0_conv_norm_b, L0_conv_qkv_w, L0_conv_qkv_b, L0_conv_proj_w, L0_conv_proj_b, L1_attn_edge_index, L1_attn_edge_values, L1_attn_positions, L1_attn_qkv_w, L1_attn_qkv_b, L1_attn_proj_w, L1_attn_proj_b, L1_attn_gate_w, L1_attn_gate_b, L1_ffn_router_w, L1_ffn_router_b, L1_ffn_expert_w, L1_ffn_expert_b):
    import jax
    import jax.numpy as jnp
    def _L0_conv_ref(x, norm_w, norm_b, qkv_w, qkv_b, proj_w, proj_b):
        import jax, jax.numpy as jnp
        import numpy as np
        CHANNELS = 128
        NUM_HEADS = 4
        GROUPS = 8
        EPS = 1e-05

        def _group_norm(x, weight, bias):
            b, c, h, w = x.shape
            xg = x.reshape(b, GROUPS, -1)
            mean = jnp.mean(xg, axis=-1, keepdims=True)
            var = jnp.mean(jnp.square(xg - mean), axis=-1, keepdims=True)
            xn = ((xg - mean) * jax.lax.rsqrt(var + EPS)).reshape(b, c, h, w)
            return xn * weight[None, :, None, None] + bias[None, :, None, None]
        b, c, h, w = x.shape
        heads = NUM_HEADS
        d = c // heads
        scale = d ** (-0.5)
        x_norm = _group_norm(x, norm_w, norm_b)
        qkv = jnp.einsum('oc,bchw->bohw', qkv_w, x_norm) + qkv_b[None, :, None, None]
        q, k, v = jnp.split(qkv, 3, axis=1)

        def to_heads(t):
            return t.reshape(b, heads, d, h * w).transpose(0, 1, 3, 2)
        q, k, v = (to_heads(q), to_heads(k), to_heads(v))
        attn = jnp.einsum('bhid,bhjd->bhij', q, k) * scale
        attn = jax.nn.softmax(attn, axis=-1)
        out = jnp.einsum('bhij,bhjd->bhid', attn, v)
        out = out.transpose(0, 1, 3, 2).reshape(b, c, h, w)
        out = jnp.einsum('oc,bchw->bohw', proj_w, out) + proj_b[None, :, None, None]
        return x + out

    def _L1_attn_ref(x, edge_index, edge_values, positions, qkv_w, qkv_b, proj_w, proj_b, gate_w, gate_b):
        import jax, jax.numpy as jnp
        import numpy as np
        BS = 32

        def _build_leaf_block_connectivity(edge_index, edge_values, positions, num_blocks, dtype):
            rows, cols = (edge_index[0], edge_index[1])
            br, bc = (rows // BS, cols // BS)
            in_blk = (br == bc) & (br < num_blocks)
            b_safe = jnp.where(in_blk, br, num_blocks)
            rl, cl = (rows % BS, cols % BS)
            dx = positions[cols] - positions[rows]
            ef_flat = jnp.concatenate([dx, edge_values[:, None]], axis=1).astype(dtype)
            diag = jnp.arange(BS)
            attn_mask = jnp.zeros((num_blocks + 1, BS, BS + 1), dtype)
            attn_mask = attn_mask.at[:, diag, diag].set(1.0)
            attn_mask = attn_mask.at[:, :, BS].set(1.0)
            attn_mask = attn_mask.at[b_safe, rl, cl].set(1.0)
            edge_feats = jnp.zeros((num_blocks + 1, BS, BS + 1, 4), dtype)
            edge_feats = edge_feats.at[b_safe, rl, cl].set(ef_flat)
            return (attn_mask[:num_blocks], edge_feats[:num_blocks])
        B, N, C = x.shape
        H = gate_b.shape[0]
        hd = C // H
        scale = hd ** (-0.5)
        nb = N // BS
        dtype = x.dtype
        attn_mask, edge_feats = _build_leaf_block_connectivity(edge_index, edge_values, positions, nb, dtype)
        x_blk = x.reshape(B, nb, BS, C)
        block_node = x_blk.mean(axis=2, keepdims=True)
        kv = jnp.concatenate([x_blk, block_node], axis=2)
        qkv_q = x_blk @ qkv_w + qkv_b
        qkv_kv = kv @ qkv_w + qkv_b
        q = qkv_q[..., :C].reshape(B, nb, BS, H, hd)
        k = qkv_kv[..., C:2 * C].reshape(B, nb, BS + 1, H, hd)
        v = qkv_kv[..., 2 * C:].reshape(B, nb, BS + 1, H, hd)
        scores = jnp.einsum('bnqhd,bnkhd->bnqkh', q, k) * scale
        diag = jnp.arange(BS)
        w_bias = edge_feats[..., 3]
        w_bias = w_bias.at[:, :, BS].set(1.0)
        w_bias = w_bias.at[:, diag, diag].set(1.0)
        scores = scores + w_bias[None, :, :, :, None]
        mask = attn_mask[None, :, :, :, None]
        neg = jnp.asarray(-1000000000.0, dtype)
        scores = jnp.where(mask == 0, neg, scores)
        attn_probs = jax.nn.softmax(scores, axis=3)
        gate = w_bias[..., None] * gate_w[:, 0] + gate_b
        gate = jnp.where(mask[0] == 0, 0.0, gate)[None]
        combined = attn_probs + gate
        out = jnp.einsum('bnqkh,bnkhd->bnqhd', combined, v).reshape(B, N, C)
        return out @ proj_w + proj_b

    def _L1_ffn_ref(x, router_w, router_b, expert_w, expert_b):
        import jax, jax.numpy as jnp
        import numpy as np
        B, N, D, C, E, K = (8, 8192, 128, 128, 8, 2)
        router_probs = jax.nn.softmax(x @ router_w + router_b, axis=-1)
        top_p, top_i = jax.lax.top_k(router_probs, K)
        top_p = top_p / jnp.sum(top_p, axis=-1, keepdims=True)
        expert_out = jnp.einsum('bnd,edc->bnec', x, expert_w) + expert_b
        gathered = jnp.take_along_axis(expert_out, top_i[..., None], axis=2)
        return jnp.einsum('bnk,bnkc->bnc', top_p, gathered)

    def _gn(v, G=32, eps=1e-5):
        B_, C_, H_, W_ = v.shape
        g = v.reshape(B_, G, C_ // G, H_, W_)
        m = jnp.mean(g, axis=(2, 3, 4), keepdims=True)
        s = jnp.var(g, axis=(2, 3, 4), keepdims=True)
        return ((g - m) / jnp.sqrt(s + eps)).reshape(v.shape)

    def _ln_c(v, eps=1e-6):
        m = jnp.mean(v, axis=1, keepdims=True)
        s = jnp.var(v, axis=1, keepdims=True)
        return (v - m) / jnp.sqrt(s + eps)

    def _ln_t(v, eps=1e-5):
        m = jnp.mean(v, axis=-1, keepdims=True)
        s = jnp.var(v, axis=-1, keepdims=True)
        return (v - m) / jnp.sqrt(s + eps)

    def _to_tokens(v):
        B_, C_, H_, W_ = v.shape
        return v.reshape(B_, C_, H_ * W_).transpose(0, 2, 1)
    def _from_tokens(t, like):
        B_, C_, H_, W_ = like.shape
        return t.transpose(0, 2, 1).reshape(B_, C_, H_, W_)

    x = _L0_conv_ref(x, L0_conv_norm_w, L0_conv_norm_b, L0_conv_qkv_w, L0_conv_qkv_b, L0_conv_proj_w, L0_conv_proj_b)
    t = _to_tokens(x)
    t = t + _L1_attn_ref(_ln_t(t), L1_attn_edge_index, L1_attn_edge_values, L1_attn_positions, L1_attn_qkv_w, L1_attn_qkv_b, L1_attn_proj_w, L1_attn_proj_b, L1_attn_gate_w, L1_attn_gate_b)
    t = t + _L1_ffn_ref(_ln_t(t), L1_ffn_router_w, L1_ffn_router_b, L1_ffn_expert_w, L1_ffn_expert_b)
    x = _from_tokens(t, x)
    return x


_drawn_inputs = setup_inputs


def setup_inputs(seed=0):
    import zlib

    import numpy as np

    out = dict(_drawn_inputs(seed))
    spreads = {'L0_conv_norm_w': (1.0, 0.2),
     'L0_conv_norm_b': (0.0, 0.1),
     'L0_conv_qkv_b': (0.0, 0.1),
     'L0_conv_proj_b': (0.0, 0.1),
     'L1_attn_qkv_b': (0.0, 0.1),
     'L1_attn_proj_b': (0.0, 0.1),
     'L1_attn_gate_b': (0.0, 0.1),
     'L1_ffn_router_b': (0.0, 0.1),
     'L1_ffn_expert_b': (0.0, 0.1)}
    factors = {'L1_attn_gate_w': 3.17}
    for name, (base, spread) in spreads.items():
        noise = np.random.default_rng([zlib.crc32(name.encode()), seed]).standard_normal(out[name].shape)
        drawn = base * np.exp(spread * noise) if base else spread * noise
        out[name] = jnp.asarray(drawn.astype(out[name].dtype))
    for name, factor in factors.items():
        out[name] = (out[name] * factor).astype(out[name].dtype)
    return out
```

```python
from contextlib import ExitStack

import concourse.bass as bass
from concourse import mybir

F32 = mybir.dt.float32
F16 = mybir.dt.float16
I32 = mybir.dt.int32
U32 = mybir.dt.uint32
ALU = mybir.AluOpType
ACT = mybir.ActivationFunctionType
AX = mybir.AxisListType

C = 128
B = 4
N = 4096
HEADS = 4
D = C // HEADS
SCALE = float(D) ** -0.5
CH = 512
NCH = N // CH
KT = N // 128
QT = CH // 128
GN_EPS = 1e-5
GROUP = C // 8
MROW = 16.0

BS = 32
E = 4194304
EP = E // 128
SLOTS = N * BS
PIECE = 2048
RUN = 64
RUNS = EP // RUN
GRP = 512
KEEP = 80
GRPS = RUNS * 8 // GRP
LIST = GRPS * KEEP
SLOT_BITS = 17
BATCH = 8
NOWHERE = 1 << 24


class Steps:

    def __init__(self, eng, sem):
        self.eng, self.sem, self.base, self.n = eng, sem, 0, 0

    def inc(self, ins):
        self.n += 1
        return ins.then_inc(self.sem, 1)

    def sync(self):
        self.eng.wait_ge(self.sem, self.base + self.n)

    def sync_apart(self, scratch):
        self.eng.wait_ge(self.sem, self.base + self.n)
        self.eng.memset(scratch, 0.0)

    def at(self, base):
        self.base, self.n = base, 0


def attention_half(nc, ctx, t, half, pool_program):
    x_all, qs, ks, vones, ident = t["x_all"], t["qs"], t["ks"], t["vones"], t["ident"]
    probs, o_t, rden, mx8, mx, mrow = t["probs"], t["o_t"], t["rden"], t["mx8"], t["mx"], t["mrow"]
    xn, part, wqkv, qkv_b, vbias = t["xn"], t["part"], t["wqkv"], t["qkv_b"], t["vbias"]
    S, O, M = t["S"], t["O"], t["M"]
    IMGS = 2

    def sem(name):
        return ctx.enter_context(nc.semaphore(f"{name}_{half}"))

    xn_ready = sem("xn_ready")
    qkv_done = sem("qkv_done")
    qkv_taken = sem("qkv_taken")
    stack_in = sem("stack_in")
    s_ready = sem("s_ready")
    p_ready = sem("p_ready")
    o_added = sem("o_added")
    m_ready = sem("m_ready")
    m_taken = sem("m_taken")
    mx_final = sem("mx_final")
    mt_ready = sem("mt_ready")
    mrow_out = sem("mrow_out")
    mrow_in = sem("mrow_in")
    o_taken = sem("o_taken")
    y_ready = sem("y_ready")
    y_taken = sem("y_taken")
    dve_own = sem("dve_own")

    STEPS = KT * 2
    TILES = HEADS * QT * NCH
    NM = TILES // STEPS
    PARTS = 6 * HEADS * 16

    def tile_of(n):
        return n // (QT * NCH), (n // NCH) % QT, n % NCH

    block = ctx.enter_context(nc.Block())

    @block.scalar
    def _(act):
        with act.Fori(0, IMGS) as img:
            b = img + half * IMGS
            with act.Fori(0, NCH // 2) as c2:
                for j in range(2):
                    turn = img * NCH + c2 * 2 + j
                    act.wait_ge(qkv_done, turn - 1 if j else turn - 0)
                    act.activation(xn[:, j, :], x_all[:, bass.ds(b * N + c2 * (2 * CH) + j * CH, CH)],
                                   ACT.Identity, scale=t["gn_a"][:, bass.ds(b, 1)],
                                   bias=t["gn_b"][:, bass.ds(b, 1)]).then_inc(xn_ready, 1)
            with act.Fori(0, NCH) as c:
                turn = (img * NCH + c) * STEPS
                for s in range(STEPS):
                    act.wait_ge(s_ready, turn + (s + 1))
                    if s >= 3:
                        act.wait_ge(o_added, turn + (s - 2))
                    act.activation(probs[:, s % 3, :], S[:, s % 2, :], ACT.Exp, scale=SCALE) \
                       .then_inc(p_ready, 1)

    @block.tensor
    def _(pe):
        def max_tile(n, turn, q_at):
            h, qt, kc = tile_of(n)
            pe.matmul(M[:, n % 2, :], qs[0:96, bass.ds(q_at + (h * CH + qt * 128), 128)],
                      ks[0:96, h, kc * CH:(kc + 1) * CH], start=True, stop=True).then_inc(m_ready, 1)

        def transpose_maxima(count):
            pe.wait_ge(mx_final, count)
            pe.matmul(M[0:HEADS * QT, 0, 0:128], mx[:, :], ident[:, :], start=True, stop=True) \
              .then_inc(mt_ready, 1)

        with pe.Fori(0, IMGS) as img:
            with pe.Fori(0, NCH // 2) as c2:
                for j in range(2):
                    turn = img * NCH + c2 * 2 + j
                    if j == 0:
                        pe.wait_ge(y_taken, img * NCH)
                        pe.wait_ge(mrow_out, img * (NCH + 1))
                    pe.wait_ge(qkv_taken, turn)
                    pe.wait_ge(xn_ready, turn + 1)
                    pe.matmul(M[:, 0, :], wqkv[:, 0:C], xn[:, j, :], start=True, stop=True)
                    pe.matmul(M[:, 1, :], wqkv[:, C:2 * C], xn[:, j, :], start=True, stop=True)
                    for k in range(QT):
                        last = pe.matmul(O[:, 0, k * C:(k + 1) * C], xn[:, j, k * 128:(k + 1) * 128],
                                         wqkv[:, 2 * C:3 * C], start=True, stop=True)
                    last.then_inc(qkv_done, 1)
            pe.wait_ge(stack_in, (img + 1) * (NCH * PARTS))
            pe.wait_ge(qkv_taken, (img + 1) * NCH)
            for n in range(TILES):
                mturn = img * ((NCH + 1) * TILES)
                if n >= 2:
                    pe.wait_ge(m_taken, mturn + (n - 1))
                max_tile(n, mturn, 0)
            transpose_maxima(img * (NCH + 1) + 1)
            with pe.Fori(0, NCH) as c:
                chunk = img * NCH + c
                turn = chunk * STEPS
                mturn = (img * (NCH + 1) + c + 1) * TILES
                q_at = c * (HEADS * CH)
                q_next = (c + 1) % NCH * (HEADS * CH)
                pe.wait_ge(mrow_in, (img * (NCH + 1) + c + 1) * 16)
                for s in range(STEPS + 1):
                    kt, hp = s // 2, s % 2
                    if s < STEPS:
                        pe.wait_ge(p_ready, turn + max(s - 1, 0))
                        for h in (2 * hp, 2 * hp + 1):
                            last = pe.matmul(S[:, s % 2, (h % 2) * CH:(h % 2 + 1) * CH],
                                             ks[0:97, h, kt * 128:(kt + 1) * 128],
                                             qs[0:97, bass.ds(q_at + h * CH, CH)], start=True, stop=True)
                        last.then_inc(s_ready, 1)
                        for n in range(NM * s, NM * s + NM):
                            if n >= 2:
                                pe.wait_ge(m_taken, mturn + (n - 1))
                            elif n == 0:
                                pe.wait_ge(mrow_out, img * (NCH + 1) + c + 1)
                            max_tile(n, mturn, q_next)
                    if s >= 1:
                        pt, ph = (s - 1) // 2, (s - 1) % 2
                        if s == 1:
                            pe.wait_ge(y_taken, chunk)
                        pe.wait_ge(p_ready, turn + s)
                        for j in range(2):
                            last = pe.matmul(O[64 * j:64 * j + 64, ph, :], vones[:, pt, 2 * ph + j, :],
                                             probs[:, (s - 1) % 3, j * CH:(j + 1) * CH],
                                             start=(pt == 0), stop=(pt == KT - 1))
                        last.then_inc(o_added, 1)
                transpose_maxima(img * (NCH + 1) + c + 2)
                pe.wait_ge(o_taken, chunk + 1)
                pe.matmul(O[:, 0, :], t["proj_w"][:, :], o_t[:, :], start=True, stop=True) \
                  .then_inc(y_ready, 1)

    @block.vector
    def _(dve):
        own = Steps(dve, dve_own)
        OWN_PREP, OWN_CHUNK = 2, 1
        OWN_IMG = NCH * (OWN_PREP + OWN_CHUNK)

        def maxima(n, mturn):
            h, qt, kc = tile_of(n)
            dve.wait_ge(m_ready, mturn + (n + 1))
            dve.reduce_max(mx8[:, h * QT + qt, kc:kc + 1], M[:, n % 2, :], AX.X).then_inc(m_taken, 1)

        def finish_maxima(count, mturn):
            dve.wait_ge(m_taken, mturn + TILES)
            dve.reduce_max(mx[:, :], mx8[:, :, :], AX.X).then_inc(mx_final, 1)
            dve.wait_ge(mt_ready, count)
            dve.wait_ge(mrow_in, (count - 1) * 16)
            dve.tensor_scalar(mrow[:, :], M[0:HEADS * QT, 0, 0:128], -1.0 / MROW, None, ALU.mult) \
               .then_inc(mrow_out, 1)

        with dve.Fori(0, IMGS) as img:
            with dve.Fori(0, NCH // 2) as c2:
                for j in range(2):
                    turn = img * NCH + c2 * 2 + j
                    own.at(img * OWN_IMG + (c2 * 2 + j) * OWN_PREP)
                    dve.wait_ge(qkv_done, turn + 1)
                    if j == 0:
                        dve.wait_ge(stack_in, (img * NCH + c2 * 2) * PARTS)
                    for m in range(2):
                        own.inc(dve.tensor_scalar(part[:, j, 2 * m, :], M[:, m, :], qkv_b[:, m:m + 1],
                                                  None, ALU.add))
                    dve.tensor_tensor(vones[:, bass.ds(c2 * (2 * QT) + j * QT, QT), :, 0:D],
                                      O[:, 0, :].rearrange("p (k h d) -> p k h d", k=QT, h=HEADS),
                                      vbias[:, :, :, :], ALU.add)
                    own.sync()
                    for m in range(2):
                        last = dve.scalar_tensor_tensor(part[:, j, 2 * m + 1, :], M[:, m, :],
                                                        qkv_b[:, m:m + 1], part[:, j, 2 * m, :],
                                                        ALU.add, ALU.subtract)
                    last.then_inc(qkv_taken, 1)
            mturn = img * ((NCH + 1) * TILES)
            for n in range(TILES):
                maxima(n, mturn)
            finish_maxima(img * (NCH + 1) + 1, mturn)
            with dve.Fori(0, NCH) as c:
                chunk = img * NCH + c
                mturn = (img * (NCH + 1) + c + 1) * TILES
                for n in range(TILES):
                    maxima(n, mturn)
                finish_maxima(img * (NCH + 1) + c + 2, mturn)
                dve.wait_ge(o_added, (chunk + 1) * STEPS)
                for h in range(HEADS):
                    r = 64 * (h % 2)
                    last = dve.reciprocal(rden[r:r + D, h // 2, :], O[r + D:r + 2 * D, h // 2, :])
                last.then_inc(dve_own, 1)
                dve.wait_ge(dve_own, img * OWN_IMG + NCH * OWN_PREP + c + 1)
                for h in range(HEADS):
                    r = 64 * (h % 2)
                    last = dve.tensor_tensor(o_t[h * D:(h + 1) * D, :], O[r:r + D, h // 2, :],
                                             rden[r:r + D, h // 2, :], ALU.mult)
                last.then_inc(o_taken, 1)
                x_now = x_all[:, bass.ds((img + half * IMGS) * N + c * CH, CH)]
                dve.wait_ge(y_ready, chunk + 1)
                dve.scalar_tensor_tensor(x_now, O[:, 0, :], t["proj_b"][:, 0:1], x_now,
                                         ALU.add, ALU.add).then_inc(y_taken, 1)

    @block.sync
    def _(sp):
        with sp.Fori(0, IMGS) as img:
            with sp.Fori(0, NCH // 2) as c2:
                for j in range(2):
                    turn = img * NCH + c2 * 2 + j
                    sp.wait_ge(qkv_taken, turn + 1)
                    for h in range(HEADS):
                        rows = slice(h * D, (h + 1) * D)
                        for r, (qp, kp) in enumerate(((0, 2), (0, 3), (1, 2))):
                            sp.dma_start(qs[r * D:(r + 1) * D, bass.ds(c2 * (2 * HEADS * CH) + (j * HEADS + h) * CH, CH)],
                                         part[rows, j, qp, :]).then_inc(stack_in, 16)
                            sp.dma_start(ks[r * D:(r + 1) * D, h, bass.ds(c2 * (2 * CH) + j * CH, CH)],
                                         part[rows, j, kp, :]).then_inc(stack_in, 16)
            with sp.Fori(0, NCH + 1) as c:
                count = img * (NCH + 1) + c + 1
                sp.wait_ge(mrow_out, count)
                sp.dma_start(qs[96:97, bass.ds(c % NCH * (HEADS * CH), HEADS * CH)]
                             .rearrange("p (r q) -> p r q", q=128), mrow[:, :]).then_inc(mrow_in, 16)
        sp.wait_ge(mrow_in, IMGS * (NCH + 1) * 16)

    @block.gpsimd
    def _(pool):
        pool_program(pool)


def constants_and_norm(nc, ctx, t, a):
    x_all = t["x_all"]

    def sem(name):
        return ctx.enter_context(nc.semaphore(name))

    def sb(name, shape, dt=F32):
        return ctx.enter_context(nc.sbuf_tensor(name, shape, dt))

    loaded = [sem(f"x_loaded_{b}") for b in range(B)]
    w_loaded, made = sem("w_loaded"), sem("constants_made")
    own_sem, gsum, rooted, ident_made = sem("norm_own"), sem("group_sums"), sem("rooted"), sem("ident_made")
    NST = N // 512
    stats = sb("stats", [128, B, NST, 6])
    mv = sb("mv", [128, B, 2])
    gmat = sb("gmat", [128, C])
    var = sb("gvar", [128, B])
    std = sb("gstd", [128, B])
    tmp = sb("gtmp", [128, B])
    normw = sb("normw", [128, 2])
    eps = sb("eps", [128, 1])
    G = t["M"]
    block = ctx.enter_context(nc.Block())
    W_LOADS = 11

    @block.sync
    def _(sp):
        for b in range(B):
            sp.dma_start(x_all[:, b * N:(b + 1) * N], a["x"][b]).then_inc(loaded[b], 16)

    @block.scalar
    def _(act):
        act.dma_start(t["wqkv"][:, :], a["qkv_wT"]).then_inc(w_loaded, 16)
        for m in range(2):
            act.dma_start(t["qkv_b"][:, m:m + 1], a["qkv_b"][m * C:(m + 1) * C].rearrange("(p o) -> p o", o=1)) \
               .then_inc(w_loaded, 16)
        for k in range(QT):
            act.dma_start(t["vbias"][:, k, :, :],
                          a["qkv_b"][2 * C:3 * C].rearrange("(o h d) -> o h d", o=1, h=HEADS)
                          .broadcast_to([128, HEADS, D])).then_inc(w_loaded, 16)
        act.dma_start(t["proj_w"][:, :], a["proj_wT"]).then_inc(w_loaded, 16)
        act.dma_start(t["proj_b"][:, 0:1], a["proj_b"].rearrange("(p o) -> p o", o=1)).then_inc(w_loaded, 16)
        act.dma_start(normw[:, 0:1], a["norm_w"].rearrange("(p o) -> p o", o=1)).then_inc(w_loaded, 16)
        act.dma_start(normw[:, 1:2], a["norm_b"].rearrange("(p o) -> p o", o=1)).then_inc(w_loaded, 16)
        act.wait_ge(own_sem, 2 * B + 3)
        act.activation(std[:, :], var[:, :], ACT.Sqrt, bias=eps[:, 0:1]).then_inc(rooted, 1)
        act.wait_ge(w_loaded, W_LOADS * 16)

    @block.gpsimd
    def _(pool):
        pool.memset(t["ident"][:, :], 0.0).then_inc(ident_made, 1)
        pool.memset(eps[:, :], GN_EPS).then_inc(made, 1)
        pool.memset(gmat[:, :], 1.0 / GROUP).then_inc(ident_made, 1)
        pool.wait_ge(ident_made, 2)
        pool.affine_select(out=t["ident"][:, :], in_=t["ident"][:, :], compare_op=ALU.not_equal, fill=1.0,
                           base=0, pattern=[[-1, 128]], channel_multiplier=1).then_inc(ident_made, 1)
        g3 = gmat[:, :].rearrange("p (g c) -> p g c", c=GROUP)
        pool.affine_select(out=g3, in_=g3, compare_op=ALU.is_ge, fill=0.0, base=0,
                           pattern=[[-GROUP, C // GROUP], [0, GROUP]], channel_multiplier=1).then_inc(ident_made, 1)
        pool.wait_ge(ident_made, 4)
        pool.affine_select(out=g3, in_=g3, compare_op=ALU.is_ge, fill=0.0, base=GROUP - 1,
                           pattern=[[GROUP, C // GROUP], [0, GROUP]], channel_multiplier=-1).then_inc(made, 1)
        pool.memset(t["vones"][:, :, :, D:2 * D], 1.0).then_inc(ident_made, 1)
        pool.wait_ge(ident_made, 5)
        pool.memset(t["ks"][96:97, :, :], MROW)

    @block.vector
    def _(dve):
        own = Steps(dve, own_sem)
        for b in range(B):
            dve.wait_ge(loaded[b], 16)
            for k in range(NST):
                last = dve.bn_stats(stats[:, b, k, :], x_all[:, b * N + k * 512:b * N + (k + 1) * 512])
            own.inc(last)
            own.sync()
            own.inc(dve.bn_aggr(mv[:, b, :], stats[:, b, :, :]))
        own.sync()
        own.inc(dve.tensor_tensor(tmp[:, :], mv[:, :, 0], mv[:, :, 0], ALU.mult))
        own.sync()
        own.inc(dve.tensor_tensor(mv[:, :, 1], mv[:, :, 1], tmp[:, :], ALU.add))
        dve.wait_ge(gsum, 1)
        own.sync()
        dve.tensor_copy(mv[:, :, :], G[:, 0, 0:2 * B].rearrange("p (b k) -> p b k", k=2)).then_inc(gsum, 1)
        dve.wait_ge(gsum, 2)
        dve.tensor_tensor(tmp[:, :], mv[:, :, 0], mv[:, :, 0], ALU.mult).then_inc(gsum, 1)
        dve.wait_ge(gsum, 3)
        own.inc(dve.tensor_tensor(var[:, :], mv[:, :, 1], tmp[:, :], ALU.subtract))
        dve.wait_ge(rooted, 1)
        own.inc(dve.reciprocal(std[:, :], std[:, :]))
        own.sync()
        dve.wait_ge(w_loaded, W_LOADS * 16)
        own.inc(dve.tensor_scalar(t["gn_a"][:, :], std[:, :], normw[:, 0:1], None, ALU.mult))
        own.sync()
        own.inc(dve.tensor_tensor(tmp[:, :], mv[:, :, 0], t["gn_a"][:, :], ALU.mult))
        own.sync()
        own.inc(dve.tensor_scalar(t["gn_b"][:, :], tmp[:, :], -1.0, normw[:, 1:2], ALU.mult, ALU.add))

    @block.tensor
    def _(pe):
        pe.wait_ge(made, 2)
        pe.wait_ge(own_sem, 2 * B + 2)
        pe.matmul(G[:, 0, 0:2 * B], gmat[:, :], mv[:, :, :].rearrange("p b k -> p (b k)"),
                  start=True, stop=True).then_inc(gsum, 1)


def slots_of(dve, own, rows, cols, base, work):
    w0, w1 = work
    own.inc(dve.tensor_scalar(w1, rows, ~(N - 1), None, ALU.bitwise_and))
    own.inc(dve.tensor_tensor(w0, rows, cols, ALU.bitwise_xor))
    own.sync()
    own.inc(dve.scalar_tensor_tensor(w0, w0, ~(BS - 1), w1, ALU.bitwise_and, ALU.bitwise_or))
    own.sync()
    if base is None:
        own.inc(dve.tensor_scalar(w1, cols, BS - 1, None, ALU.bitwise_and))
    else:
        own.inc(dve.scalar_tensor_tensor(w1, cols, BS - 1, base, ALU.bitwise_and, ALU.bitwise_or))
    own.sync()
    own.inc(dve.scalar_tensor_tensor(w1, rows, 5, w1, ALU.logical_shift_left, ALU.bitwise_or))
    own.sync()


def scatter_index(dve, own, xs, pcol, idx, dup, eq, n):
    own.inc(dve.memset(dup, 0.0))
    own.sync()
    x3 = xs.rearrange("p (n k) -> p n k", k=BATCH)
    d3 = dup.rearrange("p (n k) -> p n k", k=BATCH)
    e3 = eq.rearrange("p (n k) -> p n k", k=BATCH)
    for sft in range(1, BATCH):
        own.inc(dve.tensor_tensor(e3[:, :, 0:BATCH - sft], x3[:, :, 0:BATCH - sft], x3[:, :, sft:BATCH],
                                  ALU.is_equal))
        own.sync()
        own.inc(dve.tensor_tensor(d3[:, :, 0:BATCH - sft], d3[:, :, 0:BATCH - sft],
                                  e3[:, :, 0:BATCH - sft], ALU.max))
        own.sync()
    own.inc(dve.tensor_scalar(eq, xs, float(1 << SLOT_BITS), None, ALU.is_ge))
    own.sync()
    own.inc(dve.tensor_tensor(dup, dup, eq, ALU.max))
    own.inc(dve.tensor_scalar(idx, xs, SLOTS - 1, 7, ALU.bitwise_and, ALU.logical_shift_left))
    own.sync()
    own.inc(dve.tensor_tensor(idx, idx, pcol.to_broadcast([128, n]), ALU.bitwise_or))
    own.sync()
    own.inc(dve.scalar_tensor_tensor(idx, dup, 24, idx, ALU.logical_shift_left, ALU.bitwise_or))
    own.sync()


def edge_lists(nc, ctx, t, a, table):
    def sem(name):
        return ctx.enter_context(nc.semaphore(name))

    def sb(name, shape, dt=F32):
        return ctx.enter_context(nc.sbuf_tensor(name, shape, dt))

    PIECES = EP // PIECE
    loaded = [sem(f"edges_loaded_{j}") for j in range(2)]
    made, taken, own_sem, cleared, zeroed = (sem(n) for n in
        ("edge_consts", "piece_taken", "edge_own", "table_cleared", "zero_made"))
    rc = sb("edge_rc", [128, 2, 2, PIECE], I32)
    base = sb("edge_base", [128, PIECE], I32)
    w0, w1 = sb("edge_w0", [128, PIECE], I32), sb("edge_w1", [128, PIECE], I32)
    key = sb("edge_key", [128, PIECE])
    top = sb("edge_top", [128, PIECE // RUN * 8])
    k1 = sb("edge_k1", [128, RUNS * 8])
    g_f = sb("grp_f", [128, GRP])
    g_i = sb("grp_i", [128, GRP], I32)
    g_j = sb("grp_j", [128, GRP], I32)
    ridx = sb("grp_ridx", [128, GRP], I32)
    ga, gb = sb("grp_a", [128, GRP]), sb("grp_b", [128, GRP])
    la, lb = sb("grp_la", [128, KEEP]), sb("grp_lb", [128, KEEP])
    lists = [sb(f"list_{n}", [128, LIST]) for n in "ab"]
    li = [sb(f"list_i{n}", [128, LIST], I32) for n in range(6)]
    ebase = sb("list_ebase", [128, GRPS, KEEP])
    zero = sb("edge_zero", [128, 4096])
    row_max = sb("ovf_max", [128, 2])
    gate = sb("edge_gate", [128, 1])
    block = ctx.enter_context(nc.Block())
    ZEROS = SLOTS // 32

    @block.sync
    def _(sp):
        with sp.Fori(0, PIECES // 2) as q:
            for j in range(2):
                sp.wait_ge(taken, q * 2 + j - 1 if j else q * 2)
                for m in range(2):
                    sp.dma_start(rc[:, j, m, :], a["edges"][m].rearrange("(p e) -> p e", p=128)
                                 [:, bass.ds(q * (2 * PIECE) + j * PIECE, PIECE)]).then_inc(loaded[j], 16)
        sp.wait_ge(cleared, 32 * 16)

    @block.scalar
    def _(act):
        act.wait_ge(zeroed, 1)
        with act.Fori(0, 32) as z:
            act.dma_start(table[bass.ds(z * ZEROS, ZEROS), :].rearrange("(p r) c -> p (r c)", p=128),
                          zero[:, :]).then_inc(cleared, 16)

    @block.gpsimd
    def _(pool):
        pool.memset(zero[:, :], 0.0).then_inc(zeroed, 1)
        pool.iota(base[:, :], pattern=[[0, PIECE // RUN], [-1, RUN]], base=RUN, channel_multiplier=0) \
            .then_inc(made, 1)
        pool.iota(ridx[:, :], pattern=[[-1, GRP]], base=GRP, channel_multiplier=0).then_inc(made, 1)
        pool.iota(t["pcol"][:, :], pattern=[[0, 1]], base=0, channel_multiplier=1).then_inc(made, 1)
        pool.iota(ebase[:, :, :], pattern=[[GRP // 8 * RUN, GRPS], [0, KEEP]], base=RUN + 1,
                  channel_multiplier=EP, allow_small_or_imprecise_dtypes=True).then_inc(made, 1)

    @block.vector
    def _(dve):
        own = Steps(dve, own_sem)
        dve.wait_ge(made, 4)
        own.inc(dve.tensor_scalar(base[:, :], base[:, :], SLOT_BITS, None, ALU.logical_shift_left))
        own.inc(dve.tensor_scalar(ridx[:, :], ridx[:, :], 12, None, ALU.logical_shift_left))
        own.sync()
        OWN_PIECE = 7
        start = own.n
        with dve.Fori(0, PIECES // 2) as q:
            for j in range(2):
                own.at(q * (2 * OWN_PIECE) + (start + j * OWN_PIECE))
                dve.wait_ge(loaded[j], q * 32 + 32)
                slots_of(dve, own, rc[:, j, 0, :], rc[:, j, 1, :], base[:, :], (w0[:, :], w1[:, :]))
                own.inc(dve.scalar_tensor_tensor(key[:, :], w0[:, :], 0.0, w1[:, :], ALU.is_equal, ALU.mult))
                own.sync_apart(gate[:, 0:1])
                for r in range(PIECE // RUN):
                    last = dve.max(top[:, r * 8:(r + 1) * 8], key[:, r * RUN:(r + 1) * RUN])
                own.inc(last)
                own.sync()
                dve.tensor_copy(k1[:, bass.ds(q * (2 * PIECE // RUN * 8) + j * (PIECE // RUN * 8), PIECE // RUN * 8)],
                                top[:, :]).then_inc(taken, 1)
                assert own.n == OWN_PIECE
        dve.wait_ge(taken, PIECES)
        own.at(PIECES * OWN_PIECE + start)
        own.inc(dve.reduce_max(row_max[:, 0:1], k1[:, 7::8], AX.X))
        start = PIECES * OWN_PIECE + start + 1
        OWN_GRP = 7 + 4 * (KEEP // 8)
        with dve.Fori(0, GRPS) as g:
            own.at(g * OWN_GRP + start)
            own.inc(dve.tensor_copy(g_i[:, :], k1[:, bass.ds(g * GRP, GRP)]))
            own.sync()
            for m, gk in ((0, ga), (1, gb)):
                if m:
                    own.inc(dve.tensor_scalar(g_j[:, :], g_i[:, :], 4095, None, ALU.bitwise_and))
                else:
                    own.inc(dve.tensor_scalar(g_j[:, :], g_i[:, :], 12, None, ALU.logical_shift_right))
                own.sync()
                own.inc(dve.tensor_tensor(g_j[:, :], g_j[:, :], ridx[:, :], ALU.bitwise_or))
                own.sync()
                own.inc(dve.scalar_tensor_tensor(gk[:, :], g_i[:, :], 0.0, g_j[:, :], ALU.is_gt, ALU.mult))
                own.sync_apart(gate[:, 0:1]) if m else own.sync()
            for r in range(KEEP // 8):
                for gk, lk in ((ga, la), (gb, lb)):
                    own.inc(dve.max(lk[:, r * 8:(r + 1) * 8], gk[:, :]))
                own.sync_apart(gate[:, 0:1])
                for gk, lk in ((ga, la), (gb, lb)):
                    own.inc(dve.match_replace(gk[:, :], lk[:, r * 8:(r + 1) * 8], gk[:, :], 0.0))
                own.sync_apart(gate[:, 0:1])
            assert own.n == OWN_GRP
            dve.tensor_copy(lists[0][:, bass.ds(g * KEEP, KEEP)], la[:, :])
            dve.tensor_copy(lists[1][:, bass.ds(g * KEEP, KEEP)], lb[:, :]).then_inc(taken, 1)
        own.at(GRPS * OWN_GRP + start)
        dve.wait_ge(taken, PIECES + GRPS)
        own.inc(dve.reduce_max(row_max[:, 1:2], lists[0][:, KEEP - 1::KEEP], AX.X))
        own.inc(dve.tensor_copy(li[0][:, :], lists[0][:, :]))
        own.inc(dve.tensor_copy(li[1][:, :], lists[1][:, :]))
        own.sync()
        own.inc(dve.reduce_max(t["ovf"][:, 0:1], row_max[:, :], AX.X))
        own.inc(dve.tensor_scalar(li[2][:, :], li[0][:, :], 4095, 12, ALU.bitwise_and, ALU.logical_shift_left))
        own.inc(dve.tensor_scalar(li[3][:, :], li[1][:, :], 4095, None, ALU.bitwise_and))
        own.inc(dve.tensor_scalar(li[0][:, :], li[0][:, :], 12, None, ALU.logical_shift_right))
        own.sync()
        own.inc(dve.tensor_tensor(li[2][:, :], li[2][:, :], li[3][:, :], ALU.bitwise_or))
        own.inc(dve.tensor_scalar(li[0][:, :], li[0][:, :], -1.0, float(GRP), ALU.mult, ALU.add))
        own.sync()
        own.inc(dve.tensor_scalar(li[1][:, :], li[2][:, :], SLOT_BITS, None, ALU.logical_shift_right))
        own.inc(dve.tensor_scalar(li[2][:, :], li[2][:, :], SLOTS - 1, None, ALU.bitwise_and))
        own.inc(dve.tensor_scalar(li[0][:, :], li[0][:, :], 3, None, ALU.logical_shift_right))
        own.sync()
        own.inc(dve.scalar_tensor_tensor(lists[0][:, :], li[0][:, :], float(RUN), li[1][:, :], ALU.mult, ALU.subtract))
        own.inc(dve.tensor_scalar(li[3][:, :], li[1][:, :], 0.0, float(SLOTS), ALU.is_equal, ALU.mult))
        own.sync()
        own.inc(dve.tensor_tensor(t["list_e"][:, :], lists[0][:, :],
                                  ebase[:, :, :].rearrange("p g k -> p (g k)"), ALU.add))
        own.inc(dve.tensor_tensor(li[2][:, :], li[2][:, :], li[3][:, :], ALU.bitwise_or))
        own.sync()
        scatter_index(dve, own, li[2][:, :], t["pcol"][:, 0:1], t["list_idx"][:, :].bitcast(I32), li[4][:, :], li[5][:, :], LIST)


def scatter_batches(pool, n, idx, ev, idx8, ev8, table, landed):
    flat = table.rearrange("s (c o) -> (s c) o", o=1)
    with pool.Fori(0, n // BATCH) as r:
        pool.drain()
        pool.tensor_copy(idx8[:, :], idx[:, bass.ds(r * BATCH, BATCH)])
        pool.tensor_copy(ev8[:, :], ev[:, bass.ds(r * BATCH, BATCH)])
        pool.drain()
        for k in range(BATCH):
            pool.indirect_dma_start(flat, bass.IndirectOffsetOnAxis(ap=idx8[:, k:k + 1], axis=0),
                                    ev8[:, k:k + 1], None, bounds_check=NOWHERE - 1,
                                    oob_is_err=False).then_inc(landed, 16)
    pool.drain()


def scatter_lists(nc, ctx, t, table):
    landed = ctx.enter_context(nc.semaphore("list_landed"))
    reduced = ctx.enter_context(nc.semaphore("ovf_reduced"))

    def program(pool):
        pool.partition_all_reduce(t["ovf_all"][:, :], t["ovf"][:, :], 128, bass.bass_isa.ReduceOp.max) \
            .then_inc(reduced, 1)
        pool.wait_ge(reduced, 1)
        scatter_batches(pool, LIST, t["list_idx"], t["list_e"], t["idx8"], t["ev8"], table, landed)
        pool.wait_ge(landed, LIST * 16)
    return program


def last_edges(nc, ctx, t, a, table, scratch_m):
    def sem(name):
        return ctx.enter_context(nc.semaphore(name))

    loaded, made, sent, own_sem, landed, ev_made = (sem(n) for n in
        ("gen_loaded", "gen_index_made", "gen_sent", "gen_own", "gen_landed", "gen_ev_made"))
    t_loaded = [sem(f"table_loaded_{j}") for j in range(2)]
    reduced, masked, stored = sem("table_reduced"), sem("mask_made"), sem("mask_stored")
    GP = 512
    PIECES = EP // GP
    pool_of_space = t["qs"][:, :].bitcast(I32)
    rows, cols, w0, w1, idx, dup, eq, ev = (pool_of_space[:, n * GP:(n + 1) * GP] for n in range(8))
    ev = ev.bitcast(F32)
    mask = pool_of_space[:, 0:SLOTS // 128].bitcast(F32)
    TS = 16
    TP = (SLOTS // 128) // TS
    piece = pool_of_space[:, 8 * GP:8 * GP + 2 * TS * 128].bitcast(F32).rearrange("p (j s q) -> p j s q", j=2, q=128)
    block = ctx.enter_context(nc.Block())

    @block.sync
    def _(sp):
        full = sp.value_load(t["ovf_all"][0:1, 0:1].bitcast(I32), min_val=0, max_val=(1 << 31) - 1)
        with sp.If(full > 0):
            with sp.Fori(0, PIECES) as q:
                sp.wait_ge(made, q)
                for m, dst in ((0, rows), (1, cols)):
                    sp.dma_start(dst, a["edges"][m].rearrange("(p e) -> p e", p=128)[:, bass.ds(q * GP, GP)]) \
                      .then_inc(loaded, 16)
            sp.wait_ge(sent, PIECES)
        tab = table.rearrange("(b s) q -> b (s q)", b=128)
        with sp.Fori(0, TP // 2) as q:
            for j in range(2):
                sp.wait_ge(reduced, q * 2)
                sp.dma_start(piece[:, j, :, :].rearrange("p s q -> p (s q)"),
                             tab[:, bass.ds(q * (2 * TS * 128) + j * (TS * 128), TS * 128)]).then_inc(t_loaded[j], 16)
        sp.wait_ge(masked, 1)
        sp.dma_start(scratch_m, mask).then_inc(stored, 16)
        sp.wait_ge(stored, 16)

    @block.gpsimd
    def _(pool):
        full = pool.value_load(t["ovf_all"][0:1, 0:1].bitcast(I32), min_val=0, max_val=(1 << 31) - 1)
        with pool.If(full > 0):
            pool.iota(ev, pattern=[[1, GP]], base=1 - GP, channel_multiplier=EP,
                      allow_small_or_imprecise_dtypes=True).then_inc(ev_made, 1)
            with pool.Fori(0, PIECES) as q:
                pool.wait_ge(made, q + 1)
                pool.tensor_tensor(t["ev8"][:, :], t["ev8"][:, :], t["ev8"][:, :], ALU.add)
                scatter_batches(pool, GP, idx.bitcast(U32), ev, t["idx8"], t["ev8"], table, landed)
                pool.wait_ge(landed, GP * 16)
                pool.inc_swdge_sem([landed], [GP * 16], mode="sub")
                pool.memset(t["ev8"][:, 0:1], 0.0).then_inc(sent, 1)

    @block.vector
    def _(dve):
        own = Steps(dve, own_sem)
        full = dve.value_load(t["ovf_all"][0:1, 0:1].bitcast(I32), min_val=0, max_val=(1 << 31) - 1)
        with dve.If(full > 0):
            dve.wait_ge(ev_made, 1)
            OWN = 5 + 3 + 1 + 2 * (BATCH - 1) + 5 + 1 - 1
            with dve.Fori(0, PIECES) as q:
                own.at(q * OWN)
                dve.wait_ge(sent, q)
                dve.wait_ge(loaded, q * 32 + 32)
                slots_of(dve, own, rows, cols, None, (w0, w1))
                own.inc(dve.tensor_scalar(w0, w0, 0.0, float(SLOTS), ALU.not_equal, ALU.mult))
                own.inc(dve.tensor_scalar(w1, w1, SLOTS - 1, None, ALU.bitwise_and))
                own.sync()
                own.inc(dve.tensor_tensor(w1, w1, w0, ALU.bitwise_or))
                own.sync()
                scatter_index(dve, own, w1, t["pcol"][:, 0:1], idx, dup, eq, GP)
                assert own.n == OWN, own.n
                dve.tensor_scalar(ev, ev, float(GP), None, ALU.add).then_inc(made, 1)
        with dve.Fori(0, TP // 2) as q:
            for j in range(2):
                dve.wait_ge(t_loaded[j], q * 16 + 16)
                dve.tensor_reduce(t["t_edge"][:, bass.ds(q * (2 * TS) + j * TS, TS)], piece[:, j, :, :],
                                  AX.X, ALU.max).then_inc(reduced, 1)
        dve.wait_ge(reduced, TP)
        dve.tensor_scalar(mask, t["t_edge"][:, :], 0.0, None, ALU.is_gt).then_inc(masked, 1)
        dve.tensor_scalar(t["t_idx"][:, :], t["t_edge"][:, :], -1.0, 0.0, ALU.add, ALU.max)


def gather_values(nc, ctx, t, a, scratch_v):
    got = ctx.enter_context(nc.semaphore("values_got"))
    stored = ctx.enter_context(nc.semaphore("values_stored"))
    W = 16
    SB = SLOTS // 128

    def program(pool):
        flat = a["edge_values"].rearrange("(e o) -> e o", o=1)
        with pool.Fori(0, SB // W) as r:
            pool.drain()
            pool.tensor_copy(t["gidx"][:, :], t["t_idx"][:, bass.ds(r * W, W)])
            pool.drain()
            for k in range(W):
                pool.indirect_dma_start(t["gval"][:, k:k + 1], None, flat,
                                        bass.IndirectOffsetOnAxis(ap=t["gidx"][:, k:k + 1], axis=0)) \
                    .then_inc(got, 16)
            pool.drain()
            pool.tensor_copy(t["t_edge"][:, bass.ds(r * W, W)], t["gval"][:, :])
        pool.drain()
        pool.dma_start(scratch_v, t["t_edge"][:, :]).then_inc(stored, 16)
        pool.wait_ge(stored, 16)
    return program


TOK_EPS = 1e-5
GROUPS = B * N // CH
GPI = N // CH
NBLK = CH // BS
EXPERTS = 8


def turns(eng, body):
    for i in range(2):
        body(i, i)
    with eng.Fori(0, (GROUPS - 2) // 2) as r:
        for j in range(2):
            body(r * 2 + (2 + j), j)
    for i in range(GROUPS, GROUPS + 2):
        body(i, i % 2)


def live(g):
    return not isinstance(g, int) or 0 <= g < GROUPS


class TokenNorm:

    def __init__(self, nc, ctx, t, name):
        def sem(n):
            return ctx.enter_context(nc.semaphore(f"{name}_{n}"))

        def sb(n, shape):
            return ctx.enter_context(nc.sbuf_tensor(f"{name}_{n}", shape, F32))
        self.t = t
        self.mean_ready = sem("mean_ready")
        self.centered = sem("centered")
        self.squared = sem("squared")
        self.var_ready = sem("var_ready")
        self.log_done = sem("log_done")
        self.rstd = sem("rstd")
        self.normed = sem("normed")
        self.xc, self.xh = sb("xc", [128, 2, CH]), sb("xh", [128, 2, CH])
        self.sq, self.rs = sb("sq", [128, CH]), sb("rs", [128, CH])
        self.bank = t["M"][:, 0, :]

    def x(self, g):
        return self.t["x_all"][:, g * CH:(g + 1) * CH] if isinstance(g, int) else \
            self.t["x_all"][:, bass.ds(g * CH, CH)]

    def pe_mean(self, pe, g):
        pe.wait_ge(self.rstd, g)
        pe.matmul(self.bank, self.t["avg"][:, :], self.x(g), start=True, stop=True) \
          .then_inc(self.mean_ready, 1)

    def dve_center(self, dve, g, p):
        dve.wait_ge(self.mean_ready, g + 1)
        dve.tensor_tensor(self.xc[:, p, :], self.x(g), self.bank, ALU.subtract).then_inc(self.centered, 1)

    def act_square(self, act, g, p):
        act.wait_ge(self.centered, g + 1)
        act.wait_ge(self.var_ready, g)
        act.activation(self.sq[:, :], self.xc[:, p, :], ACT.Square).then_inc(self.squared, 1)

    def pe_var(self, pe, g):
        pe.wait_ge(self.squared, g + 1)
        pe.matmul(self.bank, self.t["avg"][:, :], self.sq[:, :], start=True, stop=True) \
          .then_inc(self.var_ready, 1)

    def act_rstd(self, act, g):
        act.wait_ge(self.var_ready, g + 1)
        act.wait_ge(self.normed, g)
        act.activation(self.rs[:, :], self.bank, ACT.Ln, bias=self.t["eps"][:, 0:1]).then_inc(self.log_done, 1)
        act.wait_ge(self.log_done, g + 1)
        act.activation(self.rs[:, :], self.rs[:, :], ACT.Exp, scale=-0.5).then_inc(self.rstd, 1)

    def dve_norm(self, dve, g, p):
        dve.wait_ge(self.rstd, g + 1)
        dve.tensor_tensor(self.xh[:, p, :], self.xc[:, p, :], self.rs[:, :], ALU.mult).then_inc(self.normed, 1)


def layer1_constants(nc, ctx, t, a, scratch_v, scratch_m):
    def sem(name):
        return ctx.enter_context(nc.semaphore(name))

    def sb(name, shape, dt=F32):
        return ctx.enter_context(nc.sbuf_tensor(name, shape, dt))
    loaded, made, own_sem = sem("l1_loaded"), sem("l1_made"), sem("l1_own")
    TT = N // 128
    w, m = sb("slot_w", [128, TT, BS]), sb("slot_m", [128, TT, BS])
    diag, tmp = sb("diag", [128, BS]), sb("slot_tmp", [128, TT, BS])
    gw = sb("gate_wb", [128, 3, HEADS])
    block = ctx.enter_context(nc.Block())

    @block.sync
    def _(sp):
        for dst, src in ((w, scratch_v), (m, scratch_m)):
            sp.dma_start(dst[:, :, :], src.rearrange("b (r k) -> (b r) k", k=BS)
                         .rearrange("(t q) k -> q t k", q=128)).then_inc(loaded, 16)
        row = lambda v, n: v.rearrange("(o n) -> o n", o=1).broadcast_to([128, n])
        col = lambda v: v.rearrange("(p o) -> p o", o=1)
        sp.dma_start(gw[:, 0, :], a["gate_w"].rearrange("h o -> (h o)").rearrange("(o n) -> o n", o=1).broadcast_to([128, HEADS])).then_inc(loaded, 16)
        sp.dma_start(gw[:, 1, :], row(a["gate_b"], HEADS)).then_inc(loaded, 16)
        sp.dma_start(t["w1"][:, :], a["qkv1_w"]).then_inc(loaded, 16)
        for k in range(2):
            sp.dma_start(t["b1"][:, k:k + 1], col(a["qkv1_b"][k * C:(k + 1) * C])).then_inc(loaded, 16)
        for h in range(HEADS):
            sp.dma_start(t["bv1"][h * BS:(h + 1) * BS, :],
                         a["qkv1_b"][2 * C + h * D:2 * C + (h + 1) * D].rearrange("(o n) -> o n", o=1)
                         .broadcast_to([BS, D])).then_inc(loaded, 16)
        sp.dma_start(t["pw1"][:, :], a["proj1_w"]).then_inc(loaded, 16)
        sp.dma_start(t["pb1"][:, 0:1], col(a["proj1_b"])).then_inc(loaded, 16)
        sp.dma_start(t["rw"][:, :], a["router_w"]).then_inc(loaded, 16)
        for k in range(QT):
            sp.dma_start(t["rb"][:, k, :], row(a["router_b"], EXPERTS)).then_inc(loaded, 16)
        sp.dma_start(t["ew"][:, :, :], a["expert_w"].rearrange("e d c -> d e c")).then_inc(loaded, 16)
        sp.dma_start(t["eb"][:, :], a["expert_b"]).then_inc(loaded, 16)
        sp.wait_ge(loaded, (4 + 1 + 2 + HEADS + 2 + 1 + QT + 2) * 16)

    @block.gpsimd
    def _(pool):
        pool.memset(diag[:, :], 0.0).then_inc(made, 1)
        pool.memset(t["avg"][:, :], 1.0 / C).then_inc(made, 1)
        pool.memset(t["eps"][:, :], TOK_EPS).then_inc(made, 1)
        pool.memset(t["kexp"][:, :, :, :, :], 0.0).then_inc(made, 1)
        pool.memset(t["vexp"][:, :, :, :], 0.0).then_inc(made, 1)
        pool.iota(t["iota8"][:, :], pattern=[[1, EXPERTS]], base=0, channel_multiplier=0,
                  allow_small_or_imprecise_dtypes=True).then_inc(made, 1)
        for q in range(128 // BS):
            pool.wait_ge(made, 6 + q)
            pool.affine_select(out=diag[:, :], in_=diag[:, :], compare_op=ALU.not_equal, fill=1.0,
                               base=-q * BS, pattern=[[-1, BS]], channel_multiplier=1).then_inc(made, 1)

    @block.vector
    def _(dve):
        own = Steps(dve, own_sem)
        dve.wait_ge(made, 6 + 128 // BS)
        dve.wait_ge(loaded, (4 + 1 + 2 + HEADS + 2 + 1 + QT + 2) * 16)
        d3 = diag[:, :].rearrange("p (o k) -> p o k", o=1).broadcast_to([128, TT, BS])
        own.inc(dve.tensor_tensor(w[:, :, :], w[:, :, :], m[:, :, :], ALU.mult))
        own.sync()
        own.inc(dve.tensor_scalar(tmp[:, :, :], w[:, :, :], -1.0, 1.0, ALU.mult, ALU.add))
        own.sync()
        own.inc(dve.tensor_tensor(tmp[:, :, :], tmp[:, :, :], d3, ALU.mult))
        own.inc(dve.tensor_tensor(m[:, :, :], m[:, :, :], d3, ALU.max))
        own.sync()
        own.inc(dve.tensor_tensor(w[:, :, :], w[:, :, :], tmp[:, :, :], ALU.add))
        own.sync()
        own.inc(dve.tensor_scalar(tmp[:, :, :], m[:, :, :], -1.0, 1e9, ALU.add, ALU.mult))
        own.inc(dve.tensor_tensor(gw[:, 2, :], gw[:, 0, :], gw[:, 1, :], ALU.add))
        own.sync()
        own.inc(dve.tensor_tensor(t["bias"][:, :, :], tmp[:, :, :], w[:, :, :], ALU.add))
        own.inc(dve.tensor_scalar(gw[:, 2, :], gw[:, 2, :], 1.0 / BS, None, ALU.mult))
        own.sync()
        for h in range(HEADS):
            own.inc(dve.tensor_scalar(t["gate"][:, :, h, :], m[:, :, :], gw[:, 1, h:h + 1],
                                      gw[:, 2, h:h + 1], ALU.mult, ALU.add))
        own.sync()
        for h in range(HEADS):
            own.inc(dve.scalar_tensor_tensor(t["gate"][:, :, h, :], w[:, :, :], gw[:, 0, h:h + 1],
                                             t["gate"][:, :, h, :], ALU.mult, ALU.add))


def block_attention(nc, ctx, t):
    def sem(name):
        return ctx.enter_context(nc.semaphore("a1_" + name))

    def sb(name, shape, dt=F32):
        return ctx.enter_context(nc.sbuf_tensor("a1_" + name, shape, dt))
    ln = TokenNorm(nc, ctx, t, "ln1")
    qk_ready, qk_taken = sem("qk_ready"), sem("qk_taken")
    v_ready, v_taken = sem("v_ready"), sem("v_taken")
    s_ready, s_taken = sem("s_ready"), sem("s_taken")
    shifted, exped, mixed = sem("shifted"), sem("exped"), sem("mixed")
    ct_ready, ct_taken = sem("ct_ready"), sem("ct_taken")
    av_ready, av_taken = sem("av_ready"), sem("av_taken")
    proj_ready, added, own_sem = sem("proj_ready"), sem("added"), sem("own")
    q_t = sb("q_t", [128, CH])
    sc = sb("sc", [128, QT, HEADS, BS])
    mix = sb("mix", [128, 2, QT, HEADS, BS])
    sm = sb("sm", [128, 6, QT * HEADS])
    ct, av = sb("ct", [128, CH]), sb("av", [128, CH])
    qb, kb = t["M"][:, 1, :], t["S"][:, 0, 0:CH]
    vb = t["S"][:, 0, CH:2 * CH]
    sbk, ctb, avb = t["S"][:, 1, CH:2 * CH], t["O"][:, 0, :], t["O"][:, 1, :]
    kexp, vexp, w1 = t["kexp"], t["vexp"], t["w1"]
    block = ctx.enter_context(nc.Block())

    @block.tensor
    def _(pe):
        def turn(i, p):
            g, f, e = i, i - 1, i - 2
            if live(g):
                ln.pe_mean(pe, g)
            if live(e):
                pe.wait_ge(mixed, e + 1)
                pe.wait_ge(ct_taken, e)
                for k in range(QT):
                    last = pe.matmul(ctb[:, k * 128:(k + 1) * 128],
                                     mix[:, p, k, :, :].rearrange("p h k -> p (h k)"), t["ident"][:, :],
                                     start=True, stop=True)
                last.then_inc(ct_ready, 1)
            if live(f):
                xh = ln.xh[:, 1 - p, :]
                pe.wait_ge(ln.normed, f + 1)
                pe.wait_ge(qk_taken, f * 2)
                pe.matmul(qb, w1[:, 0:C], xh, start=True, stop=True)
                pe.matmul(kb, w1[:, C:2 * C], xh, start=True, stop=True).then_inc(qk_ready, 1)
                pe.wait_ge(v_taken, f)
                for n in range(NBLK):
                    for h in range(HEADS):
                        last = pe.matmul(vb[h * BS:(h + 1) * BS, n * D:(n + 1) * D],
                                         xh[:, n * BS:(n + 1) * BS],
                                         w1[:, 2 * C + h * D:2 * C + (h + 1) * D], start=True, stop=True)
                last.then_inc(v_ready, 1)
            if live(g):
                ln.pe_var(pe, g)
            if live(e):
                pe.wait_ge(ct_taken, e + 1)
                pe.wait_ge(added, e)
                for n in range(NBLK):
                    last = pe.matmul(avb[:, n * BS:(n + 1) * BS], vexp[:, p, n, :],
                                     ct[:, n * BS:(n + 1) * BS], start=True, stop=True)
                last.then_inc(av_ready, 1)
            if live(f):
                pe.wait_ge(qk_taken, (f + 1) * 2)
                pe.wait_ge(s_taken, f)
                for n in range(NBLK):
                    r = n % 4 * BS
                    last = pe.matmul(sbk[r:r + BS, n // 4 * C:(n // 4 + 1) * C], q_t[:, n * BS:(n + 1) * BS],
                                     kexp[:, 1 - p, n, :, :].rearrange("p h k -> p (h k)"), start=True, stop=True)
                last.then_inc(s_ready, 1)
            if live(e):
                pe.wait_ge(av_taken, e + 1)
                pe.matmul(avb, t["pw1"][:, :], av[:, :], start=True, stop=True).then_inc(proj_ready, 1)
        turns(pe, turn)

    @block.vector
    def _(dve):
        OWN = 6
        own = Steps(dve, own_sem)

        def turn(i, p):
            g, f, e = i, i - 1, i - 2
            if live(g):
                ln.dve_center(dve, g, p)
            if live(f):
                if not isinstance(f, int) or f > 1:
                    dve.wait_ge(av_ready, f - 1)
                dve.wait_ge(v_ready, f + 1)
                for h in range(HEADS):
                    rows = slice(h * BS, (h + 1) * BS)
                    last = dve.tensor_tensor(vexp[rows, 1 - p, :, h * D:(h + 1) * D],
                                             vb.rearrange("p (n d) -> p n d", d=D)[rows, :, :],
                                             t["bv1"][rows, :].rearrange("p (o d) -> p o d", o=1)
                                             .broadcast_to([D, NBLK, D]), ALU.add)
                last.then_inc(v_taken, 1)
            if live(g):
                ln.dve_norm(dve, g, p)
            if live(f):
                own.at(f * OWN)
                grp = f % GPI * QT
                cols = slice(grp, grp + QT) if isinstance(f, int) else bass.ds(grp, QT)
                s4 = sbk.rearrange("p (t h k) -> p t h k", t=QT, h=HEADS)
                s3 = sbk.rearrange("p (t k) -> p t k", k=BS)
                c3 = sc[:, :, :, :].rearrange("p t h k -> p (t h) k")
                m3 = mix[:, 1 - p, :, :, :].rearrange("p t h k -> p (t h) k")

                def wide(n):
                    return sm[:, n, :].rearrange("p (t o) -> p t o", o=1).broadcast_to([128, QT * HEADS, BS])
                dve.wait_ge(s_ready, f + 1)
                dve.wait_ge(mixed, f)
                for k in range(QT):
                    one = slice(grp + k, grp + k + 1) if isinstance(f, int) else bass.ds(grp + k, 1)
                    last = dve.scalar_tensor_tensor(sc[:, k, :, :], s4[:, k, :, :], SCALE,
                                                    t["bias"][:, one, :].broadcast_to([128, HEADS, BS]),
                                                    ALU.mult, ALU.add)
                own.inc(last)
                dve.tensor_reduce(sm[:, 0, :], s3, AX.X, ALU.add).then_inc(s_taken, 1)
                dve.wait_ge(s_taken, f + 1)
                own.sync()
                own.inc(dve.tensor_scalar(sm[:, 0, :], sm[:, 0, :], SCALE / BS, 1.0, ALU.mult, ALU.add))
                own.inc(dve.tensor_reduce(sm[:, 1, :], c3, AX.X, ALU.max))
                own.sync()
                own.inc(dve.tensor_tensor(sm[:, 1, :], sm[:, 1, :], sm[:, 0, :], ALU.max))
                own.sync()
                own.inc(dve.tensor_tensor(c3, c3, wide(1), ALU.subtract))
                dve.tensor_tensor(sm[:, 2, :], sm[:, 0, :], sm[:, 1, :], ALU.subtract).then_inc(shifted, 1)
            if live(e):
                dve.wait_ge(proj_ready, e + 1)
                x = ln.x(e)
                dve.scalar_tensor_tensor(x, avb, t["pb1"][:, 0:1], x, ALU.add, ALU.add).then_inc(added, 1)
            if live(f):
                dve.wait_ge(exped, f * 2 + 2)
                if not isinstance(f, int) or f > 1:
                    dve.wait_ge(ct_ready, f - 1)
                own.inc(dve.tensor_reduce(sm[:, 3, :], c3, AX.X, ALU.add))
                own.sync()
                dve.tensor_tensor(sm[:, 3, :], sm[:, 3, :], sm[:, 2, :], ALU.add).then_inc(ln_own[0], 1)
                dve.wait_ge(ln_own[0], f * 4 + 1)
                dve.reciprocal(sm[:, 4, :], sm[:, 3, :]).then_inc(ln_own[0], 1)
                dve.wait_ge(ln_own[0], f * 4 + 2)
                dve.scalar_tensor_tensor(sm[:, 5, :], sm[:, 2, :], 1.0 / BS, sm[:, 4, :], ALU.mult, ALU.mult)
                dve.tensor_tensor(m3, c3, wide(4), ALU.mult).then_inc(ln_own[0], 1)
                dve.wait_ge(ln_own[0], f * 4 + 3)
                dve.tensor_tensor(mix[:, 1 - p, :, :, :], mix[:, 1 - p, :, :, :], t["gate"][:, cols, :, :],
                                  ALU.add).then_inc(ln_own[0], 1)
                dve.wait_ge(ln_own[0], f * 4 + 4)
                dve.tensor_tensor(m3, m3, wide(5), ALU.add).then_inc(mixed, 1)
        ln_own = [ctx.enter_context(nc.semaphore("a1_own2"))]
        turns(dve, turn)

    @block.scalar
    def _(act):
        def turn(i, p):
            g, f, e = i, i - 1, i - 2
            if live(g):
                ln.act_square(act, g, p)
            if live(e):
                act.wait_ge(ct_ready, e + 1)
                act.wait_ge(av_ready, e)
                act.activation(ct[:, :], ctb, ACT.Identity).then_inc(ct_taken, 1)
            if live(f):
                act.wait_ge(qk_ready, f + 1)
                act.wait_ge(s_ready, f)
                act.activation(q_t[:, :], qb, ACT.Identity, bias=t["b1"][:, 0:1]).then_inc(qk_taken, 1)
                for h in range(HEADS):
                    rows = slice(h * D, (h + 1) * D)
                    last = act.activation(kexp[rows, 1 - p, :, h, :],
                                          kb.rearrange("p (n k) -> p n k", k=BS)[rows, :, :],
                                          ACT.Identity, bias=t["b1"][rows, 1:2])
                last.then_inc(qk_taken, 1)
            if live(g):
                ln.act_rstd(act, g)
            if live(e):
                act.wait_ge(av_ready, e + 1)
                act.wait_ge(proj_ready, e)
                act.activation(av[:, :], avb, ACT.Identity).then_inc(av_taken, 1)
            if live(f):
                act.wait_ge(shifted, f + 1)
                act.activation(sc[:, :, :, :], sc[:, :, :, :], ACT.Exp).then_inc(exped, 1)
                act.activation(sm[:, 2, :], sm[:, 2, :], ACT.Exp).then_inc(exped, 1)
        turns(act, turn)


def experts(nc, ctx, t, out):
    def sem(name):
        return ctx.enter_context(nc.semaphore("moe_" + name))

    def sb(name, shape, dt=F32):
        return ctx.enter_context(nc.sbuf_tensor("moe_" + name, shape, dt))
    ln = TokenNorm(nc, ctx, t, "ln2")
    r_ready, r_taken, exped = sem("r_ready"), sem("r_taken"), sem("exped")
    gated, e_ready, e_taken = sem("gated"), sem("e_ready"), sem("e_taken")
    gt_ready, gt_taken, f_ready, summed = sem("gt_ready"), sem("gt_taken"), sem("f_ready"), sem("summed")
    stored = [sem(f"stored_{j}") for j in range(2)]
    own_sem = sem("own")
    lg = sb("lg", [128, QT, EXPERTS])
    mx, den = sb("mx", [128, QT]), sb("den", [128, QT])
    best = sb("best", [128, QT, 8])
    bidx, bidxf = sb("bidx", [128, QT, 8], U32), sb("bidxf", [128, QT, 8])
    gates = sb("gates", [128, 2, QT, EXPERTS])
    g2 = sb("g2", [128, QT, EXPERTS])
    acc = sb("acc", [128, 2, QT, C])
    gt = sb("gt", [EXPERTS, CH])
    y = sb("y", [128, 2, CH])
    gate_scratch = sb("gate", [128, 1])
    rbk, gtb, fbk = t["M"][:, 1, :], t["O"][:, 0, :], t["O"][:, 1, :]
    ebk = t["S"]
    img = out.rearrange("b c n -> c b n")
    block = ctx.enter_context(nc.Block())

    @block.tensor
    def _(pe):
        def turn(i, p):
            g, f, e = i, i - 1, i - 2
            xh = ln.xh[:, 1 - p, :]
            if live(g):
                ln.pe_mean(pe, g)
            if live(f):
                pe.wait_ge(ln.normed, f + 1)
                pe.wait_ge(r_taken, f)
                for k in range(QT):
                    last = pe.matmul(rbk[:, k * EXPERTS:(k + 1) * EXPERTS], xh[:, k * 128:(k + 1) * 128],
                                     t["rw"][:, :], start=True, stop=True)
                last.then_inc(r_ready, 1)
            if live(g):
                ln.pe_var(pe, g)
            if live(e):
                pe.wait_ge(e_taken, (e + 1) * QT)
                pe.wait_ge(gt_taken, e)
                for k in range(QT):
                    last = pe.matmul(gtb[0:EXPERTS, k * 128:(k + 1) * 128], gates[:, p, k, :],
                                     t["ident"][:, :], start=True, stop=True)
                last.then_inc(gt_ready, 1)
            def expert_products(k):
                if not isinstance(f, int) or f > 0 or k >= 2:
                    pe.wait_ge(e_taken, f * QT + (k - 1))
                for m in range(2):
                    last = pe.matmul(ebk[:, k % 2, m * CH:(m + 1) * CH], xh[:, k * 128:(k + 1) * 128],
                                     t["ew"][:, 4 * m:4 * m + 4, :].rearrange("p e c -> p (e c)"),
                                     start=True, stop=True)
                last.then_inc(e_ready, 1)
            if live(f):
                expert_products(0)
                expert_products(1)
            if live(e):
                pe.wait_ge(gt_taken, e + 1)
                pe.wait_ge(summed, e)
                pe.matmul(fbk, t["eb"][:, :], gt[:, :], start=True, stop=False, skip_group_check=True)
                for k in range(QT):
                    last = pe.matmul(fbk[:, k * 128:(k + 1) * 128], acc[:, p, k, :], t["ident"][:, :],
                                     start=False, stop=(k == QT - 1), skip_group_check=True)
                last.then_inc(f_ready, 1)
            if live(f):
                expert_products(2)
                expert_products(3)
        turns(pe, turn)

    @block.scalar
    def _(act):
        def turn(i, p):
            g, f, e = i, i - 1, i - 2
            if live(g):
                ln.act_square(act, g, p)
            if live(f):
                act.wait_ge(gated, f * 2 + 1)
                act.activation(lg[:, :, :], lg[:, :, :], ACT.Exp).then_inc(exped, 1)
            if live(g):
                ln.act_rstd(act, g)
            if live(e):
                act.wait_ge(gt_ready, e + 1)
                act.wait_ge(f_ready, e)
                act.activation(gt[:, :], gtb[0:EXPERTS, :], ACT.Identity).then_inc(gt_taken, 1)
        turns(act, turn)

    @block.vector
    def _(dve):
        own = Steps(dve, own_sem)
        OWN = 2 + 8

        def wide(v):
            return v.rearrange("p (t o) -> p t o", o=1).broadcast_to([128, QT, EXPERTS])

        def turn(i, p):
            g, f, e = i, i - 1, i - 2
            if live(g):
                ln.dve_center(dve, g, p)
            if live(f):
                own.at(f * OWN)
                dve.wait_ge(r_ready, f + 1)
                dve.tensor_tensor(lg[:, :, :], rbk[:, 0:QT * EXPERTS].rearrange("p (t e) -> p t e", t=QT),
                                  t["rb"][:, :, :], ALU.add).then_inc(r_taken, 1)
                dve.wait_ge(r_taken, f + 1)
                own.inc(dve.tensor_reduce(mx[:, :], lg[:, :, :], AX.X, ALU.max))
                own.sync()
                dve.tensor_tensor(lg[:, :, :], lg[:, :, :], wide(mx[:, :]), ALU.subtract).then_inc(gated, 1)
            if live(e):
                dve.wait_ge(f_ready, e + 1)
                if not isinstance(e, int) or e > 1:
                    dve.wait_ge(stored[p], (e - p) * 8)
                dve.tensor_tensor(y[:, p, :], fbk, ln.x(e), ALU.add).then_inc(summed, 1)
            if live(f):
                dve.wait_ge(exped, f + 1)
                own.inc(dve.tensor_reduce(den[:, :], lg[:, :, :], AX.X, ALU.add))
                own.sync()
                own.inc(dve.reciprocal(den[:, :], den[:, :]))
                own.sync()
                own.inc(dve.tensor_tensor(lg[:, :, :], lg[:, :, :], wide(den[:, :]), ALU.mult))
                own.sync_apart(gate_scratch[:, 0:1])
                for k in range(QT):
                    last = dve.max(best[:, k, :], lg[:, k, :])
                own.inc(last)
                own.sync_apart(gate_scratch[:, 0:1])
                for k in range(QT):
                    dve.max_index(bidx[:, k, :], best[:, k, :], lg[:, k, :])
                own.inc(dve.tensor_tensor(den[:, :], best[:, :, 0], best[:, :, 1], ALU.add))
                own.sync()
                own.inc(dve.reciprocal(den[:, :], den[:, :]))
                own.inc(dve.tensor_copy(bidxf[:, :, :], bidx[:, :, :]))
                own.sync()
                own.inc(dve.tensor_tensor(best[:, :, :], best[:, :, :], wide(den[:, :]), ALU.mult))
                own.sync()
                for k in range(QT):
                    dve.tensor_scalar(gates[:, 1 - p, k, :], t["iota8"][:, :], bidxf[:, k, 0:1], best[:, k, 0:1],
                                      ALU.is_equal, ALU.mult)
                    last = dve.tensor_scalar(g2[:, k, :], t["iota8"][:, :], bidxf[:, k, 1:2], best[:, k, 1:2],
                                             ALU.is_equal, ALU.mult)
                own.inc(last)
                own.sync()
                dve.tensor_tensor(gates[:, 1 - p, :, :], gates[:, 1 - p, :, :], g2[:, :, :], ALU.add) \
                   .then_inc(gated, 1)
            if live(g):
                ln.dve_norm(dve, g, p)
            if live(f):
                dve.wait_ge(gated, f * 2 + 2)
                if not isinstance(f, int) or f > 1:
                    dve.wait_ge(f_ready, f - 1)
                for k in range(QT):
                    dve.wait_ge(e_ready, f * QT + (k + 1))
                    for x in range(EXPERTS):
                        src = ebk[:, k % 2, x * C:(x + 1) * C]
                        gx = gates[:, 1 - p, k, x:x + 1]
                        if x == 0:
                            last = dve.tensor_scalar(acc[:, 1 - p, k, :], src, gx, None, ALU.mult)
                        else:
                            last = dve.scalar_tensor_tensor(acc[:, 1 - p, k, :], src, gx,
                                                            acc[:, 1 - p, k, :], ALU.mult, ALU.add)
                        if x < EXPERTS - 1:
                            last.then_inc(acc_own, 1)
                            dve.wait_ge(acc_own, f * (QT * (EXPERTS - 1)) + (k * (EXPERTS - 1) + x + 1))
                    last.then_inc(e_taken, 1)
        acc_own = ctx.enter_context(nc.semaphore("moe_acc_own"))
        turns(dve, turn)

    @block.sync
    def _(sp):
        with sp.Fori(0, B) as b:
            with sp.Fori(0, GPI // 2) as r:
                for j in range(2):
                    sp.wait_ge(summed, b * GPI + r * 2 + (j + 1))
                    sp.dma_start(img[:, bass.ds(b, 1), bass.ds(r * (2 * CH) + j * CH, CH)],
                                 y[:, j, :].rearrange("p (o n) -> p o n", o=1)).then_inc(stored[j], 16)
        for j in range(2):
            sp.wait_ge(stored[j], GROUPS // 2 * 16)


def build(nc, a, out, dbg=None):
    with ExitStack() as whole:
        def sb(name, shape, dt=F32, ctx=whole):
            return ctx.enter_context(nc.sbuf_tensor(name, shape, dt))

        t = {
            "x_all": sb("x_all", [128, B * N]),
            "ident": sb("ident", [128, 128]),
            "gn_a": sb("gn_a", [128, B]), "gn_b": sb("gn_b", [128, B]),
        }
        for name, shape in (("S", [128, 2, 2 * CH]), ("O", [128, 2, CH]), ("M", [128, 2, CH])):
            t[name] = whole.enter_context(nc.psum_tensor(name, shape, F32))
        for name, shape, dt in (
                ("pcol", [128, 1], I32), ("ovf", [128, 1], F32), ("ovf_all", [128, 1], F32),
                ("idx8", [128, BATCH], U32), ("ev8", [128, BATCH], F32),
                ("list", [128, 2 * LIST], F32)):
            t[name] = sb(name, shape, dt)
        SB = SLOTS // 128
        t["list_e"], t["list_idx"] = t["list"][:, 0:LIST], t["list"][:, LIST:2 * LIST].bitcast(U32)
        t["t_idx"] = t["list"][:, 0:SB].bitcast(U32)
        table = nc.dram_tensor("slot_table", (SLOTS, 128), F32).ap()
        scratch_v = nc.dram_tensor("slot_values", (128, SB), F32).ap()
        scratch_m = nc.dram_tensor("slot_masks", (128, SB), F32).ap()
        with ExitStack() as c:
            edge_lists(nc, c, t, a, table)
        with ExitStack() as l0:
            t.update({
                "qs": sb("q_stack", [128, NCH * HEADS * CH], F16, l0),
                "ks": sb("k_stack", [128, HEADS, N], F16, l0),
                "vones": sb("v_ones", [128, KT, HEADS, 2 * D], F32, l0),
                "probs": sb("probs", [128, 3, 2 * CH], F32, l0),
                "xn": sb("x_norm", [128, 2, CH], F32, l0),
                "part": sb("qk_halves", [128, 2, 4, CH], F16, l0),
                "o_t": sb("o_t", [128, CH], F32, l0),
                "rden": sb("rden", [128, 2, CH], F32, l0),
                "mx8": sb("mx8", [128, HEADS * QT, NCH], F32, l0),
                "mx": sb("mx", [128, HEADS * QT], F32, l0),
                "mrow": sb("mrow", [HEADS * QT, 128], F16, l0),
                "wqkv": sb("wqkv", [128, 3 * C], F32, l0),
                "qkv_b": sb("qkv_bias", [128, 2], F32, l0),
                "vbias": sb("vbias", [128, QT, HEADS, D], F32, l0),
                "proj_w": sb("proj_w", [128, C], F32, l0),
                "proj_b": sb("proj_bias", [128, 1], F32, l0),
                "t_edge": sb("t_edge", [128, SB], F32, l0),
                "gidx": sb("gidx", [128, 16], U32, l0),
                "gval": sb("gval", [128, 16], F32, l0),
            })
            with ExitStack() as c:
                constants_and_norm(nc, c, t, a)
            with ExitStack() as c:
                attention_half(nc, c, t, 0, scatter_lists(nc, c, t, table))
            with ExitStack() as c:
                last_edges(nc, c, t, a, table, scratch_m)
            with ExitStack() as c:
                attention_half(nc, c, t, 1, gather_values(nc, c, t, a, scratch_v))
        with ExitStack() as l1:
            TT = N // 128
            t.update({
                "w1": sb("l1_qkv_w", [128, 3 * C], F32, l1), "b1": sb("l1_qk_b", [128, 2], F32, l1),
                "bv1": sb("l1_v_b", [128, D], F32, l1),
                "pw1": sb("l1_proj_w", [128, C], F32, l1), "pb1": sb("l1_proj_b", [128, 1], F32, l1),
                "rw": sb("router_w", [128, EXPERTS], F32, l1), "rb": sb("router_b", [128, QT, EXPERTS], F32, l1),
                "ew": sb("expert_w", [128, EXPERTS, C], F32, l1), "eb": sb("expert_b", [EXPERTS, C], F32, l1),
                "avg": sb("avg", [128, C], F32, l1), "eps": sb("token_eps", [128, 1], F32, l1),
                "iota8": sb("iota8", [128, EXPERTS], F32, l1),
                "kexp": sb("k_diag", [128, 2, NBLK, HEADS, BS], F32, l1),
                "vexp": sb("v_diag", [128, 2, NBLK, C], F32, l1),
                "bias": sb("slot_bias", [128, TT, BS], F32, l1),
                "gate": sb("slot_gate", [128, TT, HEADS, BS], F32, l1),
            })
            with ExitStack() as c:
                layer1_constants(nc, c, t, a, scratch_v, scratch_m)
            with ExitStack() as c:
                block_attention(nc, c, t)
            if dbg is None:
                with ExitStack() as c:
                    experts(nc, c, t, out)
        if dbg is not None:
            with ExitStack() as c:
                done = c.enter_context(nc.semaphore("dbg"))
                blk = c.enter_context(nc.Block())

                @blk.sync
                def _(sp):
                    for b in range(B):
                        sp.dma_start(dbg[b], t["x_all"][:, b * N:(b + 1) * N]).then_inc(done, 16)
                    sp.wait_ge(done, B * 16)


_INPUTS = {
    "x": ("x", lambda v: v.reshape(B, C, N)),
    "norm_w": ("L0_conv_norm_w", None), "norm_b": ("L0_conv_norm_b", None),
    "qkv_wT": ("L0_conv_qkv_w", lambda v: v.T), "qkv_b": ("L0_conv_qkv_b", None),
    "proj_wT": ("L0_conv_proj_w", lambda v: v.T), "proj_b": ("L0_conv_proj_b", None),
    "edges": ("L1_attn_edge_index", None), "edge_values": ("L1_attn_edge_values", None),
    "qkv1_w": ("L1_attn_qkv_w", None), "qkv1_b": ("L1_attn_qkv_b", None),
    "proj1_w": ("L1_attn_proj_w", None), "proj1_b": ("L1_attn_proj_b", None),
    "gate_w": ("L1_attn_gate_w", None), "gate_b": ("L1_attn_gate_b", None),
    "router_w": ("L1_ffn_router_w", None), "router_b": ("L1_ffn_router_b", None),
    "expert_w": ("L1_ffn_expert_w", None), "expert_b": ("L1_ffn_expert_b", None),
}


def kernel(**inputs):
    import numpy as np
    import concourse.bacc as bacc
    from concourse.bass_utils import run_bass_kernel_spmd

    nc = bacc.Bacc("TRN2", target_bir_lowering=False, num_devices=1)
    arrays, a = {}, {}
    for name, (source, lay) in _INPUTS.items():
        v = np.asarray(inputs[source])
        v = np.ascontiguousarray(lay(v) if lay else v)
        arrays[f"in_{name}"] = v
        a[name] = nc.dram_tensor(f"in_{name}", v.shape, mybir.dt.from_np(v.dtype), kind="ExternalInput").ap()
    out = nc.dram_tensor("out_0", (B, C, N), F32, kind="ExternalOutput").ap()
    build(nc, a, out)
    r = run_bass_kernel_spmd(nc, [arrays], core_ids=[0])
    return r.results[0]["out_0"].reshape(B, C, 64, 64)
```

```python
from contextlib import ExitStack

import concourse.bass as bass
from concourse import mybir

F32 = mybir.dt.float32
F16 = mybir.dt.float16
I32 = mybir.dt.int32
U32 = mybir.dt.uint32
ALU = mybir.AluOpType
ACT = mybir.ActivationFunctionType
AX = mybir.AxisListType

C = 128
B = 4
N = 4096
HEADS = 4
D = C // HEADS
SCALE = float(D) ** -0.5
CH = 512
NCH = N // CH
KT = N // 128
QT = CH // 128
GN_EPS = 1e-5
GROUP = C // 8
MROW = 16.0

BS = 32
E = 4194304
EP = E // 128
SLOTS = N * BS
PIECE = 2048
RUN = 64
RUNS = EP // RUN
GRP = 512
KEEP = 80
GRPS = RUNS * 8 // GRP
LIST = GRPS * KEEP
SLOT_BITS = 17
BATCH = 8
NOWHERE = 1 << 24


class Steps:

    def __init__(self, eng, sem):
        self.eng, self.sem, self.base, self.n = eng, sem, 0, 0

    def inc(self, ins):
        self.n += 1
        return ins.then_inc(self.sem, 1)

    def sync(self):
        self.eng.wait_ge(self.sem, self.base + self.n)

    def sync_apart(self, scratch):
        self.eng.wait_ge(self.sem, self.base + self.n)
        self.eng.memset(scratch, 0.0)

    def at(self, base):
        self.base, self.n = base, 0


def attention_half(nc, ctx, t, half, pool_program):
    x_all, qs, ks, vones, ident = t["x_all"], t["qs"], t["ks"], t["vones"], t["ident"]
    probs, o_t, mx8, mx, mrow = t["probs"], t["o_t"], t["mx8"], t["mx"], t["mrow"]
    os, dn = t["os"], t["dn"]
    xn, wqk, wv, qk_b, vbias = t["xn"], t["wqk"], t["wv"], t["qk_b"], t["vbias"]
    S, O, M = t["S"], t["O"], t["M"]
    IMGS = 2

    def sem(name):
        return ctx.enter_context(nc.semaphore(f"{name}_{half}"))

    xn_ready = sem("xn_ready")
    qk_ready = sem("qk_ready")
    high_out = sem("high_out")
    qk_taken = sem("qk_taken")
    v_ready = sem("v_ready")
    v_taken = sem("v_taken")
    s_ready = sem("s_ready")
    p_ready = sem("p_ready")
    o_added = sem("o_added")
    m_ready = sem("m_ready")
    m_taken = sem("m_taken")
    mx_final = sem("mx_final")
    mt_ready = sem("mt_ready")
    mrow_out = sem("mrow_out")
    mrow_in = sem("mrow_in")
    o_out = sem("o_out")
    dens_out = sem("dens_out")
    recip_own = sem("recip_own")
    o_taken = sem("o_taken")
    y_ready = sem("y_ready")
    y_taken = sem("y_taken")

    STEPS = KT * 2
    TILES = HEADS * QT * NCH
    QK = 2 * HEADS
    KTILES = HEADS * QT

    def tile_of(n):
        return n // (QT * NCH), (n // NCH) % QT, n % NCH

    def tiles_of_step(s):
        return range(min(TILES, s * 9 // 4), min(TILES, (s + 1) * 9 // 4))

    R0, RN = 8, 16
    T0, TN = R0 + RN, 8
    PROJ = 100
    TRANSPOSE = 60
    PW = 2 * CH // RN

    block = ctx.enter_context(nc.Block())

    LEAD = 1

    def head_turns(eng, turn, last_turn):
        turn(0, 0)
        turn(1, 1)
        with eng.Fori(1, NCH // 2) as c2:
            for j in range(2):
                turn(c2 * 2 + j, j)
        last_turn()

    @block.scalar
    def _(act):
        for x in (xn_ready, high_out, p_ready, o_out, dens_out):
            act.sem_inc(x, LEAD)

        def den(h, chunk):
            r = 64 * (h % 2)
            if h == 0:
                act.wait_ge(o_out, chunk + LEAD)
                act.wait_ge(o_taken, chunk - 1 + LEAD)
            last = act.activation(dn[r:r + D, h // 2, :], os[r + D:r + 2 * D, h // 2, :], ACT.Identity)
            if h == HEADS - 1:
                last.then_inc(dens_out, 1)

        with act.Fori(0, IMGS) as img:
            b = img + half * IMGS

            def turn(c, j):
                act.wait_ge(v_ready, img * NCH + (c - 1 + LEAD) if not isinstance(c, int) or c > 0
                            else img * NCH + LEAD)
                act.activation(xn[:, j, :], x_all[:, bass.ds(b * N + c * CH, CH)], ACT.Identity,
                               scale=t["gn_a"][:, bass.ds(b, 1)], bias=t["gn_b"][:, bass.ds(b, 1)]) \
                   .then_inc(xn_ready, 1)
                for i in range(QK):
                    h, m = i // 2, i % 2
                    act.wait_ge(qk_ready, (img * NCH + c) * QK + (i + 1 + LEAD))
                    dst = (qs[0:96, bass.ds(c * (HEADS * CH) + h * CH, CH)], ks[0:96, h, bass.ds(c * CH, CH)])[m]
                    act.activation(dst, S[0:96, i % 4 // 2, (i % 2) * CH:(i % 2 + 1) * CH], ACT.Identity,
                                   bias=qk_b[:, m * HEADS + h:m * HEADS + h + 1]).then_inc(high_out, 1)
            head_turns(act, turn, lambda: None)

            def chunk_turn(c, first):
                chunk = img * NCH + c
                turn = chunk * STEPS
                for s in range(STEPS):
                    act.wait_ge(s_ready, turn + (s + 1 + LEAD))
                    if s >= 3:
                        act.wait_ge(o_added, turn + (s - 2 + LEAD))
                    act.activation(probs[:, s % 3, :], S[:, s % 2, :], ACT.Exp, scale=SCALE) \
                       .then_inc(p_ready, 1)
                    if not first and 1 <= s < 1 + HEADS:
                        den(s - 1, chunk)
                act.wait_ge(o_added, turn + (STEPS + LEAD))
                act.wait_ge(o_taken, chunk + LEAD)
                act.activation(os[:, :, :], O[:, :, :], ACT.Identity).then_inc(o_out, 1)
            chunk_turn(0, True)
            with act.Fori(1, NCH) as c:
                chunk_turn(c, False)
            for h in range(HEADS):
                den(h, (img + 1) * NCH)

    @block.tensor
    def _(pe):
        for x in (qk_ready, v_ready, s_ready, o_added, m_ready, mt_ready, y_ready):
            pe.sem_inc(x, LEAD)

        def max_tile(n, h, qt, q_at, keys):
            pe.matmul(M[:, n % 2, :], qs[0:96, bass.ds(q_at + (h * CH + qt * 128), 128)],
                      ks[0:96, h, keys], start=True, stop=True).then_inc(m_ready, 1)

        def transpose_maxima(count):
            pe.wait_ge(mx_final, count + LEAD)
            pe.matmul(M[0:HEADS * QT, 0, 0:128], mx[:, :], ident[:, :], start=True, stop=True) \
              .then_inc(mt_ready, 1)

        def project(chunks):
            pe.wait_ge(o_taken, chunks + LEAD)
            pe.matmul(M[:, 0, :], t["proj_w"][:, :], o_t[:, :], start=True, stop=True).then_inc(y_ready, 1)

        with pe.Fori(0, IMGS) as img:
            mturn = img * (NCH * TILES)

            def key_tiles(kc, i):
                for n in (2 * i, 2 * i + 1):
                    if not (isinstance(kc, int) and kc == 0 and n < 2):
                        pe.wait_ge(m_taken, mturn + kc * KTILES + (n - 1 + LEAD))
                    max_tile(n, n // QT, n % QT, 0, bass.ds(kc * CH, CH))

            def turn(c, j):
                first = isinstance(c, int) and c == 0
                pe.wait_ge(xn_ready, img * NCH + c + (1 + LEAD))
                for i in range(QK):
                    h, m = i // 2, i % 2
                    if not first or i >= 4:
                        pe.wait_ge(qk_taken, (img * NCH + c) * QK + (i - 3 + LEAD))
                    elif i == 0:
                        pe.wait_ge(p_ready, img * (NCH * STEPS) + LEAD)
                    pe.matmul(S[0:96, i % 4 // 2, (i % 2) * CH:(i % 2 + 1) * CH], wqk[:, m * HEADS + h, :],
                              xn[:, j, :], start=True, stop=True).then_inc(qk_ready, 1)
                    if not first:
                        if i == 0:
                            pe.wait_ge(qk_taken, (img * NCH + c) * QK + LEAD)
                        key_tiles(c - 1, i)
                if first:
                    pe.wait_ge(o_out, img * NCH + LEAD)
                pe.wait_ge(v_taken, img * NCH + c + LEAD)
                for k in range(QT):
                    last = pe.matmul(O[:, 0, k * C:(k + 1) * C], xn[:, j, k * 128:(k + 1) * 128],
                                     wv[:, :], start=True, stop=True)
                last.then_inc(v_ready, 1)
                if first:
                    pe.wait_ge(y_taken, img * NCH + LEAD)

            def last_turn():
                pe.wait_ge(qk_taken, (img + 1) * (NCH * QK) + LEAD)
                for i in range(QK):
                    key_tiles(NCH - 1, i)
                transpose_maxima(img * NCH + 1)
            head_turns(pe, turn, last_turn)

            def chunk_turn(c, first, last_chunk):
                chunk = img * NCH + c
                turn = chunk * STEPS
                mturn = (chunk + 1) * TILES
                q_at = c * (HEADS * CH)
                pe.wait_ge(mrow_in, (chunk + 1) * 16 + LEAD)
                for s in range(STEPS + 1):
                    kt, hp = s // 2, s % 2
                    if s < STEPS:
                        pe.wait_ge(p_ready, turn + (max(s - 1, 0) + LEAD))
                        for h in (2 * hp, 2 * hp + 1):
                            last = pe.matmul(S[:, s % 2, (h % 2) * CH:(h % 2 + 1) * CH],
                                             ks[0:97, h, kt * 128:(kt + 1) * 128],
                                             qs[0:97, bass.ds(q_at + h * CH, CH)], start=True, stop=True)
                        last.then_inc(s_ready, 1)
                        for n in tiles_of_step(s):
                            if n == 0 and not last_chunk:
                                pe.wait_ge(mrow_out, chunk + (1 + LEAD))
                            if n >= 2 and not last_chunk:
                                pe.wait_ge(m_taken, mturn + (n - 1 + LEAD))
                            if n == PROJ and not first:
                                project(chunk)
                                if not last_chunk:
                                    pe.wait_ge(y_taken, chunk + LEAD)
                            if not last_chunk:
                                h, qt, kc = tile_of(n)
                                max_tile(n, h, qt, (c + 1) * (HEADS * CH), slice(kc * CH, (kc + 1) * CH))
                        if s == TRANSPOSE and not last_chunk:
                            transpose_maxima(chunk + 2)
                    if s >= 1:
                        pt, ph = (s - 1) // 2, (s - 1) % 2
                        if s == 1:
                            pe.wait_ge(o_out, chunk + LEAD)
                        pe.wait_ge(p_ready, turn + (s + LEAD))
                        for j in range(2):
                            last = pe.matmul(O[64 * j:64 * j + 64, ph, :], vones[:, pt, 2 * ph + j, :],
                                             probs[:, (s - 1) % 3, j * CH:(j + 1) * CH],
                                             start=(pt == 0), stop=(pt == KT - 1))
                        last.then_inc(o_added, 1)
            chunk_turn(0, True, False)
            with pe.Fori(1, NCH - 1) as c:
                chunk_turn(c, False, False)
            chunk_turn(NCH - 1, False, True)
            pe.wait_ge(y_taken, (img + 1) * NCH - 1 + LEAD)
            project((img + 1) * NCH)

    @block.vector
    def _(dve):
        for x in (qk_taken, v_taken, m_taken, mx_final, mrow_out, o_taken, y_taken, recip_own):
            dve.sem_inc(x, LEAD)

        def maxima(mturn, n, row, kc):
            dve.wait_ge(m_ready, mturn + (n + 1 + LEAD))
            dve.reduce_max(mx8[:, row, bass.ds(kc, 1)], M[:, n % 2, :], AX.X).then_inc(m_taken, 1)

        def finish_maxima(count):
            dve.wait_ge(m_taken, count * TILES + LEAD)
            dve.reduce_max(mx[:, :], mx8[:, :, :], AX.X).then_inc(mx_final, 1)
            dve.wait_ge(mt_ready, count + LEAD)
            dve.wait_ge(mrow_in, (count - 1) * 16 + LEAD)
            dve.tensor_scalar(mrow[:, :], M[0:HEADS * QT, 0, 0:128], -1.0 / MROW, None, ALU.mult) \
               .then_inc(mrow_out, 1)

        def reciprocals(n, chunks):
            if n == 0:
                dve.wait_ge(dens_out, chunks + LEAD)
            hp, at = n * PW // CH, n * PW % CH
            last = dve.reciprocal(dn[0:64 + D, hp, at:at + PW], dn[0:64 + D, hp, at:at + PW])
            if n == RN - 1:
                last.then_inc(recip_own, 1)

        def normalise(n, chunks):
            if n == 0:
                dve.wait_ge(recip_own, chunks + LEAD)
                dve.wait_ge(y_ready, chunks - 1 + LEAD)
            h, at = n // 2, n % 2 * (CH // 2)
            r = 64 * (h % 2)
            last = dve.tensor_tensor(o_t[h * D:(h + 1) * D, at:at + CH // 2],
                                     os[r:r + D, h // 2, at:at + CH // 2],
                                     dn[r:r + D, h // 2, at:at + CH // 2], ALU.mult)
            if n == TN - 1:
                last.then_inc(o_taken, 1)

        def residual(chunks, col):
            dve.wait_ge(y_ready, chunks + LEAD)
            x_now = x_all[:, bass.ds(col, CH)]
            dve.scalar_tensor_tensor(x_now, M[:, 0, :], t["proj_b"][:, 0:1], x_now,
                                     ALU.add, ALU.add).then_inc(y_taken, 1)

        dve.memset(dn[:, :, :], 1.0)
        with dve.Fori(0, IMGS) as img:
            mturn = img * (NCH * TILES)

            def key_maxima(kc, i):
                for n in (2 * i, 2 * i + 1):
                    maxima(mturn + kc * KTILES, n, n, kc)

            def turn(c, j):
                first = isinstance(c, int) and c == 0
                for i in range(QK):
                    h, m = i // 2, i % 2
                    dve.wait_ge(high_out, (img * NCH + c) * QK + (i + 1 + LEAD))
                    r = slice(2 * D, 3 * D) if m == 0 else slice(D, 2 * D)
                    low = (qs[r, bass.ds(c * (HEADS * CH) + h * CH, CH)], ks[r, h, bass.ds(c * CH, CH)])[m]
                    dve.scalar_tensor_tensor(low, S[r, i % 4 // 2, (i % 2) * CH:(i % 2 + 1) * CH],
                                             qk_b[r, m * HEADS + h:m * HEADS + h + 1], low,
                                             ALU.add, ALU.subtract).then_inc(qk_taken, 1)
                    if not first:
                        key_maxima(c - 1, i)
                dve.wait_ge(v_ready, img * NCH + c + (1 + LEAD))
                dve.tensor_tensor(vones[:, bass.ds(c * QT, QT), :, 0:D],
                                  O[:, 0, :].rearrange("p (k h d) -> p k h d", k=QT, h=HEADS),
                                  vbias[:, :, :, :], ALU.add).then_inc(v_taken, 1)

            def last_turn():
                for i in range(QK):
                    key_maxima(NCH - 1, i)
                finish_maxima(img * NCH + 1)
            head_turns(dve, turn, last_turn)
            col = (img + half * IMGS) * N

            def chunk_turn(c, first, last_chunk):
                chunk = img * NCH + c
                mturn = (chunk + 1) * TILES
                for s in range(STEPS):
                    if not first:
                        if R0 <= s < R0 + RN:
                            reciprocals(s - R0, chunk)
                        if T0 <= s < T0 + TN:
                            normalise(s - T0, chunk)
                    for n in tiles_of_step(s):
                        if n == PROJ and not first:
                            residual(chunk, col + (c - 1) * CH)
                        if not last_chunk:
                            h, qt, kc = tile_of(n)
                            maxima(mturn, n, h * QT + qt, kc)
                if not last_chunk:
                    finish_maxima(chunk + 2)
            chunk_turn(0, True, False)
            with dve.Fori(1, NCH - 1) as c:
                chunk_turn(c, False, False)
            chunk_turn(NCH - 1, False, True)
            last_chunk = (img + 1) * NCH
            for n in range(RN):
                reciprocals(n, last_chunk)
            for n in range(TN):
                normalise(n, last_chunk)
            residual(last_chunk, col + (NCH - 1) * CH)

    @block.sync
    def _(sp):
        sp.sem_inc(mrow_in, LEAD)
        with sp.Fori(0, IMGS) as img:
            with sp.Fori(0, NCH) as c:
                sp.wait_ge(mrow_out, img * NCH + c + (1 + LEAD))
                sp.dma_start(qs[96:97, bass.ds(c * (HEADS * CH), HEADS * CH)]
                             .rearrange("p (r q) -> p r q", q=128), mrow[:, :]).then_inc(mrow_in, 16)
        sp.wait_ge(mrow_in, IMGS * NCH * 16 + LEAD)

    @block.gpsimd
    def _(pool):
        pool_program(pool)


def constants_and_norm(nc, ctx, t, a):
    x_all = t["x_all"]

    def sem(name):
        return ctx.enter_context(nc.semaphore(name))

    def sb(name, shape, dt=F32):
        return ctx.enter_context(nc.sbuf_tensor(name, shape, dt))

    loaded = [sem(f"x_loaded_{b}") for b in range(B)]
    w_loaded, made = sem("w_loaded"), sem("constants_made")
    own_sem, gsum, rooted, ident_made = sem("norm_own"), sem("group_sums"), sem("rooted"), sem("ident_made")
    NST = N // 512
    stats = sb("stats", [128, B, NST, 6])
    mv = sb("mv", [128, B, 2])
    gmat = sb("gmat", [128, C])
    var = sb("gvar", [128, B])
    std = sb("gstd", [128, B])
    tmp = sb("gtmp", [128, B])
    normw = sb("normw", [128, 2])
    eps = sb("eps", [128, 1])
    G = t["M"]
    block = ctx.enter_context(nc.Block())
    W_LOADS = 3 * 2 + 1 + QT + 4

    @block.sync
    def _(sp):
        for b in range(B):
            sp.dma_start(x_all[:, b * N:(b + 1) * N], a["x"][b]).then_inc(loaded[b], 16)

    @block.scalar
    def _(act):
        for r in range(3):
            rows = slice(r * D, (r + 1) * D)
            act.dma_start(t["wqk"][:, :, rows], a["qkv_wT"][:, 0:2 * C].rearrange("i (g d) -> i g d", d=D)) \
               .then_inc(w_loaded, 16)
            act.dma_start(t["qk_b"][rows, :], a["qkv_b"][0:2 * C].rearrange("(g d) -> d g", d=D),
                          allow_slow_non_contiguous=True) \
               .then_inc(w_loaded, 16)
        act.dma_start(t["wv"][:, :], a["qkv_wT"][:, 2 * C:3 * C]).then_inc(w_loaded, 16)
        for k in range(QT):
            act.dma_start(t["vbias"][:, k, :, :],
                          a["qkv_b"][2 * C:3 * C].rearrange("(o h d) -> o h d", o=1, h=HEADS)
                          .broadcast_to([128, HEADS, D])).then_inc(w_loaded, 16)
        act.dma_start(t["proj_w"][:, :], a["proj_wT"]).then_inc(w_loaded, 16)
        act.dma_start(t["proj_b"][:, 0:1], a["proj_b"].rearrange("(p o) -> p o", o=1)).then_inc(w_loaded, 16)
        act.dma_start(normw[:, 0:1], a["norm_w"].rearrange("(p o) -> p o", o=1)).then_inc(w_loaded, 16)
        act.dma_start(normw[:, 1:2], a["norm_b"].rearrange("(p o) -> p o", o=1)).then_inc(w_loaded, 16)
        act.wait_ge(own_sem, 2 * B + 3)
        act.activation(std[:, :], var[:, :], ACT.Sqrt, bias=eps[:, 0:1]).then_inc(rooted, 1)
        act.wait_ge(w_loaded, W_LOADS * 16)

    @block.gpsimd
    def _(pool):
        pool.memset(t["ident"][:, :], 0.0).then_inc(ident_made, 1)
        pool.memset(eps[:, :], GN_EPS).then_inc(made, 1)
        pool.memset(gmat[:, :], 1.0 / GROUP).then_inc(ident_made, 1)
        pool.wait_ge(ident_made, 2)
        pool.affine_select(out=t["ident"][:, :], in_=t["ident"][:, :], compare_op=ALU.not_equal, fill=1.0,
                           base=0, pattern=[[-1, 128]], channel_multiplier=1).then_inc(ident_made, 1)
        g3 = gmat[:, :].rearrange("p (g c) -> p g c", c=GROUP)
        pool.affine_select(out=g3, in_=g3, compare_op=ALU.is_ge, fill=0.0, base=0,
                           pattern=[[-GROUP, C // GROUP], [0, GROUP]], channel_multiplier=1).then_inc(ident_made, 1)
        pool.wait_ge(ident_made, 4)
        pool.affine_select(out=g3, in_=g3, compare_op=ALU.is_ge, fill=0.0, base=GROUP - 1,
                           pattern=[[GROUP, C // GROUP], [0, GROUP]], channel_multiplier=-1).then_inc(made, 1)
        pool.memset(t["vones"][:, :, :, D:2 * D], 1.0).then_inc(ident_made, 1)
        pool.wait_ge(ident_made, 5)
        pool.memset(t["ks"][96:97, :, :], MROW)

    @block.vector
    def _(dve):
        own = Steps(dve, own_sem)
        for b in range(B):
            dve.wait_ge(loaded[b], 16)
            for k in range(NST):
                last = dve.bn_stats(stats[:, b, k, :], x_all[:, b * N + k * 512:b * N + (k + 1) * 512])
            own.inc(last)
            own.sync()
            own.inc(dve.bn_aggr(mv[:, b, :], stats[:, b, :, :]))
        own.sync()
        own.inc(dve.tensor_tensor(tmp[:, :], mv[:, :, 0], mv[:, :, 0], ALU.mult))
        own.sync()
        own.inc(dve.tensor_tensor(mv[:, :, 1], mv[:, :, 1], tmp[:, :], ALU.add))
        dve.wait_ge(gsum, 1)
        own.sync()
        dve.tensor_copy(mv[:, :, :], G[:, 0, 0:2 * B].rearrange("p (b k) -> p b k", k=2)).then_inc(gsum, 1)
        dve.wait_ge(gsum, 2)
        dve.tensor_tensor(tmp[:, :], mv[:, :, 0], mv[:, :, 0], ALU.mult).then_inc(gsum, 1)
        dve.wait_ge(gsum, 3)
        own.inc(dve.tensor_tensor(var[:, :], mv[:, :, 1], tmp[:, :], ALU.subtract))
        dve.wait_ge(rooted, 1)
        own.inc(dve.reciprocal(std[:, :], std[:, :]))
        own.sync()
        dve.wait_ge(w_loaded, W_LOADS * 16)
        own.inc(dve.tensor_scalar(t["gn_a"][:, :], std[:, :], normw[:, 0:1], None, ALU.mult))
        own.sync()
        own.inc(dve.tensor_tensor(tmp[:, :], mv[:, :, 0], t["gn_a"][:, :], ALU.mult))
        own.sync()
        own.inc(dve.tensor_scalar(t["gn_b"][:, :], tmp[:, :], -1.0, normw[:, 1:2], ALU.mult, ALU.add))

    @block.tensor
    def _(pe):
        pe.wait_ge(made, 2)
        pe.wait_ge(own_sem, 2 * B + 2)
        pe.matmul(G[:, 0, 0:2 * B], gmat[:, :], mv[:, :, :].rearrange("p b k -> p (b k)"),
                  start=True, stop=True).then_inc(gsum, 1)


def slots_of(dve, own, rows, cols, base, work):
    w0, w1 = work
    own.inc(dve.tensor_scalar(w1, rows, ~(N - 1), None, ALU.bitwise_and))
    own.inc(dve.tensor_tensor(w0, rows, cols, ALU.bitwise_xor))
    own.sync()
    own.inc(dve.scalar_tensor_tensor(w0, w0, ~(BS - 1), w1, ALU.bitwise_and, ALU.bitwise_or))
    own.sync()
    if base is None:
        own.inc(dve.tensor_scalar(w1, cols, BS - 1, None, ALU.bitwise_and))
    else:
        own.inc(dve.scalar_tensor_tensor(w1, cols, BS - 1, base, ALU.bitwise_and, ALU.bitwise_or))
    own.sync()
    own.inc(dve.scalar_tensor_tensor(w1, rows, 5, w1, ALU.logical_shift_left, ALU.bitwise_or))
    own.sync()


def scatter_index(dve, own, xs, pcol, idx, dup, eq, n):
    own.inc(dve.memset(dup, 0.0))
    own.sync()
    x3 = xs.rearrange("p (n k) -> p n k", k=BATCH)
    d3 = dup.rearrange("p (n k) -> p n k", k=BATCH)
    e3 = eq.rearrange("p (n k) -> p n k", k=BATCH)
    for sft in range(1, BATCH):
        own.inc(dve.tensor_tensor(e3[:, :, 0:BATCH - sft], x3[:, :, 0:BATCH - sft], x3[:, :, sft:BATCH],
                                  ALU.is_equal))
        own.sync()
        own.inc(dve.tensor_tensor(d3[:, :, 0:BATCH - sft], d3[:, :, 0:BATCH - sft],
                                  e3[:, :, 0:BATCH - sft], ALU.max))
        own.sync()
    own.inc(dve.tensor_scalar(eq, xs, float(1 << SLOT_BITS), None, ALU.is_ge))
    own.sync()
    own.inc(dve.tensor_tensor(dup, dup, eq, ALU.max))
    own.inc(dve.tensor_scalar(idx, xs, SLOTS - 1, 7, ALU.bitwise_and, ALU.logical_shift_left))
    own.sync()
    own.inc(dve.tensor_tensor(idx, idx, pcol.to_broadcast([128, n]), ALU.bitwise_or))
    own.sync()
    own.inc(dve.scalar_tensor_tensor(idx, dup, 24, idx, ALU.logical_shift_left, ALU.bitwise_or))
    own.sync()


def edge_lists(nc, ctx, t, a, table):
    def sem(name):
        return ctx.enter_context(nc.semaphore(name))

    def sb(name, shape, dt=F32):
        return ctx.enter_context(nc.sbuf_tensor(name, shape, dt))

    PIECES = EP // PIECE
    loaded = [sem(f"edges_loaded_{j}") for j in range(2)]
    made, taken, own_sem, cleared, zeroed = (sem(n) for n in
        ("edge_consts", "piece_taken", "edge_own", "table_cleared", "zero_made"))
    rc = sb("edge_rc", [128, 2, 2, PIECE], I32)
    base = sb("edge_base", [128, PIECE], I32)
    w0, w1 = sb("edge_w0", [128, PIECE], I32), sb("edge_w1", [128, PIECE], I32)
    key = sb("edge_key", [128, PIECE])
    top = sb("edge_top", [128, PIECE // RUN * 8])
    k1 = sb("edge_k1", [128, RUNS * 8])
    g_f = sb("grp_f", [128, GRP])
    g_i = sb("grp_i", [128, GRP], I32)
    g_j = sb("grp_j", [128, GRP], I32)
    ridx = sb("grp_ridx", [128, GRP], I32)
    ga, gb = sb("grp_a", [128, GRP]), sb("grp_b", [128, GRP])
    la, lb = sb("grp_la", [128, KEEP]), sb("grp_lb", [128, KEEP])
    lists = [sb(f"list_{n}", [128, LIST]) for n in "ab"]
    li = [sb(f"list_i{n}", [128, LIST], I32) for n in range(6)]
    ebase = sb("list_ebase", [128, GRPS, KEEP])
    zero = sb("edge_zero", [128, 4096])
    row_max = sb("ovf_max", [128, 2])
    gate = sb("edge_gate", [128, 1])
    block = ctx.enter_context(nc.Block())
    ZEROS = SLOTS // 32
    LEAD = 2

    @block.sync
    def _(sp):
        with sp.Fori(0, PIECES // 2) as q:
            for j in range(2):
                sp.wait_ge(taken, q * 2 + (j - 1 + LEAD))
                for m in range(2):
                    sp.dma_start(rc[:, j, m, :], a["edges"][m].rearrange("(p e) -> p e", p=128)
                                 [:, bass.ds(q * (2 * PIECE) + j * PIECE, PIECE)]).then_inc(loaded[j], 16)
        sp.wait_ge(cleared, 32 * 16)

    @block.scalar
    def _(act):
        act.wait_ge(zeroed, 1)
        with act.Fori(0, 32) as z:
            act.dma_start(table[bass.ds(z * ZEROS, ZEROS), :].rearrange("(p r) c -> p (r c)", p=128),
                          zero[:, :]).then_inc(cleared, 16)

    @block.gpsimd
    def _(pool):
        pool.memset(zero[:, :], 0.0).then_inc(zeroed, 1)
        pool.iota(base[:, :], pattern=[[0, PIECE // RUN], [-1, RUN]], base=RUN, channel_multiplier=0) \
            .then_inc(made, 1)
        pool.iota(ridx[:, :], pattern=[[-1, GRP]], base=GRP, channel_multiplier=0).then_inc(made, 1)
        pool.iota(t["pcol"][:, :], pattern=[[0, 1]], base=0, channel_multiplier=1).then_inc(made, 1)
        pool.iota(ebase[:, :, :], pattern=[[GRP // 8 * RUN, GRPS], [0, KEEP]], base=RUN + 1,
                  channel_multiplier=EP, allow_small_or_imprecise_dtypes=True).then_inc(made, 1)

    @block.vector
    def _(dve):
        own = Steps(dve, own_sem)
        dve.sem_inc(taken, LEAD)
        dve.wait_ge(made, 4)
        own.inc(dve.tensor_scalar(base[:, :], base[:, :], SLOT_BITS, None, ALU.logical_shift_left))
        own.inc(dve.tensor_scalar(ridx[:, :], ridx[:, :], 12, None, ALU.logical_shift_left))
        own.sync()
        OWN_PIECE = 7
        start = own.n
        with dve.Fori(0, PIECES // 2) as q:
            for j in range(2):
                own.at(q * (2 * OWN_PIECE) + (start + j * OWN_PIECE))
                dve.wait_ge(loaded[j], q * 32 + 32)
                slots_of(dve, own, rc[:, j, 0, :], rc[:, j, 1, :], base[:, :], (w0[:, :], w1[:, :]))
                own.inc(dve.scalar_tensor_tensor(key[:, :], w0[:, :], 0.0, w1[:, :], ALU.is_equal, ALU.mult))
                own.sync_apart(gate[:, 0:1])
                for r in range(PIECE // RUN):
                    last = dve.max(top[:, r * 8:(r + 1) * 8], key[:, r * RUN:(r + 1) * RUN])
                own.inc(last)
                own.sync()
                dve.tensor_copy(k1[:, bass.ds(q * (2 * PIECE // RUN * 8) + j * (PIECE // RUN * 8), PIECE // RUN * 8)],
                                top[:, :]).then_inc(taken, 1)
                assert own.n == OWN_PIECE
        dve.wait_ge(taken, PIECES + LEAD)
        own.at(PIECES * OWN_PIECE + start)
        own.inc(dve.reduce_max(row_max[:, 0:1], k1[:, 7::8], AX.X))
        start = PIECES * OWN_PIECE + start + 1
        OWN_GRP = 7 + 4 * (KEEP // 8)
        with dve.Fori(0, GRPS) as g:
            own.at(g * OWN_GRP + start)
            own.inc(dve.tensor_copy(g_i[:, :], k1[:, bass.ds(g * GRP, GRP)]))
            own.sync()
            for m, gk in ((0, ga), (1, gb)):
                if m:
                    own.inc(dve.tensor_scalar(g_j[:, :], g_i[:, :], 4095, None, ALU.bitwise_and))
                else:
                    own.inc(dve.tensor_scalar(g_j[:, :], g_i[:, :], 12, None, ALU.logical_shift_right))
                own.sync()
                own.inc(dve.tensor_tensor(g_j[:, :], g_j[:, :], ridx[:, :], ALU.bitwise_or))
                own.sync()
                own.inc(dve.scalar_tensor_tensor(gk[:, :], g_i[:, :], 0.0, g_j[:, :], ALU.is_gt, ALU.mult))
                own.sync_apart(gate[:, 0:1]) if m else own.sync()
            for r in range(KEEP // 8):
                for gk, lk in ((ga, la), (gb, lb)):
                    own.inc(dve.max(lk[:, r * 8:(r + 1) * 8], gk[:, :]))
                own.sync_apart(gate[:, 0:1])
                for gk, lk in ((ga, la), (gb, lb)):
                    own.inc(dve.match_replace(gk[:, :], lk[:, r * 8:(r + 1) * 8], gk[:, :], 0.0))
                own.sync_apart(gate[:, 0:1])
            assert own.n == OWN_GRP
            dve.tensor_copy(lists[0][:, bass.ds(g * KEEP, KEEP)], la[:, :])
            dve.tensor_copy(lists[1][:, bass.ds(g * KEEP, KEEP)], lb[:, :]).then_inc(taken, 1)
        own.at(GRPS * OWN_GRP + start)
        dve.wait_ge(taken, PIECES + GRPS + LEAD)
        own.inc(dve.reduce_max(row_max[:, 1:2], lists[0][:, KEEP - 1::KEEP], AX.X))
        own.inc(dve.tensor_copy(li[0][:, :], lists[0][:, :]))
        own.inc(dve.tensor_copy(li[1][:, :], lists[1][:, :]))
        own.sync()
        own.inc(dve.reduce_max(t["ovf"][:, 0:1], row_max[:, :], AX.X))
        own.inc(dve.tensor_scalar(li[2][:, :], li[0][:, :], 4095, 12, ALU.bitwise_and, ALU.logical_shift_left))
        own.inc(dve.tensor_scalar(li[3][:, :], li[1][:, :], 4095, None, ALU.bitwise_and))
        own.inc(dve.tensor_scalar(li[0][:, :], li[0][:, :], 12, None, ALU.logical_shift_right))
        own.sync()
        own.inc(dve.tensor_tensor(li[2][:, :], li[2][:, :], li[3][:, :], ALU.bitwise_or))
        own.inc(dve.tensor_scalar(li[0][:, :], li[0][:, :], -1.0, float(GRP), ALU.mult, ALU.add))
        own.sync()
        own.inc(dve.tensor_scalar(li[1][:, :], li[2][:, :], SLOT_BITS, None, ALU.logical_shift_right))
        own.inc(dve.tensor_scalar(li[2][:, :], li[2][:, :], SLOTS - 1, None, ALU.bitwise_and))
        own.inc(dve.tensor_scalar(li[0][:, :], li[0][:, :], 3, None, ALU.logical_shift_right))
        own.sync()
        own.inc(dve.scalar_tensor_tensor(lists[0][:, :], li[0][:, :], float(RUN), li[1][:, :], ALU.mult, ALU.subtract))
        own.inc(dve.tensor_scalar(li[3][:, :], li[1][:, :], 0.0, float(SLOTS), ALU.is_equal, ALU.mult))
        own.sync()
        own.inc(dve.tensor_tensor(t["list_e"][:, :], lists[0][:, :],
                                  ebase[:, :, :].rearrange("p g k -> p (g k)"), ALU.add))
        own.inc(dve.tensor_tensor(li[2][:, :], li[2][:, :], li[3][:, :], ALU.bitwise_or))
        own.sync()
        scatter_index(dve, own, li[2][:, :], t["pcol"][:, 0:1], t["list_idx"][:, :].bitcast(I32), li[4][:, :], li[5][:, :], LIST)


def scatter_batches(pool, n, idx, ev, idx8, ev8, table, landed):
    flat = table.rearrange("s (c o) -> (s c) o", o=1)
    with pool.Fori(0, n // BATCH) as r:
        pool.drain()
        pool.tensor_copy(idx8[:, :], idx[:, bass.ds(r * BATCH, BATCH)])
        pool.tensor_copy(ev8[:, :], ev[:, bass.ds(r * BATCH, BATCH)])
        pool.drain()
        for k in range(BATCH):
            pool.indirect_dma_start(flat, bass.IndirectOffsetOnAxis(ap=idx8[:, k:k + 1], axis=0),
                                    ev8[:, k:k + 1], None, bounds_check=NOWHERE - 1,
                                    oob_is_err=False).then_inc(landed, 16)
    pool.drain()


def scatter_lists(nc, ctx, t, table):
    landed = ctx.enter_context(nc.semaphore("list_landed"))
    reduced = ctx.enter_context(nc.semaphore("ovf_reduced"))

    def program(pool):
        pool.partition_all_reduce(t["ovf_all"][:, :], t["ovf"][:, :], 128, bass.bass_isa.ReduceOp.max) \
            .then_inc(reduced, 1)
        pool.wait_ge(reduced, 1)
        scatter_batches(pool, LIST, t["list_idx"], t["list_e"], t["idx8"], t["ev8"], table, landed)
        pool.wait_ge(landed, LIST * 16)
    return program


def last_edges(nc, ctx, t, a, table, scratch_m):
    def sem(name):
        return ctx.enter_context(nc.semaphore(name))

    loaded, made, sent, own_sem, landed, ev_made = (sem(n) for n in
        ("gen_loaded", "gen_index_made", "gen_sent", "gen_own", "gen_landed", "gen_ev_made"))
    t_loaded = [sem(f"table_loaded_{j}") for j in range(2)]
    reduced, masked, stored = sem("table_reduced"), sem("mask_made"), sem("mask_stored")
    GP = 512
    PIECES = EP // GP
    pool_of_space = t["qs"][:, :].bitcast(I32)
    rows, cols, w0, w1, idx, dup, eq, ev = (pool_of_space[:, n * GP:(n + 1) * GP] for n in range(8))
    ev = ev.bitcast(F32)
    mask = pool_of_space[:, 0:SLOTS // 128].bitcast(F32)
    TS = 16
    TP = (SLOTS // 128) // TS
    LEAD = 1
    piece = pool_of_space[:, 8 * GP:8 * GP + 2 * TS * 128].bitcast(F32).rearrange("p (j s q) -> p j s q", j=2, q=128)
    block = ctx.enter_context(nc.Block())

    @block.sync
    def _(sp):
        full = sp.value_load(t["ovf_all"][0:1, 0:1].bitcast(I32), min_val=0, max_val=(1 << 31) - 1)
        with sp.If(full > 0):
            with sp.Fori(0, PIECES) as q:
                sp.wait_ge(made, q + LEAD)
                for m, dst in ((0, rows), (1, cols)):
                    sp.dma_start(dst, a["edges"][m].rearrange("(p e) -> p e", p=128)[:, bass.ds(q * GP, GP)]) \
                      .then_inc(loaded, 16)
            sp.wait_ge(sent, PIECES + LEAD)
        tab = table.rearrange("(b s) q -> b (s q)", b=128)
        with sp.Fori(0, TP // 2) as q:
            for j in range(2):
                sp.wait_ge(reduced, q * 2 + LEAD)
                sp.dma_start(piece[:, j, :, :].rearrange("p s q -> p (s q)"),
                             tab[:, bass.ds(q * (2 * TS * 128) + j * (TS * 128), TS * 128)]).then_inc(t_loaded[j], 16)
        sp.wait_ge(masked, 1)
        sp.dma_start(scratch_m, mask).then_inc(stored, 16)
        sp.wait_ge(stored, 16)

    @block.gpsimd
    def _(pool):
        pool.sem_inc(sent, LEAD)
        full = pool.value_load(t["ovf_all"][0:1, 0:1].bitcast(I32), min_val=0, max_val=(1 << 31) - 1)
        with pool.If(full > 0):
            pool.iota(ev, pattern=[[1, GP]], base=1 - GP, channel_multiplier=EP,
                      allow_small_or_imprecise_dtypes=True).then_inc(ev_made, 1)
            with pool.Fori(0, PIECES) as q:
                pool.wait_ge(made, q + (1 + LEAD))
                pool.tensor_tensor(t["ev8"][:, :], t["ev8"][:, :], t["ev8"][:, :], ALU.add)
                scatter_batches(pool, GP, idx.bitcast(U32), ev, t["idx8"], t["ev8"], table, landed)
                pool.wait_ge(landed, GP * 16)
                pool.inc_swdge_sem([landed], [GP * 16], mode="sub")
                pool.memset(t["ev8"][:, 0:1], 0.0).then_inc(sent, 1)

    @block.vector
    def _(dve):
        own = Steps(dve, own_sem)
        for x in (made, reduced):
            dve.sem_inc(x, LEAD)
        full = dve.value_load(t["ovf_all"][0:1, 0:1].bitcast(I32), min_val=0, max_val=(1 << 31) - 1)
        with dve.If(full > 0):
            dve.wait_ge(ev_made, 1)
            OWN = 5 + 3 + 1 + 2 * (BATCH - 1) + 5 + 1 - 1
            with dve.Fori(0, PIECES) as q:
                own.at(q * OWN)
                dve.wait_ge(sent, q + LEAD)
                dve.wait_ge(loaded, q * 32 + 32)
                slots_of(dve, own, rows, cols, None, (w0, w1))
                own.inc(dve.tensor_scalar(w0, w0, 0.0, float(SLOTS), ALU.not_equal, ALU.mult))
                own.inc(dve.tensor_scalar(w1, w1, SLOTS - 1, None, ALU.bitwise_and))
                own.sync()
                own.inc(dve.tensor_tensor(w1, w1, w0, ALU.bitwise_or))
                own.sync()
                scatter_index(dve, own, w1, t["pcol"][:, 0:1], idx, dup, eq, GP)
                assert own.n == OWN, own.n
                dve.tensor_scalar(ev, ev, float(GP), None, ALU.add).then_inc(made, 1)
        with dve.Fori(0, TP // 2) as q:
            for j in range(2):
                dve.wait_ge(t_loaded[j], q * 16 + 16)
                dve.tensor_reduce(t["t_edge"][:, bass.ds(q * (2 * TS) + j * TS, TS)], piece[:, j, :, :],
                                  AX.X, ALU.max).then_inc(reduced, 1)
        dve.wait_ge(reduced, TP + LEAD)
        dve.tensor_scalar(mask, t["t_edge"][:, :], 0.0, None, ALU.is_gt).then_inc(masked, 1)
        dve.tensor_scalar(t["t_idx"][:, :], t["t_edge"][:, :], -1.0, 0.0, ALU.add, ALU.max)


def gather_values(nc, ctx, t, a, scratch_v):
    got = ctx.enter_context(nc.semaphore("values_got"))
    stored = ctx.enter_context(nc.semaphore("values_stored"))
    W = 16
    SB = SLOTS // 128

    def program(pool):
        flat = a["edge_values"].rearrange("(e o) -> e o", o=1)
        with pool.Fori(0, SB // W) as r:
            pool.drain()
            pool.tensor_copy(t["gidx"][:, :], t["t_idx"][:, bass.ds(r * W, W)])
            pool.drain()
            for k in range(W):
                pool.indirect_dma_start(t["gval"][:, k:k + 1], None, flat,
                                        bass.IndirectOffsetOnAxis(ap=t["gidx"][:, k:k + 1], axis=0)) \
                    .then_inc(got, 16)
            pool.drain()
            pool.tensor_copy(t["t_edge"][:, bass.ds(r * W, W)], t["gval"][:, :])
        pool.drain()
        pool.dma_start(scratch_v, t["t_edge"][:, :]).then_inc(stored, 16)
        pool.wait_ge(stored, 16)
    return program


TOK_EPS = 1e-5
GROUPS = B * N // CH
GPI = N // CH
NBLK = CH // BS
EXPERTS = 8


def turns(eng, body):
    for i in range(4):
        body(i, i % 2)
    with eng.Fori(0, (GROUPS - 4) // 2) as r:
        for j in range(2):
            body(r * 2 + (4 + j), j)
    for i in range(GROUPS, GROUPS + 2):
        body(i, i % 2)


def live(g):
    return not isinstance(g, int) or 0 <= g < GROUPS


class TokenNorm:

    def __init__(self, nc, ctx, t, name):
        def sem(n):
            return ctx.enter_context(nc.semaphore(f"{name}_{n}"))

        def sb(n, shape):
            return ctx.enter_context(nc.sbuf_tensor(f"{name}_{n}", shape, F32))
        self.t = t
        self.mean_ready = sem("mean_ready")
        self.centered = sem("centered")
        self.squared = sem("squared")
        self.var_ready = sem("var_ready")
        self.log_done = sem("log_done")
        self.rstd = sem("rstd")
        self.normed = sem("normed")
        self.xc, self.xh = sb("xc", [128, 2, CH]), sb("xh", [128, 2, CH])
        self.sq, self.rs = sb("sq", [128, CH]), sb("rs", [128, CH])
        self.bank = t["M"][:, 0, :]

    def x(self, g):
        return self.t["x_all"][:, g * CH:(g + 1) * CH] if isinstance(g, int) else \
            self.t["x_all"][:, bass.ds(g * CH, CH)]

    def pe_mean(self, pe, g):
        pe.wait_ge(self.rstd, g)
        pe.matmul(self.bank, self.t["avg"][:, :], self.x(g), start=True, stop=True) \
          .then_inc(self.mean_ready, 1)

    def dve_center(self, dve, g, p):
        dve.wait_ge(self.mean_ready, g + 1)
        dve.tensor_tensor(self.xc[:, p, :], self.x(g), self.bank, ALU.subtract).then_inc(self.centered, 1)

    def act_square(self, act, g, p):
        act.wait_ge(self.centered, g + 1)
        act.wait_ge(self.var_ready, g)
        act.activation(self.sq[:, :], self.xc[:, p, :], ACT.Square).then_inc(self.squared, 1)

    def pe_var(self, pe, g):
        pe.wait_ge(self.squared, g + 1)
        pe.matmul(self.bank, self.t["avg"][:, :], self.sq[:, :], start=True, stop=True) \
          .then_inc(self.var_ready, 1)

    def act_rstd(self, act, g):
        act.wait_ge(self.var_ready, g + 1)
        act.wait_ge(self.normed, g)
        act.activation(self.rs[:, :], self.bank, ACT.Ln, bias=self.t["eps"][:, 0:1]).then_inc(self.log_done, 1)
        act.wait_ge(self.log_done, g + 1)
        act.activation(self.rs[:, :], self.rs[:, :], ACT.Exp, scale=-0.5).then_inc(self.rstd, 1)

    def dve_norm(self, dve, g, p):
        dve.wait_ge(self.rstd, g + 1)
        dve.tensor_tensor(self.xh[:, p, :], self.xc[:, p, :], self.rs[:, :], ALU.mult).then_inc(self.normed, 1)


def layer1_constants(nc, ctx, t, a, scratch_v, scratch_m):
    def sem(name):
        return ctx.enter_context(nc.semaphore(name))

    def sb(name, shape, dt=F32):
        return ctx.enter_context(nc.sbuf_tensor(name, shape, dt))
    loaded, made, own_sem = sem("l1_loaded"), sem("l1_made"), sem("l1_own")
    TT = N // 128
    w, m = sb("slot_w", [128, TT, BS]), sb("slot_m", [128, TT, BS])
    diag, tmp = sb("diag", [128, BS]), sb("slot_tmp", [128, TT, BS])
    gw = sb("gate_wb", [128, 3, HEADS])
    block = ctx.enter_context(nc.Block())

    @block.sync
    def _(sp):
        for dst, src in ((w, scratch_v), (m, scratch_m)):
            sp.dma_start(dst[:, :, :], src.rearrange("b (r k) -> (b r) k", k=BS)
                         .rearrange("(t q) k -> q t k", q=128)).then_inc(loaded, 16)
        row = lambda v, n: v.rearrange("(o n) -> o n", o=1).broadcast_to([128, n])
        col = lambda v: v.rearrange("(p o) -> p o", o=1)
        sp.dma_start(gw[:, 0, :], a["gate_w"].rearrange("h o -> (h o)").rearrange("(o n) -> o n", o=1).broadcast_to([128, HEADS])).then_inc(loaded, 16)
        sp.dma_start(gw[:, 1, :], row(a["gate_b"], HEADS)).then_inc(loaded, 16)
        sp.dma_start(t["w1"][:, :], a["qkv1_w"]).then_inc(loaded, 16)
        for k in range(2):
            sp.dma_start(t["b1"][:, k:k + 1], col(a["qkv1_b"][k * C:(k + 1) * C])).then_inc(loaded, 16)
        for h in range(HEADS):
            sp.dma_start(t["bv1"][h * BS:(h + 1) * BS, :],
                         a["qkv1_b"][2 * C + h * D:2 * C + (h + 1) * D].rearrange("(o n) -> o n", o=1)
                         .broadcast_to([BS, D])).then_inc(loaded, 16)
        sp.dma_start(t["pw1"][:, :], a["proj1_w"]).then_inc(loaded, 16)
        sp.dma_start(t["pb1"][:, 0:1], col(a["proj1_b"])).then_inc(loaded, 16)
        sp.dma_start(t["rw"][:, :], a["router_w"]).then_inc(loaded, 16)
        for k in range(QT):
            sp.dma_start(t["rb"][:, k, :], row(a["router_b"], EXPERTS)).then_inc(loaded, 16)
        sp.dma_start(t["ew"][:, :, :], a["expert_w"].rearrange("e d c -> d e c")).then_inc(loaded, 16)
        sp.dma_start(t["eb"][:, :], a["expert_b"]).then_inc(loaded, 16)
        sp.wait_ge(loaded, (4 + 1 + 2 + HEADS + 2 + 1 + QT + 2) * 16)

    @block.gpsimd
    def _(pool):
        pool.memset(diag[:, :], 0.0).then_inc(made, 1)
        pool.memset(t["avg"][:, :], 1.0 / C).then_inc(made, 1)
        pool.memset(t["eps"][:, :], TOK_EPS).then_inc(made, 1)
        pool.memset(t["kexp"][:, :, :, :, :], 0.0).then_inc(made, 1)
        pool.memset(t["vexp"][:, :, :, :], 0.0).then_inc(made, 1)
        pool.iota(t["iota8"][:, :], pattern=[[1, EXPERTS]], base=0, channel_multiplier=0,
                  allow_small_or_imprecise_dtypes=True).then_inc(made, 1)
        for q in range(128 // BS):
            pool.wait_ge(made, 6 + q)
            pool.affine_select(out=diag[:, :], in_=diag[:, :], compare_op=ALU.not_equal, fill=1.0,
                               base=-q * BS, pattern=[[-1, BS]], channel_multiplier=1).then_inc(made, 1)

    @block.vector
    def _(dve):
        own = Steps(dve, own_sem)
        dve.wait_ge(made, 6 + 128 // BS)
        dve.wait_ge(loaded, (4 + 1 + 2 + HEADS + 2 + 1 + QT + 2) * 16)
        d3 = diag[:, :].rearrange("p (o k) -> p o k", o=1).broadcast_to([128, TT, BS])
        own.inc(dve.tensor_tensor(w[:, :, :], w[:, :, :], m[:, :, :], ALU.mult))
        own.sync()
        own.inc(dve.tensor_scalar(tmp[:, :, :], w[:, :, :], -1.0, 1.0, ALU.mult, ALU.add))
        own.sync()
        own.inc(dve.tensor_tensor(tmp[:, :, :], tmp[:, :, :], d3, ALU.mult))
        own.inc(dve.tensor_tensor(m[:, :, :], m[:, :, :], d3, ALU.max))
        own.sync()
        own.inc(dve.tensor_tensor(w[:, :, :], w[:, :, :], tmp[:, :, :], ALU.add))
        own.sync()
        own.inc(dve.tensor_scalar(tmp[:, :, :], m[:, :, :], -1.0, 1e9, ALU.add, ALU.mult))
        own.inc(dve.tensor_tensor(gw[:, 2, :], gw[:, 0, :], gw[:, 1, :], ALU.add))
        own.sync()
        own.inc(dve.tensor_tensor(t["bias"][:, :, :], tmp[:, :, :], w[:, :, :], ALU.add))
        own.inc(dve.tensor_scalar(gw[:, 2, :], gw[:, 2, :], 1.0 / BS, None, ALU.mult))
        own.sync()
        for h in range(HEADS):
            own.inc(dve.tensor_scalar(t["gate"][:, :, h, :], m[:, :, :], gw[:, 1, h:h + 1],
                                      gw[:, 2, h:h + 1], ALU.mult, ALU.add))
        own.sync()
        for h in range(HEADS):
            own.inc(dve.scalar_tensor_tensor(t["gate"][:, :, h, :], w[:, :, :], gw[:, 0, h:h + 1],
                                             t["gate"][:, :, h, :], ALU.mult, ALU.add))


def block_attention(nc, ctx, t):
    def sem(name):
        return ctx.enter_context(nc.semaphore("a1_" + name))

    def sb(name, shape, dt=F32):
        return ctx.enter_context(nc.sbuf_tensor("a1_" + name, shape, dt))
    ln = TokenNorm(nc, ctx, t, "ln1")
    qk_ready, qk_taken = sem("qk_ready"), sem("qk_taken")
    v_ready, v_taken = sem("v_ready"), sem("v_taken")
    s_ready, s_taken = sem("s_ready"), sem("s_taken")
    shifted, exped, mixed = sem("shifted"), sem("exped"), sem("mixed")
    ct_ready, ct_taken = sem("ct_ready"), sem("ct_taken")
    av_ready, av_taken = sem("av_ready"), sem("av_taken")
    proj_ready, added, own_sem = sem("proj_ready"), sem("added"), sem("own")
    q_t = sb("q_t", [128, CH])
    sc = sb("sc", [128, QT, HEADS, BS])
    mix = sb("mix", [128, 2, QT, HEADS, BS])
    sm = sb("sm", [128, 6, QT * HEADS])
    ct, av = sb("ct", [128, CH]), sb("av", [128, CH])
    qb, kb = t["M"][:, 1, :], t["S"][:, 0, 0:CH]
    vb = t["S"][:, 0, CH:2 * CH]
    sbk, ctb, avb = t["S"][:, 1, CH:2 * CH], t["O"][:, 0, :], t["O"][:, 1, :]
    kexp, vexp, w1 = t["kexp"], t["vexp"], t["w1"]
    block = ctx.enter_context(nc.Block())

    @block.tensor
    def _(pe):
        def turn(i, p):
            g, f, e = i, i - 1, i - 2
            if live(g):
                ln.pe_mean(pe, g)
            if live(e):
                pe.wait_ge(mixed, e + 1)
                pe.wait_ge(ct_taken, e)
                for k in range(QT):
                    last = pe.matmul(ctb[:, k * 128:(k + 1) * 128],
                                     mix[:, p, k, :, :].rearrange("p h k -> p (h k)"), t["ident"][:, :],
                                     start=True, stop=True)
                last.then_inc(ct_ready, 1)
            if live(f):
                xh = ln.xh[:, 1 - p, :]
                pe.wait_ge(ln.normed, f + 1)
                pe.wait_ge(qk_taken, f * 2)
                pe.matmul(qb, w1[:, 0:C], xh, start=True, stop=True)
                pe.matmul(kb, w1[:, C:2 * C], xh, start=True, stop=True).then_inc(qk_ready, 1)
                pe.wait_ge(v_taken, f)
                for n in range(NBLK):
                    for h in range(HEADS):
                        last = pe.matmul(vb[h * BS:(h + 1) * BS, n * D:(n + 1) * D],
                                         xh[:, n * BS:(n + 1) * BS],
                                         w1[:, 2 * C + h * D:2 * C + (h + 1) * D], start=True, stop=True)
                last.then_inc(v_ready, 1)
            if live(g):
                ln.pe_var(pe, g)
            if live(e):
                pe.wait_ge(ct_taken, e + 1)
                pe.wait_ge(added, e)
                for n in range(NBLK):
                    last = pe.matmul(avb[:, n * BS:(n + 1) * BS], vexp[:, p, n, :],
                                     ct[:, n * BS:(n + 1) * BS], start=True, stop=True)
                last.then_inc(av_ready, 1)
            if live(f):
                pe.wait_ge(qk_taken, (f + 1) * 2)
                pe.wait_ge(s_taken, f)
                for n in range(NBLK):
                    r = n % 4 * BS
                    last = pe.matmul(sbk[r:r + BS, n // 4 * C:(n // 4 + 1) * C], q_t[:, n * BS:(n + 1) * BS],
                                     kexp[:, 1 - p, n, :, :].rearrange("p h k -> p (h k)"), start=True, stop=True)
                last.then_inc(s_ready, 1)
            if live(e):
                pe.wait_ge(av_taken, e + 1)
                pe.matmul(avb, t["pw1"][:, :], av[:, :], start=True, stop=True).then_inc(proj_ready, 1)
        turns(pe, turn)

    @block.vector
    def _(dve):
        OWN = 6
        own = Steps(dve, own_sem)

        def turn(i, p):
            g, f, e = i, i - 1, i - 2
            if live(g):
                ln.dve_center(dve, g, p)
            if live(f):
                if not isinstance(f, int) or f > 1:
                    dve.wait_ge(av_ready, f - 1)
                dve.wait_ge(v_ready, f + 1)
                for h in range(HEADS):
                    rows = slice(h * BS, (h + 1) * BS)
                    last = dve.tensor_tensor(vexp[rows, 1 - p, :, h * D:(h + 1) * D],
                                             vb.rearrange("p (n d) -> p n d", d=D)[rows, :, :],
                                             t["bv1"][rows, :].rearrange("p (o d) -> p o d", o=1)
                                             .broadcast_to([D, NBLK, D]), ALU.add)
                last.then_inc(v_taken, 1)
            if live(g):
                ln.dve_norm(dve, g, p)
            if live(f):
                own.at(f * OWN)
                grp = f % GPI * QT
                cols = slice(grp, grp + QT) if isinstance(f, int) else bass.ds(grp, QT)
                s4 = sbk.rearrange("p (t h k) -> p t h k", t=QT, h=HEADS)
                s3 = sbk.rearrange("p (t k) -> p t k", k=BS)
                c3 = sc[:, :, :, :].rearrange("p t h k -> p (t h) k")
                m3 = mix[:, 1 - p, :, :, :].rearrange("p t h k -> p (t h) k")

                def wide(n):
                    return sm[:, n, :].rearrange("p (t o) -> p t o", o=1).broadcast_to([128, QT * HEADS, BS])
                dve.wait_ge(s_ready, f + 1)
                dve.wait_ge(mixed, f)
                for k in range(QT):
                    one = slice(grp + k, grp + k + 1) if isinstance(f, int) else bass.ds(grp + k, 1)
                    last = dve.scalar_tensor_tensor(sc[:, k, :, :], s4[:, k, :, :], SCALE,
                                                    t["bias"][:, one, :].broadcast_to([128, HEADS, BS]),
                                                    ALU.mult, ALU.add)
                own.inc(last)
                dve.tensor_reduce(sm[:, 0, :], s3, AX.X, ALU.add).then_inc(s_taken, 1)
                dve.wait_ge(s_taken, f + 1)
                own.sync()
                own.inc(dve.tensor_scalar(sm[:, 0, :], sm[:, 0, :], SCALE / BS, 1.0, ALU.mult, ALU.add))
                own.inc(dve.tensor_reduce(sm[:, 1, :], c3, AX.X, ALU.max))
                own.sync()
                own.inc(dve.tensor_tensor(sm[:, 1, :], sm[:, 1, :], sm[:, 0, :], ALU.max))
                own.sync()
                own.inc(dve.tensor_tensor(c3, c3, wide(1), ALU.subtract))
                dve.tensor_tensor(sm[:, 2, :], sm[:, 0, :], sm[:, 1, :], ALU.subtract).then_inc(shifted, 1)
            if live(e):
                dve.wait_ge(proj_ready, e + 1)
                x = ln.x(e)
                dve.scalar_tensor_tensor(x, avb, t["pb1"][:, 0:1], x, ALU.add, ALU.add).then_inc(added, 1)
            if live(f):
                dve.wait_ge(exped, f * 2 + 2)
                if not isinstance(f, int) or f > 1:
                    dve.wait_ge(ct_ready, f - 1)
                own.inc(dve.tensor_reduce(sm[:, 3, :], c3, AX.X, ALU.add))
                own.sync()
                dve.tensor_tensor(sm[:, 3, :], sm[:, 3, :], sm[:, 2, :], ALU.add).then_inc(ln_own[0], 1)
                dve.wait_ge(ln_own[0], f * 4 + 1)
                dve.reciprocal(sm[:, 4, :], sm[:, 3, :]).then_inc(ln_own[0], 1)
                dve.wait_ge(ln_own[0], f * 4 + 2)
                dve.scalar_tensor_tensor(sm[:, 5, :], sm[:, 2, :], 1.0 / BS, sm[:, 4, :], ALU.mult, ALU.mult)
                dve.tensor_tensor(m3, c3, wide(4), ALU.mult).then_inc(ln_own[0], 1)
                dve.wait_ge(ln_own[0], f * 4 + 3)
                dve.tensor_tensor(mix[:, 1 - p, :, :, :], mix[:, 1 - p, :, :, :], t["gate"][:, cols, :, :],
                                  ALU.add).then_inc(ln_own[0], 1)
                dve.wait_ge(ln_own[0], f * 4 + 4)
                dve.tensor_tensor(m3, m3, wide(5), ALU.add).then_inc(mixed, 1)
        ln_own = [ctx.enter_context(nc.semaphore("a1_own2"))]
        turns(dve, turn)

    @block.scalar
    def _(act):
        def turn(i, p):
            g, f, e = i, i - 1, i - 2
            if live(g):
                ln.act_square(act, g, p)
            if live(e):
                act.wait_ge(ct_ready, e + 1)
                act.wait_ge(av_ready, e)
                act.activation(ct[:, :], ctb, ACT.Identity).then_inc(ct_taken, 1)
            if live(f):
                act.wait_ge(qk_ready, f + 1)
                act.wait_ge(s_ready, f)
                act.activation(q_t[:, :], qb, ACT.Identity, bias=t["b1"][:, 0:1]).then_inc(qk_taken, 1)
                for h in range(HEADS):
                    rows = slice(h * D, (h + 1) * D)
                    last = act.activation(kexp[rows, 1 - p, :, h, :],
                                          kb.rearrange("p (n k) -> p n k", k=BS)[rows, :, :],
                                          ACT.Identity, bias=t["b1"][rows, 1:2])
                last.then_inc(qk_taken, 1)
            if live(g):
                ln.act_rstd(act, g)
            if live(e):
                act.wait_ge(av_ready, e + 1)
                act.wait_ge(proj_ready, e)
                act.activation(av[:, :], avb, ACT.Identity).then_inc(av_taken, 1)
            if live(f):
                act.wait_ge(shifted, f + 1)
                act.activation(sc[:, :, :, :], sc[:, :, :, :], ACT.Exp).then_inc(exped, 1)
                act.activation(sm[:, 2, :], sm[:, 2, :], ACT.Exp).then_inc(exped, 1)
        turns(act, turn)


def experts(nc, ctx, t, out):
    def sem(name):
        return ctx.enter_context(nc.semaphore("moe_" + name))

    def sb(name, shape, dt=F32):
        return ctx.enter_context(nc.sbuf_tensor("moe_" + name, shape, dt))
    ln = TokenNorm(nc, ctx, t, "ln2")
    r_ready, r_taken, exped = sem("r_ready"), sem("r_taken"), sem("exped")
    gated, e_ready, e_taken = sem("gated"), sem("e_ready"), sem("e_taken")
    gt_ready, gt_taken, f_ready, summed = sem("gt_ready"), sem("gt_taken"), sem("f_ready"), sem("summed")
    stored = [sem(f"stored_{j}") for j in range(2)]
    own_sem = sem("own")
    lg = sb("lg", [128, QT, EXPERTS])
    mx, den = sb("mx", [128, QT]), sb("den", [128, QT])
    best = sb("best", [128, QT, 8])
    bidx, bidxf = sb("bidx", [128, QT, 8], U32), sb("bidxf", [128, QT, 8])
    gates = sb("gates", [128, 2, QT, EXPERTS])
    g2 = sb("g2", [128, QT, EXPERTS])
    acc = sb("acc", [128, 2, QT, C])
    gt = sb("gt", [EXPERTS, CH])
    y = sb("y", [128, 2, CH])
    gate_scratch = sb("gate", [128, 1])
    rbk, gtb, fbk = t["M"][:, 1, :], t["O"][:, 0, :], t["O"][:, 1, :]
    ebk = t["S"]
    img = out.rearrange("b c n -> c b n")
    block = ctx.enter_context(nc.Block())

    @block.tensor
    def _(pe):
        def turn(i, p):
            g, f, e = i, i - 1, i - 2
            xh = ln.xh[:, 1 - p, :]
            if live(g):
                ln.pe_mean(pe, g)
            if live(f):
                pe.wait_ge(ln.normed, f + 1)
                pe.wait_ge(r_taken, f)
                for k in range(QT):
                    last = pe.matmul(rbk[:, k * EXPERTS:(k + 1) * EXPERTS], xh[:, k * 128:(k + 1) * 128],
                                     t["rw"][:, :], start=True, stop=True)
                last.then_inc(r_ready, 1)
            if live(g):
                ln.pe_var(pe, g)
            if live(e):
                pe.wait_ge(e_taken, (e + 1) * QT)
                pe.wait_ge(gt_taken, e)
                for k in range(QT):
                    last = pe.matmul(gtb[0:EXPERTS, k * 128:(k + 1) * 128], gates[:, p, k, :],
                                     t["ident"][:, :], start=True, stop=True)
                last.then_inc(gt_ready, 1)
            def expert_products(k):
                if not isinstance(f, int) or f > 0 or k >= 2:
                    pe.wait_ge(e_taken, f * QT + (k - 1))
                for m in range(2):
                    last = pe.matmul(ebk[:, k % 2, m * CH:(m + 1) * CH], xh[:, k * 128:(k + 1) * 128],
                                     t["ew"][:, 4 * m:4 * m + 4, :].rearrange("p e c -> p (e c)"),
                                     start=True, stop=True)
                last.then_inc(e_ready, 1)
            if live(f):
                expert_products(0)
                expert_products(1)
            if live(e):
                pe.wait_ge(gt_taken, e + 1)
                pe.wait_ge(summed, e)
                pe.matmul(fbk, t["eb"][:, :], gt[:, :], start=True, stop=False, skip_group_check=True)
                for k in range(QT):
                    last = pe.matmul(fbk[:, k * 128:(k + 1) * 128], acc[:, p, k, :], t["ident"][:, :],
                                     start=False, stop=(k == QT - 1), skip_group_check=True)
                last.then_inc(f_ready, 1)
            if live(f):
                expert_products(2)
                expert_products(3)
        turns(pe, turn)

    @block.scalar
    def _(act):
        def turn(i, p):
            g, f, e = i, i - 1, i - 2
            if live(g):
                ln.act_square(act, g, p)
            if live(f):
                act.wait_ge(gated, f * 2 + 1)
                act.activation(lg[:, :, :], lg[:, :, :], ACT.Exp).then_inc(exped, 1)
            if live(g):
                ln.act_rstd(act, g)
            if live(e):
                act.wait_ge(gt_ready, e + 1)
                act.wait_ge(f_ready, e)
                act.activation(gt[:, :], gtb[0:EXPERTS, :], ACT.Identity).then_inc(gt_taken, 1)
        turns(act, turn)

    @block.vector
    def _(dve):
        own = Steps(dve, own_sem)
        OWN = 2 + 8

        def wide(v):
            return v.rearrange("p (t o) -> p t o", o=1).broadcast_to([128, QT, EXPERTS])

        def turn(i, p):
            g, f, e = i, i - 1, i - 2
            if live(g):
                ln.dve_center(dve, g, p)
            if live(f):
                own.at(f * OWN)
                dve.wait_ge(r_ready, f + 1)
                dve.tensor_tensor(lg[:, :, :], rbk[:, 0:QT * EXPERTS].rearrange("p (t e) -> p t e", t=QT),
                                  t["rb"][:, :, :], ALU.add).then_inc(r_taken, 1)
                dve.wait_ge(r_taken, f + 1)
                own.inc(dve.tensor_reduce(mx[:, :], lg[:, :, :], AX.X, ALU.max))
                own.sync()
                dve.tensor_tensor(lg[:, :, :], lg[:, :, :], wide(mx[:, :]), ALU.subtract).then_inc(gated, 1)
            if live(e):
                dve.wait_ge(f_ready, e + 1)
                if not isinstance(e, int) or e > 1:
                    dve.wait_ge(stored[p], (e - p) * 8)
                dve.tensor_tensor(y[:, p, :], fbk, ln.x(e), ALU.add).then_inc(summed, 1)
            if live(f):
                dve.wait_ge(exped, f + 1)
                own.inc(dve.tensor_reduce(den[:, :], lg[:, :, :], AX.X, ALU.add))
                own.sync()
                own.inc(dve.reciprocal(den[:, :], den[:, :]))
                own.sync()
                own.inc(dve.tensor_tensor(lg[:, :, :], lg[:, :, :], wide(den[:, :]), ALU.mult))
                own.sync_apart(gate_scratch[:, 0:1])
                for k in range(QT):
                    last = dve.max(best[:, k, :], lg[:, k, :])
                own.inc(last)
                own.sync_apart(gate_scratch[:, 0:1])
                for k in range(QT):
                    dve.max_index(bidx[:, k, :], best[:, k, :], lg[:, k, :])
                own.inc(dve.tensor_tensor(den[:, :], best[:, :, 0], best[:, :, 1], ALU.add))
                own.sync()
                own.inc(dve.reciprocal(den[:, :], den[:, :]))
                own.inc(dve.tensor_copy(bidxf[:, :, :], bidx[:, :, :]))
                own.sync()
                own.inc(dve.tensor_tensor(best[:, :, :], best[:, :, :], wide(den[:, :]), ALU.mult))
                own.sync()
                for k in range(QT):
                    dve.tensor_scalar(gates[:, 1 - p, k, :], t["iota8"][:, :], bidxf[:, k, 0:1], best[:, k, 0:1],
                                      ALU.is_equal, ALU.mult)
                    last = dve.tensor_scalar(g2[:, k, :], t["iota8"][:, :], bidxf[:, k, 1:2], best[:, k, 1:2],
                                             ALU.is_equal, ALU.mult)
                own.inc(last)
                own.sync()
                dve.tensor_tensor(gates[:, 1 - p, :, :], gates[:, 1 - p, :, :], g2[:, :, :], ALU.add) \
                   .then_inc(gated, 1)
            if live(g):
                ln.dve_norm(dve, g, p)
            if live(f):
                dve.wait_ge(gated, f * 2 + 2)
                if not isinstance(f, int) or f > 1:
                    dve.wait_ge(f_ready, f - 1)
                for k in range(QT):
                    dve.wait_ge(e_ready, f * QT + (k + 1))
                    for x in range(EXPERTS):
                        src = ebk[:, k % 2, x * C:(x + 1) * C]
                        gx = gates[:, 1 - p, k, x:x + 1]
                        if x == 0:
                            last = dve.tensor_scalar(acc[:, 1 - p, k, :], src, gx, None, ALU.mult)
                        else:
                            last = dve.scalar_tensor_tensor(acc[:, 1 - p, k, :], src, gx,
                                                            acc[:, 1 - p, k, :], ALU.mult, ALU.add)
                        if x < EXPERTS - 1:
                            last.then_inc(acc_own, 1)
                            dve.wait_ge(acc_own, f * (QT * (EXPERTS - 1)) + (k * (EXPERTS - 1) + x + 1))
                    last.then_inc(e_taken, 1)
        acc_own = ctx.enter_context(nc.semaphore("moe_acc_own"))
        turns(dve, turn)

    @block.sync
    def _(sp):
        with sp.Fori(0, B) as b:
            with sp.Fori(0, GPI // 2) as r:
                for j in range(2):
                    sp.wait_ge(summed, b * GPI + r * 2 + (j + 1))
                    sp.dma_start(img[:, bass.ds(b, 1), bass.ds(r * (2 * CH) + j * CH, CH)],
                                 y[:, j, :].rearrange("p (o n) -> p o n", o=1)).then_inc(stored[j], 16)
        for j in range(2):
            sp.wait_ge(stored[j], GROUPS // 2 * 16)


def build(nc, a, out, dbg=None):
    with ExitStack() as whole:
        def sb(name, shape, dt=F32, ctx=whole):
            return ctx.enter_context(nc.sbuf_tensor(name, shape, dt))

        t = {
            "x_all": sb("x_all", [128, B * N]),
            "ident": sb("ident", [128, 128]),
            "gn_a": sb("gn_a", [128, B]), "gn_b": sb("gn_b", [128, B]),
        }
        for name, shape in (("S", [128, 2, 2 * CH]), ("O", [128, 2, CH]), ("M", [128, 2, CH])):
            t[name] = whole.enter_context(nc.psum_tensor(name, shape, F32))
        for name, shape, dt in (
                ("pcol", [128, 1], I32), ("ovf", [128, 1], F32), ("ovf_all", [128, 1], F32),
                ("idx8", [128, BATCH], U32), ("ev8", [128, BATCH], F32),
                ("list", [128, 2 * LIST], F32)):
            t[name] = sb(name, shape, dt)
        SB = SLOTS // 128
        t["list_e"], t["list_idx"] = t["list"][:, 0:LIST], t["list"][:, LIST:2 * LIST].bitcast(U32)
        t["t_idx"] = t["list"][:, 0:SB].bitcast(U32)
        table = nc.dram_tensor("slot_table", (SLOTS, 128), F32).ap()
        scratch_v = nc.dram_tensor("slot_values", (128, SB), F32).ap()
        scratch_m = nc.dram_tensor("slot_masks", (128, SB), F32).ap()
        with ExitStack() as c:
            edge_lists(nc, c, t, a, table)
        with ExitStack() as l0:
            t.update({
                "qs": sb("q_stack", [128, NCH * HEADS * CH], F16, l0),
                "ks": sb("k_stack", [128, HEADS, N], F16, l0),
                "vones": sb("v_ones", [128, KT, HEADS, 2 * D], F32, l0),
                "probs": sb("probs", [128, 3, 2 * CH], F32, l0),
                "xn": sb("x_norm", [128, 2, CH], F32, l0),
                "o_t": sb("o_t", [128, CH], F32, l0),
                "os": sb("o_sums", [128, 2, CH], F32, l0),
                "dn": sb("dens", [128, 2, CH], F32, l0),
                "mx8": sb("mx8", [128, HEADS * QT, NCH], F32, l0),
                "mx": sb("mx", [128, HEADS * QT], F32, l0),
                "mrow": sb("mrow", [HEADS * QT, 128], F16, l0),
                "wqk": sb("w_qk", [128, 2 * HEADS, 3 * D], F32, l0),
                "wv": sb("w_v", [128, C], F32, l0),
                "qk_b": sb("qk_bias", [3 * D, 2 * HEADS], F32, l0),
                "vbias": sb("vbias", [128, QT, HEADS, D], F32, l0),
                "proj_w": sb("proj_w", [128, C], F32, l0),
                "proj_b": sb("proj_bias", [128, 1], F32, l0),
                "t_edge": sb("t_edge", [128, SB], F32, l0),
                "gidx": sb("gidx", [128, 16], U32, l0),
                "gval": sb("gval", [128, 16], F32, l0),
            })
            with ExitStack() as c:
                constants_and_norm(nc, c, t, a)
            with ExitStack() as c:
                attention_half(nc, c, t, 0, scatter_lists(nc, c, t, table))
            with ExitStack() as c:
                last_edges(nc, c, t, a, table, scratch_m)
            with ExitStack() as c:
                attention_half(nc, c, t, 1, gather_values(nc, c, t, a, scratch_v))
        with ExitStack() as l1:
            TT = N // 128
            t.update({
                "w1": sb("l1_qkv_w", [128, 3 * C], F32, l1), "b1": sb("l1_qk_b", [128, 2], F32, l1),
                "bv1": sb("l1_v_b", [128, D], F32, l1),
                "pw1": sb("l1_proj_w", [128, C], F32, l1), "pb1": sb("l1_proj_b", [128, 1], F32, l1),
                "rw": sb("router_w", [128, EXPERTS], F32, l1), "rb": sb("router_b", [128, QT, EXPERTS], F32, l1),
                "ew": sb("expert_w", [128, EXPERTS, C], F32, l1), "eb": sb("expert_b", [EXPERTS, C], F32, l1),
                "avg": sb("avg", [128, C], F32, l1), "eps": sb("token_eps", [128, 1], F32, l1),
                "iota8": sb("iota8", [128, EXPERTS], F32, l1),
                "kexp": sb("k_diag", [128, 2, NBLK, HEADS, BS], F32, l1),
                "vexp": sb("v_diag", [128, 2, NBLK, C], F32, l1),
                "bias": sb("slot_bias", [128, TT, BS], F32, l1),
                "gate": sb("slot_gate", [128, TT, HEADS, BS], F32, l1),
            })
            with ExitStack() as c:
                layer1_constants(nc, c, t, a, scratch_v, scratch_m)
            with ExitStack() as c:
                block_attention(nc, c, t)
            if dbg is None:
                with ExitStack() as c:
                    experts(nc, c, t, out)
        if dbg is not None:
            with ExitStack() as c:
                done = c.enter_context(nc.semaphore("dbg"))
                blk = c.enter_context(nc.Block())

                @blk.sync
                def _(sp):
                    for b in range(B):
                        sp.dma_start(dbg[b], t["x_all"][:, b * N:(b + 1) * N]).then_inc(done, 16)
                    sp.wait_ge(done, B * 16)


_INPUTS = {
    "x": ("x", lambda v: v.reshape(B, C, N)),
    "norm_w": ("L0_conv_norm_w", None), "norm_b": ("L0_conv_norm_b", None),
    "qkv_wT": ("L0_conv_qkv_w", lambda v: v.T), "qkv_b": ("L0_conv_qkv_b", None),
    "proj_wT": ("L0_conv_proj_w", lambda v: v.T), "proj_b": ("L0_conv_proj_b", None),
    "edges": ("L1_attn_edge_index", None), "edge_values": ("L1_attn_edge_values", None),
    "qkv1_w": ("L1_attn_qkv_w", None), "qkv1_b": ("L1_attn_qkv_b", None),
    "proj1_w": ("L1_attn_proj_w", None), "proj1_b": ("L1_attn_proj_b", None),
    "gate_w": ("L1_attn_gate_w", None), "gate_b": ("L1_attn_gate_b", None),
    "router_w": ("L1_ffn_router_w", None), "router_b": ("L1_ffn_router_b", None),
    "expert_w": ("L1_ffn_expert_w", None), "expert_b": ("L1_ffn_expert_b", None),
}


def kernel(**inputs):
    import numpy as np
    import concourse.bacc as bacc
    from concourse.bass_utils import run_bass_kernel_spmd

    nc = bacc.Bacc("TRN2", target_bir_lowering=False, num_devices=1)
    arrays, a = {}, {}
    for name, (source, lay) in _INPUTS.items():
        v = np.asarray(inputs[source])
        v = np.ascontiguousarray(lay(v) if lay else v)
        arrays[f"in_{name}"] = v
        a[name] = nc.dram_tensor(f"in_{name}", v.shape, mybir.dt.from_np(v.dtype), kind="ExternalInput").ap()
    out = nc.dram_tensor("out_0", (B, C, N), F32, kind="ExternalOutput").ap()
    build(nc, a, out)
    r = run_bass_kernel_spmd(nc, [arrays], core_ids=[0])
    return r.results[0]["out_0"].reshape(B, C, 64, 64)
```

```python
from contextlib import ExitStack

import concourse.bass as bass
from concourse import mybir

F32 = mybir.dt.float32
F16 = mybir.dt.float16
I32 = mybir.dt.int32
U32 = mybir.dt.uint32
ALU = mybir.AluOpType
ACT = mybir.ActivationFunctionType
AX = mybir.AxisListType

C = 128
B = 4
N = 4096
HEADS = 4
D = C // HEADS
SCALE = float(D) ** -0.5
CH = 512
NCH = N // CH
KT = N // 128
QT = CH // 128
GN_EPS = 1e-5
GROUP = C // 8
MROW = 16.0

BS = 32
E = 4194304
EP = E // 128
SLOTS = N * BS
PIECE = 2048
RUN = 64
RUNS = EP // RUN
GRP = 512
KEEP = 80
GRPS = RUNS * 8 // GRP
LIST = GRPS * KEEP
SLOT_BITS = 17
BATCH = 8
NOWHERE = 1 << 24


class Steps:

    def __init__(self, eng, sem):
        self.eng, self.sem, self.base, self.n = eng, sem, 0, 0

    def inc(self, ins):
        self.n += 1
        return ins.then_inc(self.sem, 1)

    def sync(self):
        self.eng.wait_ge(self.sem, self.base + self.n)

    def sync_apart(self, scratch):
        self.eng.wait_ge(self.sem, self.base + self.n)
        self.eng.memset(scratch, 0.0)

    def at(self, base):
        self.base, self.n = base, 0


def attention(nc, ctx, t, img0, IMGS, pool_program, beside=None):
    x_all, qs, ks, vones, ident = t["x_all"], t["qs"], t["ks"], t["vones"], t["ident"]
    probs, o_t, mx8, mx, mrow = t["probs"], t["o_t"], t["mx8"], t["mx"], t["mrow"]
    os, dn = t["os"], t["dn"]
    xn, wqk, wv, qk_b, vbias = t["xn"], t["wqk"], t["wv"], t["qk_b"], t["vbias"]
    S, O, M = t["S"], t["O"], t["M"]

    def sem(name):
        return ctx.enter_context(nc.semaphore(f"{name}_{img0}"))

    xn_ready = sem("xn_ready")
    qk_ready = sem("qk_ready")
    high_out = sem("high_out")
    qk_taken = sem("qk_taken")
    v_ready = sem("v_ready")
    v_taken = sem("v_taken")
    s_ready = sem("s_ready")
    p_ready = sem("p_ready")
    o_added = sem("o_added")
    m_ready = sem("m_ready")
    m_taken = sem("m_taken")
    mx_final = sem("mx_final")
    mt_ready = sem("mt_ready")
    mrow_out = sem("mrow_out")
    mrow_in = sem("mrow_in")
    o_out = sem("o_out")
    dens_out = sem("dens_out")
    recip_own = sem("recip_own")
    o_taken = sem("o_taken")
    y_ready = sem("y_ready")
    y_taken = sem("y_taken")

    STEPS = KT * 2
    TILES = HEADS * QT * NCH
    QK = 2 * HEADS
    KTILES = HEADS * QT

    def tile_of(n):
        return n // (QT * NCH), (n // NCH) % QT, n % NCH

    def tiles_of_step(s):
        return range(min(TILES, s * 9 // 4), min(TILES, (s + 1) * 9 // 4))

    R0, RN = 8, 16
    T0, TN = R0 + RN, 8
    PROJ = 100
    TRANSPOSE = 60
    PW = 2 * CH // RN

    block = ctx.enter_context(nc.Block())

    LEAD = 1

    def head_turns(eng, turn, last_turn):
        turn(0, 0)
        turn(1, 1)
        with eng.Fori(1, NCH // 2) as c2:
            for j in range(2):
                turn(c2 * 2 + j, j)
        last_turn()

    @block.scalar
    def _(act):
        for x in (xn_ready, high_out, p_ready, o_out, dens_out):
            act.sem_inc(x, LEAD)

        def den(h, chunk):
            r = 64 * (h % 2)
            if h == 0:
                act.wait_ge(o_out, chunk + LEAD)
                act.wait_ge(o_taken, chunk - 1 + LEAD)
            last = act.activation(dn[r:r + D, h // 2, :], os[r + D:r + 2 * D, h // 2, :], ACT.Identity)
            if h == HEADS - 1:
                last.then_inc(dens_out, 1)

        with act.Fori(0, IMGS) as img:
            b = img + img0

            def turn(c, j):
                act.wait_ge(v_ready, img * NCH + (c - 1 + LEAD) if not isinstance(c, int) or c > 0
                            else img * NCH + LEAD)
                act.activation(xn[:, j, :], x_all[:, bass.ds(b * N + c * CH, CH)], ACT.Identity,
                               scale=t["gn_a"][:, bass.ds(b, 1)], bias=t["gn_b"][:, bass.ds(b, 1)]) \
                   .then_inc(xn_ready, 1)
                for i in range(QK):
                    h, m = i // 2, i % 2
                    act.wait_ge(qk_ready, (img * NCH + c) * QK + (i + 1 + LEAD))
                    dst = (qs[0:96, bass.ds(c * (HEADS * CH) + h * CH, CH)], ks[0:96, h, bass.ds(c * CH, CH)])[m]
                    act.activation(dst, S[0:96, i % 4 // 2, (i % 2) * CH:(i % 2 + 1) * CH], ACT.Identity,
                                   bias=qk_b[:, m * HEADS + h:m * HEADS + h + 1]).then_inc(high_out, 1)
            head_turns(act, turn, lambda: None)

            def chunk_turn(c, first):
                chunk = img * NCH + c
                turn = chunk * STEPS
                for s in range(STEPS):
                    act.wait_ge(s_ready, turn + (s + 1 + LEAD))
                    if s >= 3:
                        act.wait_ge(o_added, turn + (s - 2 + LEAD))
                    act.activation(probs[:, s % 3, :], S[:, s % 2, :], ACT.Exp, scale=SCALE) \
                       .then_inc(p_ready, 1)
                    if not first and 1 <= s < 1 + HEADS:
                        den(s - 1, chunk)
                act.wait_ge(o_added, turn + (STEPS + LEAD))
                act.wait_ge(o_taken, chunk + LEAD)
                act.activation(os[:, :, :], O[:, :, :], ACT.Identity).then_inc(o_out, 1)
            chunk_turn(0, True)
            with act.Fori(1, NCH) as c:
                chunk_turn(c, False)
            for h in range(HEADS):
                den(h, (img + 1) * NCH)

    @block.tensor
    def _(pe):
        for x in (qk_ready, v_ready, s_ready, o_added, m_ready, mt_ready, y_ready):
            pe.sem_inc(x, LEAD)

        def max_tile(n, h, qt, q_at, keys):
            pe.matmul(M[:, n % 2, :], qs[0:96, bass.ds(q_at + (h * CH + qt * 128), 128)],
                      ks[0:96, h, keys], start=True, stop=True).then_inc(m_ready, 1)

        def transpose_maxima(count):
            pe.wait_ge(mx_final, count + LEAD)
            pe.matmul(M[0:HEADS * QT, 0, 0:128], mx[:, :], ident[:, :], start=True, stop=True) \
              .then_inc(mt_ready, 1)

        def project(chunks):
            pe.wait_ge(o_taken, chunks + LEAD)
            pe.matmul(M[:, 0, :], t["proj_w"][:, :], o_t[:, :], start=True, stop=True).then_inc(y_ready, 1)

        with pe.Fori(0, IMGS) as img:
            mturn = img * (NCH * TILES)

            def key_tiles(kc, i):
                for n in (2 * i, 2 * i + 1):
                    if not (isinstance(kc, int) and kc == 0 and n < 2):
                        pe.wait_ge(m_taken, mturn + kc * KTILES + (n - 1 + LEAD))
                    max_tile(n, n // QT, n % QT, 0, bass.ds(kc * CH, CH))

            def turn(c, j):
                first = isinstance(c, int) and c == 0
                pe.wait_ge(xn_ready, img * NCH + c + (1 + LEAD))
                for i in range(QK):
                    h, m = i // 2, i % 2
                    if not first or i >= 4:
                        pe.wait_ge(qk_taken, (img * NCH + c) * QK + (i - 3 + LEAD))
                    elif i == 0:
                        pe.wait_ge(p_ready, img * (NCH * STEPS) + LEAD)
                    pe.matmul(S[0:96, i % 4 // 2, (i % 2) * CH:(i % 2 + 1) * CH], wqk[:, m * HEADS + h, :],
                              xn[:, j, :], start=True, stop=True).then_inc(qk_ready, 1)
                    if not first:
                        if i == 0:
                            pe.wait_ge(qk_taken, (img * NCH + c) * QK + LEAD)
                        key_tiles(c - 1, i)
                if first:
                    pe.wait_ge(o_out, img * NCH + LEAD)
                pe.wait_ge(v_taken, img * NCH + c + LEAD)
                for k in range(QT):
                    last = pe.matmul(O[:, 0, k * C:(k + 1) * C], xn[:, j, k * 128:(k + 1) * 128],
                                     wv[:, :], start=True, stop=True)
                last.then_inc(v_ready, 1)
                if first:
                    pe.wait_ge(y_taken, img * NCH + LEAD)

            def last_turn():
                pe.wait_ge(qk_taken, (img + 1) * (NCH * QK) + LEAD)
                for i in range(QK):
                    key_tiles(NCH - 1, i)
                transpose_maxima(img * NCH + 1)
            head_turns(pe, turn, last_turn)

            def chunk_turn(c, first, last_chunk):
                chunk = img * NCH + c
                turn = chunk * STEPS
                mturn = (chunk + 1) * TILES
                q_at = c * (HEADS * CH)
                pe.wait_ge(mrow_in, (chunk + 1) * 16 + LEAD)
                def score_tile(n):
                    if n == 0 and not last_chunk:
                        pe.wait_ge(mrow_out, chunk + (1 + LEAD))
                    if n >= 2 and not last_chunk:
                        pe.wait_ge(m_taken, mturn + (n - 1 + LEAD))
                    if n == PROJ and not first:
                        project(chunk)
                        if not last_chunk:
                            pe.wait_ge(y_taken, chunk + LEAD)
                    if not last_chunk:
                        h, qt, kc = tile_of(n)
                        max_tile(n, h, qt, (c + 1) * (HEADS * CH), slice(kc * CH, (kc + 1) * CH))

                for s in range(STEPS + 1):
                    kt, hp = s // 2, s % 2
                    tiles = list(tiles_of_step(s)) if s < STEPS else []
                    if s < STEPS:
                        pe.wait_ge(p_ready, turn + (max(s - 1, 0) + LEAD))
                        for h in (2 * hp, 2 * hp + 1):
                            last = pe.matmul(S[:, s % 2, (h % 2) * CH:(h % 2 + 1) * CH],
                                             ks[0:97, h, kt * 128:(kt + 1) * 128],
                                             qs[0:97, bass.ds(q_at + h * CH, CH)], start=True, stop=True)
                            if h % 2 == 0 and len(tiles) > 2:
                                score_tile(tiles.pop(0))
                        last.then_inc(s_ready, 1)
                        if tiles:
                            score_tile(tiles.pop(0))
                        if s == TRANSPOSE and not last_chunk:
                            transpose_maxima(chunk + 2)
                    if s >= 1:
                        pt, ph = (s - 1) // 2, (s - 1) % 2
                        if s == 1:
                            pe.wait_ge(o_out, chunk + LEAD)
                        pe.wait_ge(p_ready, turn + (s + LEAD))
                        for j in range(2):
                            last = pe.matmul(O[64 * j:64 * j + 64, ph, :], vones[:, pt, 2 * ph + j, :],
                                             probs[:, (s - 1) % 3, j * CH:(j + 1) * CH],
                                             start=(pt == 0), stop=(pt == KT - 1))
                        last.then_inc(o_added, 1)
                    for n in tiles:
                        score_tile(n)
            chunk_turn(0, True, False)
            with pe.Fori(1, NCH - 1) as c:
                chunk_turn(c, False, False)
            chunk_turn(NCH - 1, False, True)
            pe.wait_ge(y_taken, (img + 1) * NCH - 1 + LEAD)
            project((img + 1) * NCH)

    @block.vector
    def _(dve):
        for x in (qk_taken, v_taken, m_taken, mx_final, mrow_out, o_taken, y_taken, recip_own):
            dve.sem_inc(x, LEAD)

        def maxima(mturn, n, row, kc):
            dve.wait_ge(m_ready, mturn + (n + 1 + LEAD))
            dve.reduce_max(mx8[:, row, bass.ds(kc, 1)], M[:, n % 2, :], AX.X).then_inc(m_taken, 1)

        def finish_maxima(count):
            dve.wait_ge(m_taken, count * TILES + LEAD)
            dve.reduce_max(mx[:, :], mx8[:, :, :], AX.X).then_inc(mx_final, 1)
            dve.wait_ge(mt_ready, count + LEAD)
            dve.wait_ge(mrow_in, (count - 1) * 16 + LEAD)
            dve.tensor_scalar(mrow[:, :], M[0:HEADS * QT, 0, 0:128], -1.0 / MROW, None, ALU.mult) \
               .then_inc(mrow_out, 1)

        def reciprocals(n, chunks):
            if n == 0:
                dve.wait_ge(dens_out, chunks + LEAD)
            hp, at = n * PW // CH, n * PW % CH
            last = dve.reciprocal(dn[0:64 + D, hp, at:at + PW], dn[0:64 + D, hp, at:at + PW])
            if n == RN - 1:
                last.then_inc(recip_own, 1)

        def normalise(n, chunks):
            if n == 0:
                dve.wait_ge(recip_own, chunks + LEAD)
                dve.wait_ge(y_ready, chunks - 1 + LEAD)
            h, at = n // 2, n % 2 * (CH // 2)
            r = 64 * (h % 2)
            last = dve.tensor_tensor(o_t[h * D:(h + 1) * D, at:at + CH // 2],
                                     os[r:r + D, h // 2, at:at + CH // 2],
                                     dn[r:r + D, h // 2, at:at + CH // 2], ALU.mult)
            if n == TN - 1:
                last.then_inc(o_taken, 1)

        def residual(chunks, col):
            dve.wait_ge(y_ready, chunks + LEAD)
            x_now = x_all[:, bass.ds(col, CH)]
            dve.scalar_tensor_tensor(x_now, M[:, 0, :], t["proj_b"][:, 0:1], x_now,
                                     ALU.add, ALU.add).then_inc(y_taken, 1)

        dve.memset(dn[:, :, :], 1.0)
        with dve.Fori(0, IMGS) as img:
            mturn = img * (NCH * TILES)

            def key_maxima(kc, i):
                for n in (2 * i, 2 * i + 1):
                    maxima(mturn + kc * KTILES, n, n, kc)

            def turn(c, j):
                first = isinstance(c, int) and c == 0
                for i in range(QK):
                    h, m = i // 2, i % 2
                    dve.wait_ge(high_out, (img * NCH + c) * QK + (i + 1 + LEAD))
                    r = slice(2 * D, 3 * D) if m == 0 else slice(D, 2 * D)
                    low = (qs[r, bass.ds(c * (HEADS * CH) + h * CH, CH)], ks[r, h, bass.ds(c * CH, CH)])[m]
                    dve.scalar_tensor_tensor(low, S[r, i % 4 // 2, (i % 2) * CH:(i % 2 + 1) * CH],
                                             qk_b[r, m * HEADS + h:m * HEADS + h + 1], low,
                                             ALU.add, ALU.subtract).then_inc(qk_taken, 1)
                    if not first:
                        key_maxima(c - 1, i)
                dve.wait_ge(v_ready, img * NCH + c + (1 + LEAD))
                dve.tensor_tensor(vones[:, bass.ds(c * QT, QT), :, 0:D],
                                  O[:, 0, :].rearrange("p (k h d) -> p k h d", k=QT, h=HEADS),
                                  vbias[:, :, :, :], ALU.add).then_inc(v_taken, 1)

            def last_turn():
                for i in range(QK):
                    key_maxima(NCH - 1, i)
                finish_maxima(img * NCH + 1)
            head_turns(dve, turn, last_turn)
            col = (img + img0) * N

            def chunk_turn(c, first, last_chunk):
                chunk = img * NCH + c
                mturn = (chunk + 1) * TILES
                for s in range(STEPS):
                    if not first:
                        if R0 <= s < R0 + RN:
                            reciprocals(s - R0, chunk)
                        if T0 <= s < T0 + TN:
                            normalise(s - T0, chunk)
                    for n in tiles_of_step(s):
                        if n == PROJ and not first:
                            residual(chunk, col + (c - 1) * CH)
                        if not last_chunk:
                            h, qt, kc = tile_of(n)
                            maxima(mturn, n, h * QT + qt, kc)
                            if n == TILES - 1:
                                finish_maxima(chunk + 2)
                    if beside:
                        beside.dve(dve, c, s, first, last_chunk)
            chunk_turn(0, True, False)
            with dve.Fori(1, NCH - 1) as c:
                chunk_turn(c, False, False)
            chunk_turn(NCH - 1, False, True)
            last_chunk = (img + 1) * NCH
            for n in range(RN):
                reciprocals(n, last_chunk)
            for n in range(TN):
                normalise(n, last_chunk)
            residual(last_chunk, col + (NCH - 1) * CH)

    @block.sync
    def _(sp):
        sp.sem_inc(mrow_in, LEAD)
        with sp.Fori(0, IMGS) as img:
            with sp.Fori(0, NCH) as c:
                sp.wait_ge(mrow_out, img * NCH + c + (1 + LEAD))
                sp.dma_start(qs[96:97, bass.ds(c * (HEADS * CH), HEADS * CH)]
                             .rearrange("p (r q) -> p r q", q=128), mrow[:, :]).then_inc(mrow_in, 16)
        sp.wait_ge(mrow_in, IMGS * NCH * 16 + LEAD)

    @block.gpsimd
    def _(pool):
        pool_program(pool)


def constants_and_norm(nc, ctx, t, a):
    x_all = t["x_all"]

    def sem(name):
        return ctx.enter_context(nc.semaphore(name))

    def sb(name, shape, dt=F32):
        return ctx.enter_context(nc.sbuf_tensor(name, shape, dt))

    w_loaded, made = sem("w_loaded"), sem("constants_made")
    own_sem, gsum, rooted, ident_made = sem("norm_own"), sem("group_sums"), sem("rooted"), sem("ident_made")
    NST = N // 512
    stats = sb("stats", [128, B, NST, 6])
    mv = sb("mv", [128, B, 2])
    gmat = sb("gmat", [128, C])
    var = sb("gvar", [128, B])
    std = sb("gstd", [128, B])
    tmp = sb("gtmp", [128, B])
    normw = sb("normw", [128, 2])
    eps = sb("eps", [128, 1])
    G = t["M"]
    block = ctx.enter_context(nc.Block())
    W_LOADS = 3 * 2 + 1 + QT + 4

    @block.scalar
    def _(act):
        for r in range(3):
            rows = slice(r * D, (r + 1) * D)
            act.dma_start(t["wqk"][:, :, rows], a["qkv_wT"][:, 0:2 * C].rearrange("i (g d) -> i g d", d=D)) \
               .then_inc(w_loaded, 16)
            act.dma_start(t["qk_b"][rows, :], a["qkv_b"][0:2 * C].rearrange("(g d) -> d g", d=D),
                          allow_slow_non_contiguous=True) \
               .then_inc(w_loaded, 16)
        act.dma_start(t["wv"][:, :], a["qkv_wT"][:, 2 * C:3 * C]).then_inc(w_loaded, 16)
        for k in range(QT):
            act.dma_start(t["vbias"][:, k, :, :],
                          a["qkv_b"][2 * C:3 * C].rearrange("(o h d) -> o h d", o=1, h=HEADS)
                          .broadcast_to([128, HEADS, D])).then_inc(w_loaded, 16)
        act.dma_start(t["proj_w"][:, :], a["proj_wT"]).then_inc(w_loaded, 16)
        act.dma_start(t["proj_b"][:, 0:1], a["proj_b"].rearrange("(p o) -> p o", o=1)).then_inc(w_loaded, 16)
        act.dma_start(normw[:, 0:1], a["norm_w"].rearrange("(p o) -> p o", o=1)).then_inc(w_loaded, 16)
        act.dma_start(normw[:, 1:2], a["norm_b"].rearrange("(p o) -> p o", o=1)).then_inc(w_loaded, 16)
        act.wait_ge(own_sem, 2 * B + 3)
        act.activation(std[:, :], var[:, :], ACT.Sqrt, bias=eps[:, 0:1]).then_inc(rooted, 1)
        act.wait_ge(w_loaded, W_LOADS * 16)

    @block.gpsimd
    def _(pool):
        pool.memset(t["ident"][:, :], 0.0).then_inc(ident_made, 1)
        pool.memset(eps[:, :], GN_EPS).then_inc(made, 1)
        pool.memset(gmat[:, :], 1.0 / GROUP).then_inc(ident_made, 1)
        pool.wait_ge(ident_made, 2)
        pool.affine_select(out=t["ident"][:, :], in_=t["ident"][:, :], compare_op=ALU.not_equal, fill=1.0,
                           base=0, pattern=[[-1, 128]], channel_multiplier=1).then_inc(ident_made, 1)
        g3 = gmat[:, :].rearrange("p (g c) -> p g c", c=GROUP)
        pool.affine_select(out=g3, in_=g3, compare_op=ALU.is_ge, fill=0.0, base=0,
                           pattern=[[-GROUP, C // GROUP], [0, GROUP]], channel_multiplier=1).then_inc(ident_made, 1)
        pool.wait_ge(ident_made, 4)
        pool.affine_select(out=g3, in_=g3, compare_op=ALU.is_ge, fill=0.0, base=GROUP - 1,
                           pattern=[[GROUP, C // GROUP], [0, GROUP]], channel_multiplier=-1).then_inc(made, 1)
        pool.memset(t["vones"][:, :, :, D:2 * D], 1.0).then_inc(ident_made, 1)
        pool.wait_ge(ident_made, 5)
        pool.memset(t["ks"][96:97, :, :], MROW)

    @block.vector
    def _(dve):
        own = Steps(dve, own_sem)
        for b in range(B):
            for k in range(NST):
                last = dve.bn_stats(stats[:, b, k, :], x_all[:, b * N + k * 512:b * N + (k + 1) * 512])
            own.inc(last)
            own.sync()
            own.inc(dve.bn_aggr(mv[:, b, :], stats[:, b, :, :]))
        own.sync()
        own.inc(dve.tensor_tensor(tmp[:, :], mv[:, :, 0], mv[:, :, 0], ALU.mult))
        own.sync()
        own.inc(dve.tensor_tensor(mv[:, :, 1], mv[:, :, 1], tmp[:, :], ALU.add))
        dve.wait_ge(gsum, 1)
        own.sync()
        dve.tensor_copy(mv[:, :, :], G[:, 0, 0:2 * B].rearrange("p (b k) -> p b k", k=2)).then_inc(gsum, 1)
        dve.wait_ge(gsum, 2)
        dve.tensor_tensor(tmp[:, :], mv[:, :, 0], mv[:, :, 0], ALU.mult).then_inc(gsum, 1)
        dve.wait_ge(gsum, 3)
        own.inc(dve.tensor_tensor(var[:, :], mv[:, :, 1], tmp[:, :], ALU.subtract))
        dve.wait_ge(rooted, 1)
        own.inc(dve.reciprocal(std[:, :], std[:, :]))
        own.sync()
        dve.wait_ge(w_loaded, W_LOADS * 16)
        own.inc(dve.tensor_scalar(t["gn_a"][:, :], std[:, :], normw[:, 0:1], None, ALU.mult))
        own.sync()
        own.inc(dve.tensor_tensor(tmp[:, :], mv[:, :, 0], t["gn_a"][:, :], ALU.mult))
        own.sync()
        own.inc(dve.tensor_scalar(t["gn_b"][:, :], tmp[:, :], -1.0, normw[:, 1:2], ALU.mult, ALU.add))

    @block.tensor
    def _(pe):
        pe.wait_ge(made, 2)
        pe.wait_ge(own_sem, 2 * B + 2)
        pe.matmul(G[:, 0, 0:2 * B], gmat[:, :], mv[:, :, :].rearrange("p b k -> p (b k)"),
                  start=True, stop=True).then_inc(gsum, 1)


def slots_of(dve, own, rows, cols, work):
    w0, w1 = work
    own.inc(dve.tensor_scalar(w1, rows, ~(N - 1), None, ALU.bitwise_and))
    own.inc(dve.tensor_tensor(w0, rows, cols, ALU.bitwise_xor))
    own.sync()
    own.inc(dve.scalar_tensor_tensor(w0, w0, ~(BS - 1), w1, ALU.bitwise_and, ALU.bitwise_or))
    own.sync()
    own.inc(dve.tensor_scalar(w1, cols, BS - 1, None, ALU.bitwise_and))
    own.sync()
    own.inc(dve.scalar_tensor_tensor(w1, rows, 5, w1, ALU.logical_shift_left, ALU.bitwise_or))
    own.sync()


def scatter_index(dve, own, xs, pcol, idx, dup, eq, n):
    own.inc(dve.memset(dup, 0.0))
    own.sync()
    x3 = xs.rearrange("p (n k) -> p n k", k=BATCH)
    d3 = dup.rearrange("p (n k) -> p n k", k=BATCH)
    e3 = eq.rearrange("p (n k) -> p n k", k=BATCH)
    for sft in range(1, BATCH):
        own.inc(dve.tensor_tensor(e3[:, :, 0:BATCH - sft], x3[:, :, 0:BATCH - sft], x3[:, :, sft:BATCH],
                                  ALU.is_equal))
        own.sync()
        own.inc(dve.tensor_tensor(d3[:, :, 0:BATCH - sft], d3[:, :, 0:BATCH - sft],
                                  e3[:, :, 0:BATCH - sft], ALU.max))
        own.sync()
    own.inc(dve.tensor_scalar(eq, xs, float(1 << SLOT_BITS), None, ALU.is_ge))
    own.sync()
    own.inc(dve.tensor_tensor(dup, dup, eq, ALU.max))
    own.inc(dve.tensor_scalar(idx, xs, SLOTS - 1, 7, ALU.bitwise_and, ALU.logical_shift_left))
    own.sync()
    own.inc(dve.tensor_tensor(idx, idx, pcol.to_broadcast([128, n]), ALU.bitwise_or))
    own.sync()
    own.inc(dve.scalar_tensor_tensor(idx, dup, 24, idx, ALU.logical_shift_left, ALU.bitwise_or))
    own.sync()


def edge_lists(nc, ctx, t, a, table):
    def sem(name):
        return ctx.enter_context(nc.semaphore(name))

    def sb(name, shape, dt=F32):
        return ctx.enter_context(nc.sbuf_tensor(name, shape, dt))

    PIECES = EP // PIECE
    GRP_EDGES = GRP // 8 * RUN
    PLACED = 2.0 ** -63
    assert GRP_EDGES == 2 * PIECE == 4096 and GRP_EDGES << SLOT_BITS == 1 << 29
    loaded = [sem(f"edges_loaded_{j}") for j in range(2)]
    made, taken, own_sem, cleared, zeroed, x_loaded = (sem(n) for n in
        ("edge_consts", "piece_taken", "edge_own", "table_cleared", "zero_made", "x_loaded"))
    rc = sb("edge_rc", [128, 2, 2, PIECE], I32)
    base = sb("edge_base", [128, 2, PIECE], I32)
    w0, w1 = sb("edge_w0", [128, PIECE], I32), sb("edge_w1", [128, PIECE], I32)
    key = sb("edge_key", [128, PIECE])
    top = sb("edge_top", [128, PIECE // RUN * 8])
    k1 = sb("edge_k1", [128, RUNS * 8])
    group = sb("edge_group", [128, GRP])
    latest = sb("edge_latest", [128, KEEP])
    keys = sb("list_keys", [128, LIST])
    li = [sb(f"list_i{n}", [128, LIST], I32) for n in range(5)]
    ebase = sb("list_ebase", [128, GRPS, KEEP])
    zero = sb("edge_zero", [128, 4096])
    row_max = sb("ovf_max", [128, 2])
    gate = sb("edge_gate", [128, 1])
    block = ctx.enter_context(nc.Block())
    CLEARS = 32
    ZEROS = SLOTS // CLEARS
    LEAD = 2

    @block.sync
    def _(sp):
        with sp.Fori(0, PIECES // 2) as q:
            for j in range(2):
                sp.wait_ge(taken, q * 2 + (j - 1 + LEAD))
                for m in range(2):
                    sp.dma_start(rc[:, j, m, :], a["edges"][m].rearrange("(p e) -> p e", p=128)
                                 [:, bass.ds(q * (2 * PIECE) + j * PIECE, PIECE)]).then_inc(loaded[j], 16)
        for b in range(B):
            sp.dma_start(t["x_all"][:, b * N:(b + 1) * N], a["x"][b]).then_inc(x_loaded, 16)
        sp.wait_ge(x_loaded, B * 16)
        sp.wait_ge(cleared, CLEARS * 16)

    @block.scalar
    def _(act):
        act.wait_ge(zeroed, 1)
        with act.Fori(0, PIECES) as q:
            act.wait_ge(taken, q + LEAD)
            for z in range(CLEARS // PIECES):
                act.dma_start(table[bass.ds(q * (CLEARS // PIECES * ZEROS) + z * ZEROS, ZEROS), :]
                              .rearrange("(p r) c -> p (r c)", p=128), zero[:, :]).then_inc(cleared, 16)

    @block.gpsimd
    def _(pool):
        pool.memset(zero[:, :], 0.0).then_inc(zeroed, 1)
        pool.iota(base[:, :, :], pattern=[[-PIECE, 2], [-1, PIECE]], base=2 * GRP_EDGES - 1, channel_multiplier=0) \
            .then_inc(made, 1)
        pool.iota(t["pcol"][:, :], pattern=[[0, 1]], base=0, channel_multiplier=1).then_inc(made, 1)
        pool.iota(ebase[:, :, :], pattern=[[GRP_EDGES, GRPS], [0, KEEP]], base=GRP_EDGES,
                  channel_multiplier=EP, allow_small_or_imprecise_dtypes=True).then_inc(made, 1)

    @block.vector
    def _(dve):
        own = Steps(dve, own_sem)
        dve.sem_inc(taken, LEAD)
        dve.wait_ge(made, 3)
        own.inc(dve.tensor_scalar(base[:, :, :], base[:, :, :], SLOT_BITS, None, ALU.logical_shift_left))
        own.sync()
        OWN_PIECE = 6
        start = own.n
        with dve.Fori(0, PIECES // 2) as q:
            for j in range(2):
                own.at(q * (2 * OWN_PIECE) + (start + j * OWN_PIECE))
                dve.wait_ge(loaded[j], q * 32 + 32)
                rows, cols = rc[:, j, 0, :], rc[:, j, 1, :]
                own.inc(dve.tensor_tensor(w0[:, :], rows, cols, ALU.bitwise_xor))
                own.sync()
                own.inc(dve.scalar_tensor_tensor(w1[:, :], rows, ~(N - 1), w0[:, :], ALU.bitwise_and, ALU.bitwise_or))
                own.inc(dve.scalar_tensor_tensor(w0[:, :], rows, 5, w0[:, :], ALU.logical_shift_left, ALU.bitwise_or))
                own.sync()
                own.inc(dve.scalar_tensor_tensor(w1[:, :], w1[:, :], float(BS), base[:, j, :], ALU.is_lt, ALU.mult))
                own.sync()
                own.inc(dve.tensor_tensor(key[:, :].bitcast(I32), w0[:, :], w1[:, :], ALU.bitwise_or))
                own.sync_apart(gate[:, 0:1])
                for r in range(PIECE // RUN):
                    last = dve.max(top[:, r * 8:(r + 1) * 8], key[:, r * RUN:(r + 1) * RUN])
                own.inc(last)
                own.sync()
                dve.scalar_tensor_tensor(
                    k1[:, bass.ds(q * (2 * PIECE // RUN * 8) + j * (PIECE // RUN * 8), PIECE // RUN * 8)],
                    top[:, :], PLACED, top[:, :], ALU.is_ge, ALU.mult).then_inc(taken, 1)
                assert own.n == OWN_PIECE
        dve.wait_ge(taken, PIECES + LEAD)
        own.at(PIECES * OWN_PIECE + start)
        own.inc(dve.reduce_max(row_max[:, 0:1], k1[:, 7::8], AX.X))
        start = PIECES * OWN_PIECE + start + 1
        OWN_GRP = 1 + 2 * (KEEP // 8)
        with dve.Fori(0, GRPS) as g:
            own.at(g * OWN_GRP + start)
            own.inc(dve.tensor_copy(group[:, :], k1[:, bass.ds(g * GRP, GRP)]))
            own.sync_apart(gate[:, 0:1])
            for r in range(KEEP // 8):
                own.inc(dve.max(latest[:, r * 8:(r + 1) * 8], group[:, :]))
                own.sync_apart(gate[:, 0:1])
                own.inc(dve.match_replace(group[:, :], latest[:, r * 8:(r + 1) * 8], group[:, :], 0.0))
                own.sync_apart(gate[:, 0:1])
            assert own.n == OWN_GRP
            dve.tensor_copy(keys[:, bass.ds(g * KEEP, KEEP)], latest[:, :]).then_inc(taken, 1)
        own.at(GRPS * OWN_GRP + start)
        dve.wait_ge(taken, PIECES + GRPS + LEAD)
        place, slot, none, row = (li[n][:, :] for n in range(4))
        bits = keys[:, :].bitcast(I32)
        own.inc(dve.reduce_max(row_max[:, 1:2], keys[:, KEEP - 1::KEEP], AX.X))
        own.inc(dve.tensor_scalar(place, bits, SLOT_BITS, GRP_EDGES - 1, ALU.logical_shift_right, ALU.bitwise_and))
        own.inc(dve.tensor_scalar(slot, bits, SLOTS - 1, None, ALU.bitwise_and))
        own.inc(dve.tensor_scalar(none, keys[:, :], 0.0, float(SLOTS), ALU.is_equal, ALU.mult))
        own.inc(dve.tensor_scalar(row, bits, 5, BS - 1, ALU.logical_shift_right, ALU.bitwise_and))
        own.sync()
        own.inc(dve.tensor_tensor(slot, slot, row, ALU.bitwise_xor))
        own.sync()
        own.inc(dve.reduce_max(t["ovf"][:, 0:1], row_max[:, :], AX.X))
        own.inc(dve.tensor_tensor(t["list_e"][:, :], ebase[:, :, :].rearrange("p g k -> p (g k)"), place,
                                  ALU.subtract))
        own.inc(dve.tensor_tensor(slot, slot, none, ALU.bitwise_or))
        own.sync()
        scatter_index(dve, own, slot, t["pcol"][:, 0:1], t["list_idx"][:, :].bitcast(I32), li[3][:, :], li[4][:, :], LIST)


def scatter_batches(pool, n, idx, ev, idx8, ev8, table, landed):
    flat = table.rearrange("s (c o) -> (s c) o", o=1)
    with pool.Fori(0, n // BATCH) as r:
        pool.drain()
        pool.tensor_copy(idx8[:, :], idx[:, bass.ds(r * BATCH, BATCH)])
        pool.tensor_copy(ev8[:, :], ev[:, bass.ds(r * BATCH, BATCH)])
        pool.drain()
        for k in range(BATCH):
            pool.indirect_dma_start(flat, bass.IndirectOffsetOnAxis(ap=idx8[:, k:k + 1], axis=0),
                                    ev8[:, k:k + 1], None, bounds_check=NOWHERE - 1,
                                    oob_is_err=False).then_inc(landed, 16)
    pool.drain()


def scatter_lists(nc, ctx, t, table):
    landed = ctx.enter_context(nc.semaphore("list_landed"))
    reduced = ctx.enter_context(nc.semaphore("ovf_reduced"))

    def program(pool):
        pool.partition_all_reduce(t["ovf_all"][:, :], t["ovf"][:, :], 128, bass.bass_isa.ReduceOp.max) \
            .then_inc(reduced, 1)
        pool.wait_ge(reduced, 1)
        scatter_batches(pool, LIST, t["list_idx"], t["list_e"], t["idx8"], t["ev8"], table, landed)
        pool.wait_ge(landed, LIST * 16)
    return program


class TableMaxima:
    TS, BUFS = 4, 4
    PIECES = SLOTS // 128 // TS
    FIRST, EACH = 36, 20
    LAST = PIECES - FIRST - (NCH - 2) * EACH

    def __init__(self, nc, ctx, t, table):
        assert not (self.FIRST % self.BUFS or self.EACH % self.BUFS or self.PIECES % self.BUFS)
        self.t, self.table = t, table
        self.loaded = [ctx.enter_context(nc.semaphore(f"slots_loaded_{k}")) for k in range(self.BUFS)]
        self.reduced = ctx.enter_context(nc.semaphore("slots_reduced"))
        W, own = self.TS * 128, ctx.enter_context(nc.sbuf_tensor("slots", [128, 2, self.TS * 128], F32))
        self.piece = [t["list"][:, k * W:(k + 1) * W] for k in range(2)] + [own[:, k, :] for k in range(2)]

    def pool(self, pool):
        W = self.TS * 128
        pool.sem_inc(self.reduced, self.BUFS)
        tab = self.table.rearrange("(b s) q -> b (s q)", b=128)
        with pool.Fori(0, self.PIECES // self.BUFS) as r:
            for k in range(self.BUFS):
                pool.wait_ge(self.reduced, r * self.BUFS + (k + 1))
                pool.dma_start(self.piece[k],
                               tab[:, bass.ds(r * (self.BUFS * W) + k * W, W)]).then_inc(self.loaded[k], 16)
        for k in range(self.BUFS):
            pool.wait_ge(self.loaded[k], self.PIECES // self.BUFS * 16)

    def pieces(self, s, first, last):
        steps = 2 * KT
        if last:
            return s * self.LAST // steps
        late = 2 * max(s - (steps - 6), 0)
        return min(s, (self.FIRST if first else self.EACH) - 12) + late

    def dve(self, dve, c, s, first, last):
        base = 0 if first else (c - 1) * self.EACH + self.FIRST
        for n in range(self.pieces(s, first, last), self.pieces(s + 1, first, last)):
            k = n % self.BUFS
            turn = 0 if first else (c - 1) * (self.EACH // self.BUFS) + self.FIRST // self.BUFS
            dve.wait_ge(self.loaded[k], (turn + n // self.BUFS) * 16 + 16)
            dve.tensor_reduce(self.t["t_edge"][:, bass.ds((base + n) * self.TS, self.TS)],
                              self.piece[k].rearrange("p (s q) -> p s q", q=128), AX.X, ALU.max).then_inc(self.reduced, 1)


def last_edges(nc, ctx, t, a, table, scratch_m):
    def sem(name):
        return ctx.enter_context(nc.semaphore(name))

    loaded, made, sent, own_sem, landed, ev_made = (sem(n) for n in
        ("gen_loaded", "gen_index_made", "gen_sent", "gen_own", "gen_landed", "gen_ev_made"))
    t_loaded = [sem(f"table_loaded_{j}") for j in range(2)]
    reduced, masked, stored = sem("table_reduced"), sem("mask_made"), sem("mask_stored")
    GP = 512
    PIECES = EP // GP
    pool_of_space = t["qs"][:, :].bitcast(I32)
    rows, cols, w0, w1, idx, dup, eq, ev = (pool_of_space[:, n * GP:(n + 1) * GP] for n in range(8))
    ev = ev.bitcast(F32)
    mask = pool_of_space[:, 0:SLOTS // 128].bitcast(F32)
    TS = 16
    TP = (SLOTS // 128) // TS
    LEAD = 2
    piece = pool_of_space[:, 8 * GP:8 * GP + 2 * TS * 128].bitcast(F32).rearrange("p (j s q) -> p j s q", j=2, q=128)
    block = ctx.enter_context(nc.Block())

    @block.sync
    def _(sp):
        full = sp.value_load(t["ovf_all"][0:1, 0:1].bitcast(I32), min_val=0, max_val=(1 << 31) - 1)
        with sp.If(full > 0):
            with sp.Fori(0, PIECES) as q:
                sp.wait_ge(made, q + LEAD)
                for m, dst in ((0, rows), (1, cols)):
                    sp.dma_start(dst, a["edges"][m].rearrange("(p e) -> p e", p=128)[:, bass.ds(q * GP, GP)]) \
                      .then_inc(loaded, 16)
            sp.wait_ge(sent, PIECES + LEAD)
            tab = table.rearrange("(b s) q -> b (s q)", b=128)
            with sp.Fori(0, TP // 2) as q:
                for j in range(2):
                    sp.wait_ge(reduced, q * 2 + (j - 1 + LEAD))
                    sp.dma_start(piece[:, j, :, :].rearrange("p s q -> p (s q)"),
                                 tab[:, bass.ds(q * (2 * TS * 128) + j * (TS * 128), TS * 128)]).then_inc(t_loaded[j], 16)
        sp.wait_ge(masked, 1)
        sp.dma_start(scratch_m, mask).then_inc(stored, 16)
        sp.wait_ge(stored, 16)

    @block.gpsimd
    def _(pool):
        pool.sem_inc(sent, LEAD)
        full = pool.value_load(t["ovf_all"][0:1, 0:1].bitcast(I32), min_val=0, max_val=(1 << 31) - 1)
        with pool.If(full > 0):
            pool.iota(ev, pattern=[[1, GP]], base=1 - GP, channel_multiplier=EP,
                      allow_small_or_imprecise_dtypes=True).then_inc(ev_made, 1)
            with pool.Fori(0, PIECES) as q:
                pool.wait_ge(made, q + (1 + LEAD))
                pool.tensor_tensor(t["ev8"][:, :], t["ev8"][:, :], t["ev8"][:, :], ALU.add)
                scatter_batches(pool, GP, idx.bitcast(U32), ev, t["idx8"], t["ev8"], table, landed)
                pool.wait_ge(landed, GP * 16)
                pool.inc_swdge_sem([landed], [GP * 16], mode="sub")
                pool.memset(t["ev8"][:, 0:1], 0.0).then_inc(sent, 1)

    @block.vector
    def _(dve):
        own = Steps(dve, own_sem)
        for x in (made, reduced):
            dve.sem_inc(x, LEAD)
        full = dve.value_load(t["ovf_all"][0:1, 0:1].bitcast(I32), min_val=0, max_val=(1 << 31) - 1)
        with dve.If(full > 0):
            dve.wait_ge(ev_made, 1)
            OWN = 5 + 3 + 1 + 2 * (BATCH - 1) + 5 + 1 - 1
            with dve.Fori(0, PIECES) as q:
                own.at(q * OWN)
                dve.wait_ge(sent, q + LEAD)
                dve.wait_ge(loaded, q * 32 + 32)
                slots_of(dve, own, rows, cols, (w0, w1))
                own.inc(dve.tensor_scalar(w0, w0, 0.0, float(SLOTS), ALU.not_equal, ALU.mult))
                own.inc(dve.tensor_scalar(w1, w1, SLOTS - 1, None, ALU.bitwise_and))
                own.sync()
                own.inc(dve.tensor_tensor(w1, w1, w0, ALU.bitwise_or))
                own.sync()
                scatter_index(dve, own, w1, t["pcol"][:, 0:1], idx, dup, eq, GP)
                assert own.n == OWN, own.n
                dve.tensor_scalar(ev, ev, float(GP), None, ALU.add).then_inc(made, 1)
            with dve.Fori(0, TP // 2) as q:
                for j in range(2):
                    dve.wait_ge(t_loaded[j], q * 16 + 16)
                    dve.tensor_reduce(t["t_edge"][:, bass.ds(q * (2 * TS) + j * TS, TS)], piece[:, j, :, :],
                                      AX.X, ALU.max).then_inc(reduced, 1)
            dve.wait_ge(reduced, TP + LEAD)
        dve.tensor_scalar(mask, t["t_edge"][:, :], 0.0, None, ALU.is_gt).then_inc(masked, 1)
        dve.tensor_scalar(t["t_idx"][:, :], t["t_edge"][:, :], -1.0, 0.0, ALU.add, ALU.max)


def gather_values(nc, ctx, t, a, scratch_v):
    got = ctx.enter_context(nc.semaphore("values_got"))
    stored = ctx.enter_context(nc.semaphore("values_stored"))
    W = 16
    SB = SLOTS // 128

    def program(pool):
        flat = a["edge_values"].rearrange("(e o) -> e o", o=1)
        with pool.Fori(0, SB // W) as r:
            pool.drain()
            pool.tensor_copy(t["gidx"][:, :], t["t_idx"][:, bass.ds(r * W, W)])
            pool.drain()
            for k in range(W):
                pool.indirect_dma_start(t["gval"][:, k:k + 1], None, flat,
                                        bass.IndirectOffsetOnAxis(ap=t["gidx"][:, k:k + 1], axis=0)) \
                    .then_inc(got, 16)
            pool.drain()
            pool.tensor_copy(t["t_edge"][:, bass.ds(r * W, W)], t["gval"][:, :])
        pool.drain()
        pool.dma_start(scratch_v, t["t_edge"][:, :]).then_inc(stored, 16)
        pool.wait_ge(stored, 16)
    return program


TOK_EPS = 1e-5
GROUPS = B * N // CH
GPI = N // CH
NBLK = CH // BS
EXPERTS = 8
EXP_AND_LN_SET = 6


def turns(eng, body):
    for i in range(4):
        body(i, i % 2)
    with eng.Fori(0, (GROUPS - 6) // 2) as r:
        for j in range(2):
            body(r * 2 + (4 + j), j)
    for i in range(GROUPS - 2, GROUPS + 2):
        body(i, i % 2)


def live(g):
    return not isinstance(g, int) or 0 <= g < GROUPS


def load_exp_and_ln(nc, act):
    act.add_instruction(mybir.InstLoadActFuncSet(act_func_set_id=EXP_AND_LN_SET, name=nc.get_next_instruction_name(),
                                                 engine=act.engine, ins=[], outs=[]))


class TokenNorm:

    def __init__(self, nc, ctx, t, name):
        def sem(n):
            return ctx.enter_context(nc.semaphore(f"{name}_{n}"))

        def sb(n, shape):
            return ctx.enter_context(nc.sbuf_tensor(f"{name}_{n}", shape, F32))
        self.t = t
        self.mean_ready = sem("mean_ready")
        self.centered = sem("centered")
        self.squared = sem("squared")
        self.var_ready = sem("var_ready")
        self.log_done = sem("log_done")
        self.rstd = sem("rstd")
        self.normed = sem("normed")
        self.xc, self.xh = sb("xc", [128, 2, CH]), sb("xh", [128, 2, CH])
        self.sq, self.rs = sb("sq", [128, CH]), sb("rs", [128, CH])
        self.bank = t["M"][:, 0, :]

    def x(self, g):
        return self.t["x_all"][:, g * CH:(g + 1) * CH] if isinstance(g, int) else \
            self.t["x_all"][:, bass.ds(g * CH, CH)]

    def pe_mean(self, pe, g):
        pe.wait_ge(self.rstd, g)
        pe.matmul(self.bank, self.t["avg"][:, :], self.x(g), start=True, stop=True) \
          .then_inc(self.mean_ready, 1)

    def dve_center(self, dve, g, p):
        dve.wait_ge(self.mean_ready, g + 1)
        dve.tensor_tensor(self.xc[:, p, :], self.x(g), self.bank, ALU.subtract).then_inc(self.centered, 1)

    def act_square(self, act, g, p):
        act.wait_ge(self.centered, g + 1)
        act.wait_ge(self.var_ready, g)
        act.activation(self.sq[:, :], self.xc[:, p, :], ACT.Square).then_inc(self.squared, 1)

    def pe_var(self, pe, g):
        pe.wait_ge(self.squared, g + 1)
        pe.matmul(self.bank, self.t["avg"][:, :], self.sq[:, :], start=True, stop=True) \
          .then_inc(self.var_ready, 1)

    def act_rstd(self, act, g):
        act.wait_ge(self.var_ready, g + 1)
        act.wait_ge(self.normed, g)
        act.activation(self.rs[:, :], self.bank, ACT.Ln, bias=self.t["eps"][:, 0:1]).then_inc(self.log_done, 1)
        act.wait_ge(self.log_done, g + 1)
        act.activation(self.rs[:, :], self.rs[:, :], ACT.Exp, scale=-0.5).then_inc(self.rstd, 1)

    def dve_norm(self, dve, g, p):
        dve.wait_ge(self.rstd, g + 1)
        dve.tensor_tensor(self.xh[:, p, :], self.xc[:, p, :], self.rs[:, :], ALU.mult).then_inc(self.normed, 1)


def layer1_constants(nc, ctx, t, a, scratch_v, scratch_m):
    def sem(name):
        return ctx.enter_context(nc.semaphore(name))

    def sb(name, shape, dt=F32):
        return ctx.enter_context(nc.sbuf_tensor(name, shape, dt))
    loaded, made, own_sem = sem("l1_loaded"), sem("l1_made"), sem("l1_own")
    TT = N // 128
    w, m = sb("slot_w", [128, TT, BS]), sb("slot_m", [128, TT, BS])
    diag, tmp = sb("diag", [128, BS]), sb("slot_tmp", [128, TT, BS])
    gw = sb("gate_wb", [128, 3, HEADS])
    block = ctx.enter_context(nc.Block())

    @block.sync
    def _(sp):
        for dst, src in ((w, scratch_v), (m, scratch_m)):
            sp.dma_start(dst[:, :, :], src.rearrange("b (r k) -> (b r) k", k=BS)
                         .rearrange("(t q) k -> q t k", q=128)).then_inc(loaded, 16)
        row = lambda v, n: v.rearrange("(o n) -> o n", o=1).broadcast_to([128, n])
        col = lambda v: v.rearrange("(p o) -> p o", o=1)
        sp.dma_start(gw[:, 0, :], a["gate_w"].rearrange("h o -> (h o)").rearrange("(o n) -> o n", o=1).broadcast_to([128, HEADS])).then_inc(loaded, 16)
        sp.dma_start(gw[:, 1, :], row(a["gate_b"], HEADS)).then_inc(loaded, 16)
        sp.dma_start(t["w1"][:, :], a["qkv1_w"]).then_inc(loaded, 16)
        for k in range(2):
            sp.dma_start(t["b1"][:, k:k + 1], col(a["qkv1_b"][k * C:(k + 1) * C])).then_inc(loaded, 16)
        for h in range(HEADS):
            sp.dma_start(t["bv1"][h * BS:(h + 1) * BS, :],
                         a["qkv1_b"][2 * C + h * D:2 * C + (h + 1) * D].rearrange("(o n) -> o n", o=1)
                         .broadcast_to([BS, D])).then_inc(loaded, 16)
        sp.dma_start(t["pw1"][:, :], a["proj1_w"]).then_inc(loaded, 16)
        sp.dma_start(t["pb1"][:, 0:1], col(a["proj1_b"])).then_inc(loaded, 16)
        sp.dma_start(t["rw"][:, :], a["router_w"]).then_inc(loaded, 16)
        for k in range(QT):
            sp.dma_start(t["rb"][:, k, :], row(a["router_b"], EXPERTS)).then_inc(loaded, 16)
        sp.dma_start(t["ew"][:, :, :], a["expert_w"].rearrange("e d c -> d e c")).then_inc(loaded, 16)
        sp.dma_start(t["eb"][:, :], a["expert_b"]).then_inc(loaded, 16)
        sp.wait_ge(loaded, (4 + 1 + 2 + HEADS + 2 + 1 + QT + 2) * 16)

    @block.gpsimd
    def _(pool):
        pool.memset(diag[:, :], 0.0).then_inc(made, 1)
        pool.memset(t["avg"][:, :], 1.0 / C).then_inc(made, 1)
        pool.memset(t["eps"][:, :], TOK_EPS).then_inc(made, 1)
        pool.memset(t["kexp"][:, :, :, :, :], 0.0).then_inc(made, 1)
        pool.memset(t["vexp"][:, :, :, :], 0.0).then_inc(made, 1)
        pool.iota(t["iota8"][:, :], pattern=[[1, EXPERTS]], base=0, channel_multiplier=0,
                  allow_small_or_imprecise_dtypes=True).then_inc(made, 1)
        for q in range(128 // BS):
            pool.wait_ge(made, 6 + q)
            pool.affine_select(out=diag[:, :], in_=diag[:, :], compare_op=ALU.not_equal, fill=1.0,
                               base=-q * BS, pattern=[[-1, BS]], channel_multiplier=1).then_inc(made, 1)

    @block.vector
    def _(dve):
        own = Steps(dve, own_sem)
        dve.wait_ge(made, 6 + 128 // BS)
        dve.wait_ge(loaded, (4 + 1 + 2 + HEADS + 2 + 1 + QT + 2) * 16)
        d3 = diag[:, :].rearrange("p (o k) -> p o k", o=1).broadcast_to([128, TT, BS])
        own.inc(dve.tensor_tensor(w[:, :, :], w[:, :, :], m[:, :, :], ALU.mult))
        own.sync()
        own.inc(dve.tensor_scalar(tmp[:, :, :], w[:, :, :], -1.0, 1.0, ALU.mult, ALU.add))
        own.sync()
        own.inc(dve.tensor_tensor(tmp[:, :, :], tmp[:, :, :], d3, ALU.mult))
        own.inc(dve.tensor_tensor(m[:, :, :], m[:, :, :], d3, ALU.max))
        own.sync()
        own.inc(dve.tensor_tensor(w[:, :, :], w[:, :, :], tmp[:, :, :], ALU.add))
        own.sync()
        own.inc(dve.tensor_scalar(tmp[:, :, :], m[:, :, :], -1.0, 1e9, ALU.add, ALU.mult))
        own.inc(dve.tensor_tensor(gw[:, 2, :], gw[:, 0, :], gw[:, 1, :], ALU.add))
        own.sync()
        own.inc(dve.tensor_tensor(t["bias"][:, :, :], tmp[:, :, :], w[:, :, :], ALU.add))
        own.inc(dve.tensor_scalar(gw[:, 2, :], gw[:, 2, :], 1.0 / BS, None, ALU.mult))
        own.sync()
        for h in range(HEADS):
            own.inc(dve.tensor_scalar(t["gate"][:, :, h, :], m[:, :, :], gw[:, 1, h:h + 1],
                                      gw[:, 2, h:h + 1], ALU.mult, ALU.add))
        own.sync()
        for h in range(HEADS):
            own.inc(dve.scalar_tensor_tensor(t["gate"][:, :, h, :], w[:, :, :], gw[:, 0, h:h + 1],
                                             t["gate"][:, :, h, :], ALU.mult, ALU.add))


def block_attention(nc, ctx, t):
    def sem(name):
        return ctx.enter_context(nc.semaphore("a1_" + name))

    def sb(name, shape, dt=F32):
        return ctx.enter_context(nc.sbuf_tensor("a1_" + name, shape, dt))
    ln = TokenNorm(nc, ctx, t, "ln1")
    qk_ready, qk_taken = sem("qk_ready"), sem("qk_taken")
    v_ready, v_taken = sem("v_ready"), sem("v_taken")
    s_ready, s_taken = sem("s_ready"), sem("s_taken")
    shifted, exped, mixed = sem("shifted"), sem("exped"), sem("mixed")
    ct_ready, ct_taken = sem("ct_ready"), sem("ct_taken")
    av_ready, av_taken = sem("av_ready"), sem("av_taken")
    proj_ready, added = sem("proj_ready"), sem("added")
    own_sem = [sem("scores_own"), sem("mix_own")]
    q_t = sb("q_t", [128, CH])
    sc = sb("sc", [128, QT, HEADS, BS])
    mix = sb("mix", [128, QT, HEADS, BS])
    sm = sb("sm", [128, 6, QT * HEADS])
    ct, av = sb("ct", [128, CH]), sb("av", [128, CH])
    qb, kb = t["M"][:, 1, :], t["S"][:, 0, 0:CH]
    vb = t["S"][:, 0, CH:2 * CH]
    sbk, ctb, avb = t["S"][:, 1, CH:2 * CH], t["O"][:, 0, :], t["O"][:, 1, :]
    kexp, vexp, w1 = t["kexp"], t["vexp"], t["w1"]
    block = ctx.enter_context(nc.Block())

    @block.tensor
    def _(pe):
        def turn(i, p):
            g, f, e = i, i - 1, i - 2
            if isinstance(g, int) and g == 0:
                ln.pe_mean(pe, g)
            if live(f):
                xh = ln.xh[:, 1 - p, :]
                pe.wait_ge(ln.normed, f + 1)
                pe.wait_ge(qk_taken, f * 2)
                pe.matmul(qb, w1[:, 0:C], xh, start=True, stop=True)
                pe.matmul(kb, w1[:, C:2 * C], xh, start=True, stop=True).then_inc(qk_ready, 1)
                pe.wait_ge(v_taken, f)
                for n in range(NBLK):
                    for h in range(HEADS):
                        last = pe.matmul(vb[h * BS:(h + 1) * BS, n * D:(n + 1) * D],
                                         xh[:, n * BS:(n + 1) * BS],
                                         w1[:, 2 * C + h * D:2 * C + (h + 1) * D], start=True, stop=True)
                last.then_inc(v_ready, 1)
            if live(g):
                ln.pe_var(pe, g)
            if live(e):
                pe.wait_ge(mixed, e + 1)
                pe.wait_ge(ct_taken, e)
                for k in range(QT):
                    last = pe.matmul(ctb[:, k * 128:(k + 1) * 128],
                                     mix[:, k, :, :].rearrange("p h k -> p (h k)"), t["ident"][:, :],
                                     start=True, stop=True)
                last.then_inc(ct_ready, 1)
            if live(f):
                pe.wait_ge(qk_taken, (f + 1) * 2)
                pe.wait_ge(s_taken, f)
                for n in range(NBLK):
                    r = n % 4 * BS
                    last = pe.matmul(sbk[r:r + BS, n // 4 * C:(n // 4 + 1) * C], q_t[:, n * BS:(n + 1) * BS],
                                     kexp[:, 1 - p, n, :, :].rearrange("p h k -> p (h k)"), start=True, stop=True)
                last.then_inc(s_ready, 1)
            if live(e):
                pe.wait_ge(ct_taken, e + 1)
                pe.wait_ge(added, e)
                for n in range(NBLK):
                    last = pe.matmul(avb[:, n * BS:(n + 1) * BS], vexp[:, p, n, :],
                                     ct[:, n * BS:(n + 1) * BS], start=True, stop=True)
                last.then_inc(av_ready, 1)
            if live(g + 1):
                ln.pe_mean(pe, g + 1)
            if live(e):
                pe.wait_ge(av_taken, e + 1)
                pe.matmul(avb, t["pw1"][:, :], av[:, :], start=True, stop=True).then_inc(proj_ready, 1)
        turns(pe, turn)

    @block.vector
    def _(dve):
        scores_own, mix_own = Steps(dve, own_sem[0]), Steps(dve, own_sem[1])
        OWN_SCORES, OWN_MIX = 5, 5
        s4 = sbk.rearrange("p (t h k) -> p t h k", t=QT, h=HEADS)
        s3 = sbk.rearrange("p (t k) -> p t k", k=BS)
        c3 = sc[:, :, :, :].rearrange("p t h k -> p (t h) k")
        m3 = mix[:, :, :, :].rearrange("p t h k -> p (t h) k")

        def wide(n):
            return sm[:, n, :].rearrange("p (t o) -> p t o", o=1).broadcast_to([128, QT * HEADS, BS])

        def columns(g, k, n):
            at = g % GPI * QT + k
            return slice(at, at + n) if isinstance(g, int) else bass.ds(at, n)

        def shifted_scores(f):
            own = scores_own
            own.at(f * OWN_SCORES)
            dve.wait_ge(s_ready, f + 1)
            for k in range(QT):
                last = dve.scalar_tensor_tensor(sc[:, k, :, :], s4[:, k, :, :], SCALE,
                                                t["bias"][:, columns(f, k, 1), :].broadcast_to([128, HEADS, BS]),
                                                ALU.mult, ALU.add)
            own.inc(last)
            dve.tensor_reduce(sm[:, 0, :], s3, AX.X, ALU.add).then_inc(s_taken, 1)
            dve.wait_ge(s_taken, f + 1)
            own.sync()
            own.inc(dve.tensor_scalar(sm[:, 0, :], sm[:, 0, :], SCALE / BS, 1.0, ALU.mult, ALU.add))
            own.inc(dve.tensor_reduce(sm[:, 1, :], c3, AX.X, ALU.max))
            own.sync()
            own.inc(dve.tensor_tensor(sm[:, 1, :], sm[:, 1, :], sm[:, 0, :], ALU.max))
            own.sync()
            own.inc(dve.tensor_tensor(c3, c3, wide(1), ALU.subtract))
            dve.tensor_tensor(sm[:, 2, :], sm[:, 0, :], sm[:, 1, :], ALU.subtract).then_inc(shifted, 1)
            assert own.n == OWN_SCORES

        def weights(e):
            own = mix_own
            own.at(e * OWN_MIX)
            dve.wait_ge(exped, e * 2 + 2)
            own.inc(dve.tensor_reduce(sm[:, 3, :], c3, AX.X, ALU.add))
            own.sync()
            own.inc(dve.tensor_tensor(sm[:, 3, :], sm[:, 3, :], sm[:, 2, :], ALU.add))
            own.sync()
            own.inc(dve.reciprocal(sm[:, 4, :], sm[:, 3, :]))
            own.sync()
            dve.wait_ge(ct_ready, e)
            dve.scalar_tensor_tensor(sm[:, 5, :], sm[:, 2, :], 1.0 / BS, sm[:, 4, :], ALU.mult, ALU.mult)
            own.inc(dve.tensor_tensor(m3, c3, wide(4), ALU.mult))
            own.sync()
            own.inc(dve.tensor_tensor(mix[:, :, :, :], mix[:, :, :, :], t["gate"][:, columns(e, 0, QT), :, :],
                                      ALU.add))
            own.sync()
            dve.tensor_tensor(m3, m3, wide(5), ALU.add).then_inc(mixed, 1)
            assert own.n == OWN_MIX

        def turn(i, p):
            g, f, e = i, i - 1, i - 2
            if isinstance(g, int) and g == 0:
                ln.dve_center(dve, g, p)
            if live(e):
                weights(e)
            if live(f):
                if not isinstance(f, int) or f > 1:
                    dve.wait_ge(av_ready, f - 1)
                dve.wait_ge(v_ready, f + 1)
                for h in range(HEADS):
                    rows = slice(h * BS, (h + 1) * BS)
                    last = dve.tensor_tensor(vexp[rows, 1 - p, :, h * D:(h + 1) * D],
                                             vb.rearrange("p (n d) -> p n d", d=D)[rows, :, :],
                                             t["bv1"][rows, :].rearrange("p (o d) -> p o d", o=1)
                                             .broadcast_to([D, NBLK, D]), ALU.add)
                last.then_inc(v_taken, 1)
            if live(f):
                if live(f - 1):
                    dve.wait_ge(mixed, f)
                shifted_scores(f)
            if live(g):
                ln.dve_norm(dve, g, p)
            if live(g + 1):
                ln.dve_center(dve, g + 1, 1 - p)
            if live(e):
                dve.wait_ge(proj_ready, e + 1)
                x = ln.x(e)
                dve.scalar_tensor_tensor(x, avb, t["pb1"][:, 0:1], x, ALU.add, ALU.add).then_inc(added, 1)
        turns(dve, turn)

    @block.scalar
    def _(act):
        load_exp_and_ln(nc, act)

        def turn(i, p):
            g, f, e = i, i - 1, i - 2
            if live(g):
                ln.act_square(act, g, p)
            if live(f):
                act.wait_ge(qk_ready, f + 1)
                act.wait_ge(s_ready, f)
                act.activation(q_t[:, :], qb, ACT.Identity, bias=t["b1"][:, 0:1]).then_inc(qk_taken, 1)
                for h in range(HEADS):
                    rows = slice(h * D, (h + 1) * D)
                    last = act.activation(kexp[rows, 1 - p, :, h, :],
                                          kb.rearrange("p (n k) -> p n k", k=BS)[rows, :, :],
                                          ACT.Identity, bias=t["b1"][rows, 1:2])
                last.then_inc(qk_taken, 1)
            if live(e):
                act.wait_ge(ct_ready, e + 1)
                act.wait_ge(av_ready, e)
                act.activation(ct[:, :], ctb, ACT.Identity).then_inc(ct_taken, 1)
            if live(g):
                ln.act_rstd(act, g)
            if live(e):
                act.wait_ge(av_ready, e + 1)
                act.wait_ge(proj_ready, e)
                act.activation(av[:, :], avb, ACT.Identity).then_inc(av_taken, 1)
            if live(f):
                act.wait_ge(shifted, f + 1)
                act.activation(sc[:, :, :, :], sc[:, :, :, :], ACT.Exp).then_inc(exped, 1)
                act.activation(sm[:, 2, :], sm[:, 2, :], ACT.Exp).then_inc(exped, 1)
        turns(act, turn)


def experts(nc, ctx, t, out):
    def sem(name):
        return ctx.enter_context(nc.semaphore("moe_" + name))

    def sb(name, shape, dt=F32):
        return ctx.enter_context(nc.sbuf_tensor("moe_" + name, shape, dt))
    ln = TokenNorm(nc, ctx, t, "ln2")
    r_ready, r_taken, exped = sem("r_ready"), sem("r_taken"), sem("exped")
    gated, e_ready = sem("gated"), sem("e_ready")
    acc_own = sem("acc_own")
    gt_ready, gt_taken, f_ready, summed = sem("gt_ready"), sem("gt_taken"), sem("f_ready"), sem("summed")
    stored = [sem(f"stored_{j}") for j in range(2)]
    own_sem = sem("own")
    lg = sb("lg", [128, QT, EXPERTS])
    mx, den = sb("mx", [128, QT]), sb("den", [128, QT])
    best = sb("best", [128, QT, 8])
    bidx, bidxf = sb("bidx", [128, QT, 8], U32), sb("bidxf", [128, QT, 8])
    gates = sb("gates", [128, 2, QT, EXPERTS])
    g2 = sb("g2", [128, QT, EXPERTS])
    acc = sb("acc", [128, 2, QT, C])
    gt = sb("gt", [EXPERTS, CH])
    y = sb("y", [128, 2, CH])
    gate_scratch = sb("gate", [128, 1])
    rbk, gtb, fbk = t["M"][:, 1, :], t["O"][:, 0, :], t["O"][:, 1, :]
    ebk = t["S"]
    img = out.rearrange("b c n -> c b n")
    block = ctx.enter_context(nc.Block())

    @block.tensor
    def _(pe):
        def turn(i, p):
            g, f, e = i, i - 1, i - 2
            xh = ln.xh[:, 1 - p, :]
            if live(g):
                ln.pe_mean(pe, g)
            if live(f):
                pe.wait_ge(ln.normed, f + 1)
                pe.wait_ge(r_taken, f)
                for k in range(QT):
                    last = pe.matmul(rbk[:, k * EXPERTS:(k + 1) * EXPERTS], xh[:, k * 128:(k + 1) * 128],
                                     t["rw"][:, :], start=True, stop=True)
                last.then_inc(r_ready, 1)
            if live(e):
                pe.wait_ge(acc_own, (e + 1) * (QT * EXPERTS))
                pe.wait_ge(gt_taken, e)
                for k in range(QT):
                    last = pe.matmul(gtb[0:EXPERTS, k * 128:(k + 1) * 128], gates[:, p, k, :],
                                     t["ident"][:, :], start=True, stop=True)
                last.then_inc(gt_ready, 1)
            HALF = EXPERTS // 2

            def expert_products(q):
                kp, m = q // 2, q % 2
                if not isinstance(f, int) or f > 0 or q >= 2:
                    pe.wait_ge(acc_own, f * (QT * EXPERTS) + (q - 1) * (2 * HALF))
                for k in range(2):
                    last = pe.matmul(ebk[:, k, m * CH:(m + 1) * CH],
                                     xh[:, (2 * kp + k) * 128:(2 * kp + k + 1) * 128],
                                     t["ew"][:, 4 * m:4 * m + 4, :].rearrange("p e c -> p (e c)"),
                                     start=True, stop=True)
                last.then_inc(e_ready, 1)
            if live(f):
                expert_products(0)
            if live(g):
                ln.pe_var(pe, g)
            if live(e):
                pe.wait_ge(gt_taken, e + 1)
                pe.wait_ge(summed, e)
                pe.matmul(fbk, t["eb"][:, :], gt[:, :], start=True, stop=False, skip_group_check=True)
                for k in range(QT):
                    last = pe.matmul(fbk[:, k * 128:(k + 1) * 128], acc[:, p, k, :], t["ident"][:, :],
                                     start=False, stop=(k == QT - 1), skip_group_check=True)
                last.then_inc(f_ready, 1)
            if live(f):
                for q in range(1, QT):
                    expert_products(q)
        turns(pe, turn)

    @block.scalar
    def _(act):
        load_exp_and_ln(nc, act)

        def turn(i, p):
            g, f, e = i, i - 1, i - 2
            if live(g):
                ln.act_square(act, g, p)
            if live(e):
                act.wait_ge(gt_ready, e + 1)
                act.wait_ge(f_ready, e)
                act.activation(gt[:, :], gtb[0:EXPERTS, :], ACT.Identity).then_inc(gt_taken, 1)
            if live(f):
                act.wait_ge(gated, f * 2 + 1)
                act.activation(lg[:, :, :], lg[:, :, :], ACT.Exp).then_inc(exped, 1)
            if live(g):
                ln.act_rstd(act, g)
        turns(act, turn)

    @block.vector
    def _(dve):
        own = Steps(dve, own_sem)
        OWN = 2 + 8

        def wide(v):
            return v.rearrange("p (t o) -> p t o", o=1).broadcast_to([128, QT, EXPERTS])

        def turn(i, p):
            g, f, e = i, i - 1, i - 2
            if live(g):
                ln.dve_center(dve, g, p)
            if live(f):
                own.at(f * OWN)
                dve.wait_ge(r_ready, f + 1)
                dve.tensor_tensor(lg[:, :, :], rbk[:, 0:QT * EXPERTS].rearrange("p (t e) -> p t e", t=QT),
                                  t["rb"][:, :, :], ALU.add).then_inc(r_taken, 1)
                dve.wait_ge(r_taken, f + 1)
                own.inc(dve.tensor_reduce(mx[:, :], lg[:, :, :], AX.X, ALU.max))
                own.sync()
                dve.tensor_tensor(lg[:, :, :], lg[:, :, :], wide(mx[:, :]), ALU.subtract).then_inc(gated, 1)
            if live(f):
                dve.wait_ge(exped, f + 1)
                own.inc(dve.tensor_reduce(den[:, :], lg[:, :, :], AX.X, ALU.add))
                own.sync()
                own.inc(dve.reciprocal(den[:, :], den[:, :]))
                own.sync()
                own.inc(dve.tensor_tensor(lg[:, :, :], lg[:, :, :], wide(den[:, :]), ALU.mult))
                own.sync_apart(gate_scratch[:, 0:1])
                for k in range(QT):
                    last = dve.max(best[:, k, :], lg[:, k, :])
                own.inc(last)
                own.sync_apart(gate_scratch[:, 0:1])
                for k in range(QT):
                    dve.max_index(bidx[:, k, :], best[:, k, :], lg[:, k, :])
                own.inc(dve.tensor_tensor(den[:, :], best[:, :, 0], best[:, :, 1], ALU.add))
                own.sync()
                own.inc(dve.reciprocal(den[:, :], den[:, :]))
                own.inc(dve.tensor_copy(bidxf[:, :, :], bidx[:, :, :]))
                own.sync()
                own.inc(dve.tensor_tensor(best[:, :, :], best[:, :, :], wide(den[:, :]), ALU.mult))
                own.sync()
                for k in range(QT):
                    dve.tensor_scalar(gates[:, 1 - p, k, :], t["iota8"][:, :], bidxf[:, k, 0:1], best[:, k, 0:1],
                                      ALU.is_equal, ALU.mult)
                    last = dve.tensor_scalar(g2[:, k, :], t["iota8"][:, :], bidxf[:, k, 1:2], best[:, k, 1:2],
                                             ALU.is_equal, ALU.mult)
                own.inc(last)
                own.sync()
                dve.tensor_tensor(gates[:, 1 - p, :, :], gates[:, 1 - p, :, :], g2[:, :, :], ALU.add) \
                   .then_inc(gated, 1)
            if live(e):
                dve.wait_ge(f_ready, e + 1)
                if not isinstance(e, int) or e > 1:
                    dve.wait_ge(stored[p], (e - p) * 8)
                dve.tensor_tensor(y[:, p, :], fbk, ln.x(e), ALU.add).then_inc(summed, 1)
            if live(g) and not live(f):
                ln.dve_norm(dve, g, p)
            if live(f):
                dve.wait_ge(gated, f * 2 + 2)
                if not isinstance(f, int) or f > 1:
                    dve.wait_ge(f_ready, f - 1)
                done = f * (QT * EXPERTS)
                for q in range(QT):
                    kp, m = q // 2, q % 2
                    if q == 2 and live(g):
                        ln.dve_norm(dve, g, p)
                    dve.wait_ge(e_ready, f * QT + (q + 1))
                    for x in range(4 * m, 4 * m + 4):
                        for k in range(2):
                            n = kp * 2 * EXPERTS + x * 2 + k
                            tile = 2 * kp + k
                            src = ebk[:, k, x * C:(x + 1) * C]
                            gx = gates[:, 1 - p, tile, x:x + 1]
                            if x == 0:
                                last = dve.tensor_scalar(acc[:, 1 - p, tile, :], src, gx, None, ALU.mult)
                            else:
                                dve.wait_ge(acc_own, done + (n - 1))
                                last = dve.scalar_tensor_tensor(acc[:, 1 - p, tile, :], src, gx,
                                                                acc[:, 1 - p, tile, :], ALU.mult, ALU.add)
                            last.then_inc(acc_own, 1)
        turns(dve, turn)

    @block.sync
    def _(sp):
        with sp.Fori(0, B) as b:
            with sp.Fori(0, GPI // 2) as r:
                for j in range(2):
                    sp.wait_ge(summed, b * GPI + r * 2 + (j + 1))
                    sp.dma_start(img[:, bass.ds(b, 1), bass.ds(r * (2 * CH) + j * CH, CH)],
                                 y[:, j, :].rearrange("p (o n) -> p o n", o=1)).then_inc(stored[j], 16)
        for j in range(2):
            sp.wait_ge(stored[j], GROUPS // 2 * 16)


def build(nc, a, out, dbg=None):
    with ExitStack() as whole:
        def sb(name, shape, dt=F32, ctx=whole):
            return ctx.enter_context(nc.sbuf_tensor(name, shape, dt))

        t = {
            "x_all": sb("x_all", [128, B * N]),
            "ident": sb("ident", [128, 128]),
            "gn_a": sb("gn_a", [128, B]), "gn_b": sb("gn_b", [128, B]),
        }
        for name, shape in (("S", [128, 2, 2 * CH]), ("O", [128, 2, CH]), ("M", [128, 2, CH])):
            t[name] = whole.enter_context(nc.psum_tensor(name, shape, F32))
        for name, shape, dt in (
                ("pcol", [128, 1], I32), ("ovf", [128, 1], F32), ("ovf_all", [128, 1], F32),
                ("idx8", [128, BATCH], U32), ("ev8", [128, BATCH], F32),
                ("list", [128, 2 * LIST], F32)):
            t[name] = sb(name, shape, dt)
        SB = SLOTS // 128
        t["list_e"], t["list_idx"] = t["list"][:, 0:LIST], t["list"][:, LIST:2 * LIST].bitcast(U32)
        t["t_idx"] = t["list"][:, 0:SB].bitcast(U32)
        table = nc.dram_tensor("slot_table", (SLOTS, 128), F32).ap()
        scratch_v = nc.dram_tensor("slot_values", (128, SB), F32).ap()
        scratch_m = nc.dram_tensor("slot_masks", (128, SB), F32).ap()
        with ExitStack() as c:
            edge_lists(nc, c, t, a, table)
        with ExitStack() as l0:
            t.update({
                "qs": sb("q_stack", [128, NCH * HEADS * CH], F16, l0),
                "ks": sb("k_stack", [128, HEADS, N], F16, l0),
                "vones": sb("v_ones", [128, KT, HEADS, 2 * D], F32, l0),
                "probs": sb("probs", [128, 3, 2 * CH], F32, l0),
                "xn": sb("x_norm", [128, 2, CH], F32, l0),
                "o_t": sb("o_t", [128, CH], F32, l0),
                "os": sb("o_sums", [128, 2, CH], F32, l0),
                "dn": sb("dens", [128, 2, CH], F32, l0),
                "mx8": sb("mx8", [128, HEADS * QT, NCH], F32, l0),
                "mx": sb("mx", [128, HEADS * QT], F32, l0),
                "mrow": sb("mrow", [HEADS * QT, 128], F16, l0),
                "wqk": sb("w_qk", [128, 2 * HEADS, 3 * D], F32, l0),
                "wv": sb("w_v", [128, C], F32, l0),
                "qk_b": sb("qk_bias", [3 * D, 2 * HEADS], F32, l0),
                "vbias": sb("vbias", [128, QT, HEADS, D], F32, l0),
                "proj_w": sb("proj_w", [128, C], F32, l0),
                "proj_b": sb("proj_bias", [128, 1], F32, l0),
                "t_edge": sb("t_edge", [128, SB], F32, l0),
                "gidx": sb("gidx", [128, 16], U32, l0),
                "gval": sb("gval", [128, 16], F32, l0),
            })
            with ExitStack() as c:
                constants_and_norm(nc, c, t, a)
            with ExitStack() as c:
                attention(nc, c, t, 0, 1, scatter_lists(nc, c, t, table))
            with ExitStack() as c:
                beside = TableMaxima(nc, c, t, table)
                attention(nc, c, t, 1, 1, beside.pool, beside)
            with ExitStack() as c:
                last_edges(nc, c, t, a, table, scratch_m)
            with ExitStack() as c:
                attention(nc, c, t, 2, 2, gather_values(nc, c, t, a, scratch_v))
        with ExitStack() as l1:
            TT = N // 128
            t.update({
                "w1": sb("l1_qkv_w", [128, 3 * C], F32, l1), "b1": sb("l1_qk_b", [128, 2], F32, l1),
                "bv1": sb("l1_v_b", [128, D], F32, l1),
                "pw1": sb("l1_proj_w", [128, C], F32, l1), "pb1": sb("l1_proj_b", [128, 1], F32, l1),
                "rw": sb("router_w", [128, EXPERTS], F32, l1), "rb": sb("router_b", [128, QT, EXPERTS], F32, l1),
                "ew": sb("expert_w", [128, EXPERTS, C], F32, l1), "eb": sb("expert_b", [EXPERTS, C], F32, l1),
                "avg": sb("avg", [128, C], F32, l1), "eps": sb("token_eps", [128, 1], F32, l1),
                "iota8": sb("iota8", [128, EXPERTS], F32, l1),
                "kexp": sb("k_diag", [128, 2, NBLK, HEADS, BS], F32, l1),
                "vexp": sb("v_diag", [128, 2, NBLK, C], F32, l1),
                "bias": sb("slot_bias", [128, TT, BS], F32, l1),
                "gate": sb("slot_gate", [128, TT, HEADS, BS], F32, l1),
            })
            with ExitStack() as c:
                layer1_constants(nc, c, t, a, scratch_v, scratch_m)
            with ExitStack() as c:
                block_attention(nc, c, t)
            if dbg is None:
                with ExitStack() as c:
                    experts(nc, c, t, out)
        if dbg is not None:
            with ExitStack() as c:
                done = c.enter_context(nc.semaphore("dbg"))
                blk = c.enter_context(nc.Block())

                @blk.sync
                def _(sp):
                    for b in range(B):
                        sp.dma_start(dbg[b], t["x_all"][:, b * N:(b + 1) * N]).then_inc(done, 16)
                    sp.wait_ge(done, B * 16)


_INPUTS = {
    "x": ("x", lambda v: v.reshape(B, C, N)),
    "norm_w": ("L0_conv_norm_w", None), "norm_b": ("L0_conv_norm_b", None),
    "qkv_wT": ("L0_conv_qkv_w", lambda v: v.T), "qkv_b": ("L0_conv_qkv_b", None),
    "proj_wT": ("L0_conv_proj_w", lambda v: v.T), "proj_b": ("L0_conv_proj_b", None),
    "edges": ("L1_attn_edge_index", None), "edge_values": ("L1_attn_edge_values", None),
    "qkv1_w": ("L1_attn_qkv_w", None), "qkv1_b": ("L1_attn_qkv_b", None),
    "proj1_w": ("L1_attn_proj_w", None), "proj1_b": ("L1_attn_proj_b", None),
    "gate_w": ("L1_attn_gate_w", None), "gate_b": ("L1_attn_gate_b", None),
    "router_w": ("L1_ffn_router_w", None), "router_b": ("L1_ffn_router_b", None),
    "expert_w": ("L1_ffn_expert_w", None), "expert_b": ("L1_ffn_expert_b", None),
}


def kernel(**inputs):
    import numpy as np
    import concourse.bacc as bacc
    from concourse.bass_utils import run_bass_kernel_spmd

    nc = bacc.Bacc("TRN2", target_bir_lowering=False, num_devices=1)
    arrays, a = {}, {}
    for name, (source, lay) in _INPUTS.items():
        v = np.asarray(inputs[source])
        v = np.ascontiguousarray(lay(v) if lay else v)
        arrays[f"in_{name}"] = v
        a[name] = nc.dram_tensor(f"in_{name}", v.shape, mybir.dt.from_np(v.dtype), kind="ExternalInput").ap()
    out = nc.dram_tensor("out_0", (B, C, N), F32, kind="ExternalOutput").ap()
    build(nc, a, out)
    r = run_bass_kernel_spmd(nc, [arrays], core_ids=[0])
    return r.results[0]["out_0"].reshape(B, C, 64, 64)
```
